# Optimizing a Trainium2 kernel written in Bass

```python
import numpy as np
import jax
import jax.numpy as jnp

def _softmax(x, axis=-1):
    return jax.nn.softmax(x, axis=axis)

def _gelu(x):
    return jax.nn.gelu(x, approximate=True)

def _silu(x):
    return jax.nn.silu(x)

def _sigmoid(x):
    return jax.nn.sigmoid(x)

def _layernorm(x, axis=-1, eps=1e-05):
    m = jnp.mean(x, axis=axis, keepdims=True)
    v = jnp.var(x, axis=axis, keepdims=True)
    return (x - m) / jnp.sqrt(v + eps)

def _scatter_add(tgt, idx, src, axis=0):
    return tgt.at[idx].add(src)

def _segment_sum(src, seg, n):
    return jax.ops.segment_sum(src, seg, n)
kernel_name = 'mk_xattn_ffn_d2_seqx_r8_4c4a1b'

def setup_inputs(seed: int=0):
    np.random.seed(seed)
    _w = jnp.asarray

    def _rec_inputs():
        import jax
        import jax.numpy as jnp
        _rk = jax.random.key(seed)
        x = -0.0003929 + 0.9999 * jax.random.normal(jax.random.fold_in(_rk, 1), (16, 128, 128), jnp.float32)
        _lenS = 128 - jax.random.randint(jax.random.fold_in(_rk, 7), (16,), 0, max(1, 128 // 4) + 1, jnp.int32)
        _lenS2 = 128 - jax.random.randint(jax.random.fold_in(_rk, 8), (16,), 0, max(1, 128 // 4) + 1, jnp.int32)
        _ctx_1024P = jax.random.normal(jax.random.fold_in(_rk, 11), (16, 16, 128), jnp.float32)
        _ctx_1024c = jax.random.dirichlet(jax.random.fold_in(_rk, 511), 0.3 * jnp.ones((16,), jnp.float32), (16, 128))
        _ctx_1024t = jnp.einsum('bsk,bkd->bsd', _ctx_1024c, _ctx_1024P)
        _ctx_1024t = _ctx_1024t * jax.lax.rsqrt(jnp.mean(jnp.square(_ctx_1024t)) + 1e-12) * 0.953939
        ctx_1024 = 2.81802e-05 + 1.00001 * (_ctx_1024t + 0.3 * jax.random.normal(jax.random.fold_in(_rk, 611), (16, 128, 128), jnp.float32))
        _validS = jnp.arange(128)[None, :] < _lenS[:, None]
        _validS2 = jnp.arange(128)[None, :] < _lenS2[:, None]
        _causal = jnp.tril(jnp.ones((128, 128), dtype=bool))
        mask_BxSxS2_bf1 = jnp.ones((16, 128, 128), dtype=bool)
        return (x, ctx_1024, mask_BxSxS2_bf1)
    x, ctx_1024, mask_BxSxS2_bf1 = _rec_inputs()

    def _L0_xattn_setup():
        import jax, jax.numpy as jnp
        import numpy as np

        def _iterative_inv(mat, n_iter=6):
            I = jnp.eye(mat.shape[-1], dtype=mat.dtype)
            K = mat
            scale = 1.0 / jnp.max(jnp.sum(K, axis=-2), axis=-1)[..., None, None]
            V = scale * jnp.swapaxes(K, -1, -2)
            for _ in range(n_iter):
                KV = K @ V
                V = 0.25 * V @ (13.0 * I - KV @ (15.0 * I - KV @ (7.0 * I - KV)))
            return V
        key = jax.random.key(seed)
        B, L, d_model, H, M = (4, 512, 128, 16, 128)
        ks = jax.random.split(key, 11)
        s = 0.02
        return {'queries': jax.random.normal(ks[0], (B, L, d_model), jnp.float32), 'keys': jax.random.normal(ks[1], (B, L, d_model), jnp.float32), 'values': jax.random.normal(ks[2], (B, L, d_model), jnp.float32), 'Wq': jax.random.normal(ks[3], (d_model, d_model), jnp.float32) * s, 'bq': jnp.zeros((d_model,), jnp.float32), 'Wk': jax.random.normal(ks[4], (d_model, d_model), jnp.float32) * s, 'bk': jnp.zeros((d_model,), jnp.float32), 'Wv': jax.random.normal(ks[5], (d_model, d_model), jnp.float32) * s, 'bv': jnp.zeros((d_model,), jnp.float32), 'Wo': jax.random.normal(ks[6], (d_model, d_model), jnp.float32) * s, 'bo': jnp.zeros((d_model,), jnp.float32), 'n_heads': 16, 'n_landmarks': 128}
    _L0_xattn_all = _L0_xattn_setup()
    _L0_xattn_in = {k: v for k, v in _L0_xattn_all.items() if k in ('Wq', 'bq', 'Wk', 'bk', 'Wv', 'bv', 'Wo', 'bo')}
    del _L0_xattn_all

    def _L0_ffn_setup():
        import jax, jax.numpy as jnp
        import numpy as np
        B, S, H = (2, 128, 128)
        E, F = (16, 64)
        G, TOPK_G, TOPK = (4, 2, 4)
        N_SHARED = 2
        ROUTE_SCALE = 1.0
        FS = N_SHARED * F

        def _gate(x, w_gate):
            T = x.shape[0]
            scores = jax.nn.sigmoid(x @ w_gate.T)
            sv = scores.reshape(T, G, E // G)
            group_scores = jax.lax.top_k(sv, 2)[0].sum(-1)
            top_groups = jax.lax.top_k(group_scores, TOPK_G)[1]
            allowed = jnp.zeros((T, G), dtype=bool).at[jnp.arange(T)[:, None], top_groups].set(True)
            masked = jnp.where(allowed[:, :, None], sv, -jnp.inf).reshape(T, E)
            _, idx = jax.lax.top_k(masked, TOPK)
            w = jnp.take_along_axis(scores, idx, axis=1)
            w = w / (w.sum(-1, keepdims=True) + 1e-06) * ROUTE_SCALE
            return (w, idx)

        def _swiglu(x, w1, w3, w2):
            return jax.nn.silu(x @ w1.T) * (x @ w3.T) @ w2.T
        key = jax.random.key(seed)
        ks = jax.random.split(key, 8)
        scale = 0.02
        return {'hidden_states': jax.random.normal(ks[0], (B, S, H), dtype=jnp.float32), 'w_gate': jax.random.normal(ks[1], (E, H), dtype=jnp.float32) * scale, 'w1_e': jax.random.normal(ks[2], (E, F, H), dtype=jnp.float32) * scale, 'w3_e': jax.random.normal(ks[3], (E, F, H), dtype=jnp.float32) * scale, 'w2_e': jax.random.normal(ks[4], (E, H, F), dtype=jnp.float32) * scale, 'w1_s': jax.random.normal(ks[5], (FS, H), dtype=jnp.float32) * scale, 'w3_s': jax.random.normal(ks[6], (FS, H), dtype=jnp.float32) * scale, 'w2_s': jax.random.normal(ks[7], (H, FS), dtype=jnp.float32) * scale}
    _L0_ffn_all = _L0_ffn_setup()
    _L0_ffn_in = {k: v for k, v in _L0_ffn_all.items() if k in ('w_gate', 'w1_e', 'w3_e', 'w2_e', 'w1_s', 'w3_s', 'w2_s')}
    del _L0_ffn_all

    def _L1_xattn_setup():
        import jax, jax.numpy as jnp
        import numpy as np
        N_HEADS = 16
        D_MODEL = 128
        D_K = D_MODEL // N_HEADS
        NEG_INF = -1000000000.0
        key = jax.random.key(seed)
        ks = jax.random.split(key, 12)
        B, S = (2, 256)
        scale = 1.0 / np.sqrt(D_MODEL)
        inp = {'query': jax.random.normal(ks[0], (B, S, D_MODEL), jnp.float32), 'key': jax.random.normal(ks[1], (B, S, D_MODEL), jnp.float32), 'value': jax.random.normal(ks[2], (B, S, D_MODEL), jnp.float32), 'mask': jnp.ones((B, S, S), dtype=bool), 'Wq': jax.random.normal(ks[3], (D_MODEL, D_MODEL), jnp.float32) * scale, 'bq': jnp.zeros((D_MODEL,), jnp.float32), 'Wk': jax.random.normal(ks[4], (D_MODEL, D_MODEL), jnp.float32) * scale, 'bk': jnp.zeros((D_MODEL,), jnp.float32), 'Wv': jax.random.normal(ks[5], (D_MODEL, D_MODEL), jnp.float32) * scale, 'bv': jnp.zeros((D_MODEL,), jnp.float32), 'Wo': jax.random.normal(ks[6], (D_MODEL, D_MODEL), jnp.float32) * scale, 'bo': jnp.zeros((D_MODEL,), jnp.float32)}
        return inp
    _L1_xattn_all = _L1_xattn_setup()
    _L1_xattn_in = {k: v for k, v in _L1_xattn_all.items() if k in ('Wq', 'bq', 'Wk', 'bk', 'Wv', 'bv', 'Wo', 'bo')}
    del _L1_xattn_all

    def _L1_ffn_setup():
        import jax, jax.numpy as jnp
        import numpy as np
        E = 8
        K = 2
        D = 128
        H = 128
        B, T = (2, 128)
        key = jax.random.key(seed)
        ks = jax.random.split(key, 6)
        s = 0.02
        return {'x': jax.random.normal(ks[0], (B, T, D), dtype=jnp.float32), 'gate_w': jax.random.normal(ks[1], (E, D), dtype=jnp.float32) * s, 'lb_bias': jnp.zeros((E,), dtype=jnp.float32), 'w1': jax.random.normal(ks[2], (E, H, D), dtype=jnp.float32) * s, 'w2': jax.random.normal(ks[3], (E, D, H), dtype=jnp.float32) * s, 'cfc': jax.random.normal(ks[4], (H, D), dtype=jnp.float32) * s, 'cproj': jax.random.normal(ks[5], (D, H), dtype=jnp.float32) * s}
    _L1_ffn_all = _L1_ffn_setup()
    _L1_ffn_in = {k: v for k, v in _L1_ffn_all.items() if k in ('gate_w', 'lb_bias', 'w1', 'w2', 'cfc', 'cproj')}
    del _L1_ffn_all
    return {'x': x, 'ctx_1024': ctx_1024, 'mask_BxSxS2_bf1': mask_BxSxS2_bf1, 'L0_xattn_Wq': _L0_xattn_in['Wq'], 'L0_xattn_bq': _L0_xattn_in['bq'], 'L0_xattn_Wk': _L0_xattn_in['Wk'], 'L0_xattn_bk': _L0_xattn_in['bk'], 'L0_xattn_Wv': _L0_xattn_in['Wv'], 'L0_xattn_bv': _L0_xattn_in['bv'], 'L0_xattn_Wo': _L0_xattn_in['Wo'], 'L0_xattn_bo': _L0_xattn_in['bo'], 'L0_ffn_w_gate': _L0_ffn_in['w_gate'], 'L0_ffn_w1_e': _L0_ffn_in['w1_e'], 'L0_ffn_w3_e': _L0_ffn_in['w3_e'], 'L0_ffn_w2_e': _L0_ffn_in['w2_e'], 'L0_ffn_w1_s': _L0_ffn_in['w1_s'], 'L0_ffn_w3_s': _L0_ffn_in['w3_s'], 'L0_ffn_w2_s': _L0_ffn_in['w2_s'], 'L1_xattn_Wq': _L1_xattn_in['Wq'], 'L1_xattn_bq': _L1_xattn_in['bq'], 'L1_xattn_Wk': _L1_xattn_in['Wk'], 'L1_xattn_bk': _L1_xattn_in['bk'], 'L1_xattn_Wv': _L1_xattn_in['Wv'], 'L1_xattn_bv': _L1_xattn_in['bv'], 'L1_xattn_Wo': _L1_xattn_in['Wo'], 'L1_xattn_bo': _L1_xattn_in['bo'], 'L1_ffn_gate_w': _L1_ffn_in['gate_w'], 'L1_ffn_lb_bias': _L1_ffn_in['lb_bias'], 'L1_ffn_w1': _L1_ffn_in['w1'], 'L1_ffn_w2': _L1_ffn_in['w2'], 'L1_ffn_cfc': _L1_ffn_in['cfc'], 'L1_ffn_cproj': _L1_ffn_in['cproj']}

def reference(x, ctx_1024, mask_BxSxS2_bf1, L0_xattn_Wq, L0_xattn_bq, L0_xattn_Wk, L0_xattn_bk, L0_xattn_Wv, L0_xattn_bv, L0_xattn_Wo, L0_xattn_bo, L0_ffn_w_gate, L0_ffn_w1_e, L0_ffn_w3_e, L0_ffn_w2_e, L0_ffn_w1_s, L0_ffn_w3_s, L0_ffn_w2_s, L1_xattn_Wq, L1_xattn_bq, L1_xattn_Wk, L1_xattn_bk, L1_xattn_Wv, L1_xattn_bv, L1_xattn_Wo, L1_xattn_bo, L1_ffn_gate_w, L1_ffn_lb_bias, L1_ffn_w1, L1_ffn_w2, L1_ffn_cfc, L1_ffn_cproj):
    import jax
    import jax.numpy as jnp

    def _L0_xattn_ref(queries, keys, values, Wq, bq, Wk, bk, Wv, bv, Wo, bo, n_heads, n_landmarks):
        import jax, jax.numpy as jnp
        import numpy as np

        def _iterative_inv(mat, n_iter=6):
            I = jnp.eye(mat.shape[-1], dtype=mat.dtype)
            K = mat
            scale = 1.0 / jnp.max(jnp.sum(K, axis=-2), axis=-1)[..., None, None]
            V = scale * jnp.swapaxes(K, -1, -2)
            for _ in range(n_iter):
                KV = K @ V
                V = 0.25 * V @ (13.0 * I - KV @ (15.0 * I - KV @ (7.0 * I - KV)))
            return V
        B, L, _ = queries.shape
        H, M = (n_heads, n_landmarks)
        q = (queries @ Wq + bq).reshape(B, L, H, -1).transpose(0, 2, 1, 3)
        k = (keys @ Wk + bk).reshape(B, L, H, -1).transpose(0, 2, 1, 3)
        v = (values @ Wv + bv).reshape(B, L, H, -1).transpose(0, 2, 1, 3)
        D = q.shape[-1]
        Q_l = q.reshape(B, H, M, L // M, D).mean(axis=-2)
        K_l = k.reshape(B, H, M, L // M, D).mean(axis=-2)
        kernel_1 = jax.nn.softmax(jnp.einsum('bhld,bhmd->bhlm', q, K_l), axis=-1)
        kernel_2 = jax.nn.softmax(jnp.einsum('bhnd,bhmd->bhnm', Q_l, K_l), axis=-1)
        kernel_3 = jax.nn.softmax(jnp.einsum('bhmd,bhld->bhml', Q_l, k), axis=-1)
        X = kernel_1 @ _iterative_inv(kernel_2) @ (kernel_3 @ v)
        X = X.transpose(0, 2, 1, 3).reshape(B, L, H * D)
        return X @ Wo + bo

    def _L0_ffn_ref(hidden_states, w_gate, w1_e, w3_e, w2_e, w1_s, w3_s, w2_s):
        import jax, jax.numpy as jnp
        import numpy as np
        B, S, H = (2, 128, 128)
        E, F = (16, 64)
        G, TOPK_G, TOPK = (4, 2, 4)
        N_SHARED = 2
        ROUTE_SCALE = 1.0
        FS = N_SHARED * F

        def _gate(x, w_gate):
            T = x.shape[0]
            scores = jax.nn.sigmoid(x @ w_gate.T)
            sv = scores.reshape(T, G, E // G)
            group_scores = jax.lax.top_k(sv, 2)[0].sum(-1)
            top_groups = jax.lax.top_k(group_scores, TOPK_G)[1]
            allowed = jnp.zeros((T, G), dtype=bool).at[jnp.arange(T)[:, None], top_groups].set(True)
            masked = jnp.where(allowed[:, :, None], sv, -jnp.inf).reshape(T, E)
            _, idx = jax.lax.top_k(masked, TOPK)
            w = jnp.take_along_axis(scores, idx, axis=1)
            w = w / (w.sum(-1, keepdims=True) + 1e-06) * ROUTE_SCALE
            return (w, idx)

        def _swiglu(x, w1, w3, w2):
            return jax.nn.silu(x @ w1.T) * (x @ w3.T) @ w2.T
        shape = hidden_states.shape
        x = hidden_states.reshape(-1, H)
        weights, idx = _gate(x, w_gate)
        combine = (jax.nn.one_hot(idx, E, dtype=x.dtype) * weights[..., None]).sum(1)
        g = jax.nn.silu(jnp.einsum('th,efh->tef', x, w1_e))
        u = jnp.einsum('th,efh->tef', x, w3_e)
        routed = jnp.einsum('tef,ehf,te->th', g * u, w2_e, combine)
        shared = _swiglu(x, w1_s, w3_s, w2_s)
        return (routed + shared).reshape(shape)

    def _L1_xattn_ref(query, key, value, mask, Wq, bq, Wk, bk, Wv, bv, Wo, bo):
        import jax, jax.numpy as jnp
        import numpy as np
        N_HEADS = 16
        D_MODEL = 128
        D_K = D_MODEL // N_HEADS
        NEG_INF = -1000000000.0
        B = query.shape[0]

        def proj(x, W, b):
            y = x @ W.T + b
            return y.reshape(B, -1, N_HEADS, D_K).transpose(0, 2, 1, 3)
        q = proj(query, Wq, bq)
        k = proj(key, Wk, bk)
        v = proj(value, Wv, bv)
        scores = jnp.einsum('bhqd,bhkd->bhqk', q, k) / jnp.sqrt(jnp.float32(D_K))
        scores = jnp.where(mask[:, None, :, :], scores, NEG_INF)
        attn = jax.nn.softmax(scores, axis=-1)
        x = jnp.einsum('bhqk,bhkd->bhqd', attn, v)
        x = x.transpose(0, 2, 1, 3).reshape(B, -1, N_HEADS * D_K)
        return x @ Wo.T + bo

    def _L1_ffn_ref(x, gate_w, lb_bias, w1, w2, cfc, cproj):
        import jax, jax.numpy as jnp
        import numpy as np
        E = 8
        K = 2
        D = 128
        H = 128
        B, T = (2, 128)
        Bx, Tx, Dx = x.shape
        logits = jnp.einsum('btd,ed->bte', x, gate_w)
        _, idx = jax.lax.top_k(logits + lb_bias, K)
        sel_logits = jnp.take_along_axis(logits, idx, axis=-1)
        w = jax.nn.sigmoid(sel_logits)
        w = w / (jnp.sum(w, axis=-1, keepdims=True) + 1e-06)
        xf = x.reshape(-1, Dx)
        idxf = idx.reshape(-1, K)
        wf = w.reshape(-1, K)
        onehot = jax.nn.one_hot(idxf, E, dtype=wf.dtype)
        we = jnp.einsum('nke,nk->ne', onehot, wf)
        hidden = jnp.square(jax.nn.relu(jnp.einsum('nd,ehd->neh', xf, w1)))
        expert_out = jnp.einsum('neh,edh->ned', hidden, w2)
        moe_out = jnp.einsum('ned,ne->nd', expert_out, we).reshape(Bx, Tx, Dx)
        sh = jnp.square(jax.nn.relu(jnp.einsum('btd,hd->bth', x, cfc)))
        shared = jnp.einsum('bth,dh->btd', sh, cproj)
        return moe_out + shared
    x = x + _L0_xattn_ref(_layernorm(x, axis=-1), ctx_1024, ctx_1024, L0_xattn_Wq, L0_xattn_bq, L0_xattn_Wk, L0_xattn_bk, L0_xattn_Wv, L0_xattn_bv, L0_xattn_Wo, L0_xattn_bo, 16, 128)
    x = x + _L0_ffn_ref(_layernorm(x, axis=-1), L0_ffn_w_gate, L0_ffn_w1_e, L0_ffn_w3_e, L0_ffn_w2_e, L0_ffn_w1_s, L0_ffn_w3_s, L0_ffn_w2_s)
    x = x + _L1_xattn_ref(_layernorm(x, axis=-1), ctx_1024, ctx_1024, mask_BxSxS2_bf1, L1_xattn_Wq, L1_xattn_bq, L1_xattn_Wk, L1_xattn_bk, L1_xattn_Wv, L1_xattn_bv, L1_xattn_Wo, L1_xattn_bo)
    x = x + _L1_ffn_ref(_layernorm(x, axis=-1), L1_ffn_gate_w, L1_ffn_lb_bias, L1_ffn_w1, L1_ffn_w2, L1_ffn_cfc, L1_ffn_cproj)
    return x

_drawn_inputs = setup_inputs


def setup_inputs(seed=0):
    import zlib

    import numpy as np

    out = dict(_drawn_inputs(seed))
    spreads = {'L0_xattn_bq': (0.0, 0.8),
     'L0_xattn_bk': (0.0, 0.8),
     'L0_xattn_bv': (0.0, 0.402),
     'L0_xattn_bo': (0.0, 0.1),
     'L1_xattn_bq': (0.0, 0.402),
     'L1_xattn_bk': (0.0, 0.8),
     'L1_xattn_bv': (0.0, 0.1),
     'L1_xattn_bo': (0.0, 0.1),
     'L1_ffn_lb_bias': (0.0, 0.8)}
    factors = {'L0_xattn_Wq': 8.0,
     'L0_xattn_Wk': 8.0,
     'L0_ffn_w_gate': 8.0,
     'L0_ffn_w1_e': 8.0,
     'L0_ffn_w3_e': 8.0,
     'L0_ffn_w2_e': 8.0,
     'L0_ffn_w1_s': 8.0,
     'L0_ffn_w3_s': 8.0,
     'L0_ffn_w2_s': 8.0,
     'L1_ffn_gate_w': 7.998,
     'L1_ffn_w1': 7.192,
     'L1_ffn_w2': 6.639,
     'L1_ffn_cfc': 4.857,
     'L1_ffn_cproj': 4.596}
    for name, (base, spread) in spreads.items():
        noise = np.random.default_rng([zlib.crc32(name.encode()), seed]).standard_normal(out[name].shape)
        drawn = base * np.exp(spread * noise) if base else spread * noise
        out[name] = jnp.asarray(drawn.astype(out[name].dtype))
    for name, factor in factors.items():
        out[name] = (out[name] * factor).astype(out[name].dtype)
    return out
```

```python
from contextlib import ExitStack

import concourse.bass as bass
from concourse import mybir

ALU = mybir.AluOpType
ACT = mybir.ActivationFunctionType
AX = mybir.AxisListType
F32 = mybir.dt.float32
U8 = mybir.dt.uint8

P = 128
HEADS = 16
DH = P // HEADS
GROUP = 4
GROUPS = HEADS // GROUP
STEPS = 5
SLOTS = STEPS * 2 * GROUPS
HALVES = 2 * SLOTS
BANK = 512
LN_EPS = 1e-5
SUM_EPS = 1e-6
MASKED = -1e9
SCORE_SCALE = float(DH) ** -0.5

ATTN_W = 4 * P
ATTN_B = 2 + 2 * P
E0N, E1N = 16, 8
G0N = 4
UP = E0N * 64
CHUNKS = UP // P + 1

FIELDS = [("wq0", P), ("wk0", P), ("wv0", P), ("bq0", 1), ("bk0", 1), ("bv0", P), ("ident", P), ("rowmask", GROUP),
          ("ones", P),
          ("wo0", P), ("bo0", P), ("wk1", P), ("wv1", P), ("bk1", 1), ("bv1", P), ("wq1", P), ("bq1", 1),
          ("gate0", E0N), ("low4", G0N * G0N), ("low16", E0N * E0N), ("low8", E1N * E1N),
          ("w1", UP), ("w3", UP), ("w1s", P), ("w3s", P), ("w2", CHUNKS * P),
          ("wo1", P), ("bo1", P), ("gate1", E1N), ("lb", E1N), ("up1", UP), ("up1s", P), ("down1", CHUNKS * P)]
AT = {}
_at = 0
for _name, _n in FIELDS:
    AT[_name] = (_at, _at + _n)
    _at += _n
PACKED = _at
FIRST = AT["ones"][1]


def build(nc, x_d, ctx_d, mask_d, w_d, out_d):
    B = x_d.shape[0]
    with ExitStack() as ctx:
        def sb(name, *shape, dt=F32):
            return ctx.enter_context(nc.sbuf_tensor(name, [P, *shape], dt))

        def sem(name):
            return ctx.enter_context(nc.semaphore(name))

        core_bank = [ctx.enter_context(nc.psum_tensor(f"core_bank{g}", [P, BANK], F32)) for g in range(GROUPS)]
        pre_bank = [ctx.enter_context(nc.psum_tensor(f"pre_bank{i}", [P, BANK], F32)) for i in range(2)]
        post_bank = [ctx.enter_context(nc.psum_tensor(f"post_bank{i}", [P, BANK], F32)) for i in range(2)]

        W = sb("packed", PACKED)

        def field(name):
            return W[:, AT[name][0]:AT[name][1]]

        E_first = sb("E_first", HEADS, P)
        E_work = sb("E_work", HEADS, P)
        E_last = sb("E_last", HEADS, P)
        EE = sb("EE", HEADS, P)
        F = sb("F", HEADS, P)
        x_pre = sb("x_pre", P)
        ctx_pre = sb("ctx_pre", P)
        stats_pre = sb("stats_pre", 6)
        mv_pre = sb("mv_pre", 2)
        rstd_pre = sb("rstd_pre", 2)
        xn_pre = sb("xn_pre", P)
        xcT_pre = sb("xcT_pre", 2 * P)
        q0T = sb("q0T", P)
        k0T = sb("k0T", P)
        k0m = sb("k0m", GROUP, P)
        v0 = sb("v0", HEADS, DH)
        negmax0 = sb("negmax0", HEADS)
        rowsum0 = sb("rowsum0", HEADS)
        rinv0 = sb("rinv0", HEADS)
        A = sb("A", HEADS, P)
        A_T = sb("A_T", HEADS, P)
        colsum = sb("colsum", HEADS)
        colmax = sb("colmax", 2)
        scale_diag = sb("scale_diag", HEADS)
        neg_scale = sb("neg_scale", HEADS)
        Av_next = sb("Av_next", HEADS, DH)
        Av = sb("Av", HEADS, DH)
        U = [sb(f"U{r}", HEADS, DH) for r in range(3)]
        u34 = sb("u34", HEADS, DH)
        X0 = sb("X0", HEADS, DH)
        x_post = sb("x_post", P)
        ctx_post = sb("ctx_post", P)
        mask_post = sb("mask_post", P, dt=U8)
        x_bo = sb("x_bo", P)
        x1 = sb("x1", P)
        x2 = sb("x2", P)
        x2_bo = sb("x2_bo", P)
        x3 = sb("x3", P)
        x4 = sb("x4", P)
        XcT = sb("XcT", 2 * P)
        k1T = sb("k1T", P)
        k1m = sb("k1m", GROUP, P)
        q1T = sb("q1T", P)
        v1 = sb("v1", HEADS, DH)
        stats_post = sb("stats_post", 6)
        mv_post = sb("mv_post", 2)
        rstd_post = sb("rstd_post", 2)
        xn_post = sb("xn_post", P)
        xnT = sb("xnT", P)
        logits = sb("logits", E0N)
        gate_e = sb("gate_e", E0N)
        gate_d = sb("gate_d", E0N)
        score = sb("score", E0N)
        pairs = sb("pairs", G0N, 6)
        gscore = sb("gscore", G0N)
        greater = sb("greater", E0N * E0N)
        equal = sb("equal", E0N * E0N)
        rank = sb("rank", E0N)
        penalty = sb("penalty", G0N)
        choice = sb("choice", E0N)
        chosen = sb("chosen", E0N)
        total = sb("total", 3)
        combine = sb("combine", E0N)
        act_t = sb("act_t", BANK)
        act_g = sb("act_g", BANK)
        hidden = sb("hidden", CHUNKS * P)
        hiddenT = sb("hiddenT", CHUNKS, P)
        S1 = sb("S1", HEADS, P)
        P1 = sb("P1", HEADS, P)
        P1_T = sb("P1_T", HEADS, P)
        negmax1 = sb("negmax1", HEADS)
        rowsum1 = sb("rowsum1", HEADS)
        rinv1 = sb("rinv1", HEADS)
        X1 = sb("X1", HEADS, DH)
        X1T = sb("X1T", P)
        held, held_pool = sb("held", 1), sb("held_pool", 1)
        const_eps = sb("const_eps", 1)
        const_mhalf = sb("const_mhalf", 1)

        ident = field("ident")
        hid3 = hidden[:, 0:UP]

        first_loaded, rest_loaded = sem("first_loaded"), sem("rest_loaded")
        pool_consts = sem("pool_consts")
        x_pre_loaded, ctx_pre_loaded = sem("x_pre_loaded"), sem("ctx_pre_loaded")
        pre_stats_done = sem("pre_stats_done")
        pre_var_ready = sem("pre_var_ready")
        pre_veps_ready = sem("pre_veps_ready")
        pre_rstd_ready = sem("pre_rstd_ready")
        pre_xn_ready = sem("pre_xn_ready")
        pre_T_ready, pre_T_copied = sem("pre_T_ready"), sem("pre_T_copied")
        qkv0_ready = sem("qkv0_ready")
        q0k0_copied, v0_copied = sem("q0k0_copied"), sem("v0_copied")
        k0_masked = sem("k0_masked")
        scores0_ready, negmax0_ready, exp0_done = sem("scores0_ready"), sem("negmax0_ready"), sem("exp0_done")
        rinv0_ready, A_ready = sem("rinv0_ready"), sem("A_ready")
        A_T_ready, A_T_copied, colsum_ready = sem("A_T_ready"), sem("A_T_copied"), sem("colsum_ready")
        Av_ready, Av_copied, Av_kept = sem("Av_ready"), sem("Av_copied"), sem("Av_kept")
        colsumT_ready, colmax_steps = sem("colsumT_ready"), sem("colmax_steps")
        scale_ready, scale_copied = sem("scale_ready"), sem("scale_copied")
        gram_ready, E_first_ready = sem("gram_ready"), sem("E_first_ready")
        square_ready, square_copied, F_ready = sem("square_ready"), sem("square_copied"), sem("F_ready")
        product_ready, E_copied = sem("product_ready"), sem("E_copied")
        x_post_loaded, ctx_post_loaded, mask_loaded = sem("x_post_loaded"), sem("ctx_post_loaded"), sem("mask_loaded")
        u_ready, u_copied, u34_ready, X0_ready = sem("u_ready"), sem("u_copied"), sem("u34_ready"), sem("X0_ready")
        x_bo_ready = sem("x_bo_ready")
        X0T_ready, X0T_copied = sem("X0T_ready"), sem("X0T_copied")
        proj0_ready, x1_ready, k1_copied, v1_copied = sem("proj0_ready"), sem("x1_ready"), sem("k1_copied"), sem("v1_copied")
        k1_masked = sem("k1_masked")
        post_stats_done, post_var_ready, post_veps_ready = sem("post_stats_done"), sem("post_var_ready"), sem("post_veps_ready")
        post_rstd_ready, post_xn_ready = sem("post_rstd_ready"), sem("post_xn_ready")
        xnT_ready, xnT_copied = sem("xnT_ready"), sem("xnT_copied")
        logits_ready, logits_copied, gate_exp_done = sem("logits_ready"), sem("logits_copied"), sem("gate_exp_done")
        gate_steps = sem("gate_steps")
        combine_ready = sem("combine_ready")
        gate_up_ready, up_ready = sem("gate_up_ready"), sem("up_ready")
        shared_up_ready = sem("shared_up_ready")
        tanh_done, swish_ready, hidden0_ready, hidden0_scaled = sem("tanh_done"), sem("swish_ready"), sem("hidden0_ready"), sem("hidden0_scaled")
        hiddenT_ready, hiddenT_copied = sem("hiddenT_ready"), sem("hiddenT_copied")
        down_ready = sem("down_ready")
        x2_ready, x2_bo_ready = sem("x2_ready"), sem("x2_bo_ready")
        q1_ready, q1_copied = sem("q1_ready"), sem("q1_copied")
        scores_filled = sem("scores_filled")
        scores1_ready, scores1_copied = sem("scores1_ready"), sem("scores1_copied")
        negmax1_ready, exp1_done = sem("negmax1_ready"), sem("exp1_done")
        P1_T_ready, P1_T_copied = sem("P1_T_ready"), sem("P1_T_copied")
        rinv1_ready, av1_ready, X1_ready = sem("rinv1_ready"), sem("av1_ready"), sem("X1_ready")
        X1T_ready, X1T_copied, proj1_ready, x3_ready = sem("X1T_ready"), sem("X1T_copied"), sem("proj1_ready"), sem("x3_ready")
        up1_ready, relu_done, relu_weighted, hidden1_ready = sem("up1_ready"), sem("relu_done"), sem("relu_weighted"), sem("hidden1_ready")
        x4_ready, out_stored = sem("x4_ready"), sem("out_stored")

        GATE0, GATE1 = 18, 8
        GATES = GATE0 + GATE1

        def group(t, g):
            return t[:, GROUP * g:GROUP * (g + 1), :]

        def columns(bank, n):
            return bank[:, 0:n]

        def by_head(ap, n):
            return ap.rearrange("p (h c) -> p h c", c=n)

        def across(ap, n):
            return ap.unsqueeze(2).broadcast_to([ap.shape[0], ap.shape[1], n])

        def repeated(ap, n):
            return ap.unsqueeze(1).broadcast_to([ap.shape[0], n, ap.shape[1]])

        def wait_prior(engine, semaphore, count):
            if not (isinstance(count, int) and count <= 0):
                engine.wait_ge(semaphore, count)

        block = ctx.enter_context(nc.Block())

        def pipeline(engine, body, edge):
            edge(0, None)
            body(0, True, False)
            body(1, True, True)
            with engine.Fori(2, B - 1) as c:
                body(c, True, True)
            body(B - 1, False, True)
            edge(None, B - 1)

        @block.sync
        def _(sp):
            sp.dma_start(W[:, 0:FIRST], w_d[:, 0:FIRST]).then_inc(first_loaded, 16)

            def load_pre(p):
                wait_prior(sp, pre_xn_ready, p)
                sp.dma_start(x_pre[:], x_d[p]).then_inc(x_pre_loaded, 16)
                wait_prior(sp, pre_T_ready, p)
                sp.dma_start(ctx_pre[:], ctx_d[p]).then_inc(ctx_pre_loaded, 16)

            def load_post(p):
                wait_prior(sp, x_bo_ready, p)
                sp.dma_start(x_post[:], x_d[p]).then_inc(x_post_loaded, 16)
                wait_prior(sp, X0T_ready, p)
                sp.dma_start(ctx_post[:], ctx_d[p]).then_inc(ctx_post_loaded, 16)
                wait_prior(sp, scores1_copied, GROUPS * p)
                sp.dma_start(mask_post[:], mask_d[p]).then_inc(mask_loaded, 16)

            def store(p):
                sp.wait_ge(x4_ready, p + 1)
                sp.dma_start(out_d[p], x4[:]).then_inc(out_stored, 16)

            load_pre(0)
            sp.dma_start(W[:, FIRST:PACKED], w_d[:, FIRST:PACKED]).then_inc(rest_loaded, 16)
            load_pre(1)
            load_pre(2)
            load_post(0)
            with sp.Fori(1, B - 2) as c:
                load_pre(c + 2)
                load_post(c)
                store(c - 1)
            for c in (B - 2, B - 1):
                load_post(c)
                store(c - 1)
            store(B - 1)
            sp.wait_ge(out_stored, 16 * B)

        @block.tensor
        def _(pe):
            mm = nc.tensor.matmul
            pe.wait_ge(first_loaded, 16)

            def core_half(c, h):
                slot, half = h // 2, h % 2
                step, phase, g = slot // (2 * GROUPS), slot // GROUPS % 2, slot % GROUPS
                src = E_first if step == 0 else E_work
                n = STEPS * GROUPS * c + GROUPS * step + g + 1
                if half == 0 and phase == 0 and step == 0:
                    pe.wait_ge(E_first_ready, GROUPS * c + g + 1)
                    wait_prior(pe, E_copied, STEPS * GROUPS * (c - 1) + (STEPS - 1) * GROUPS + g + 1)
                elif half == 0 and phase == 0:
                    pe.wait_ge(E_copied, n - GROUPS)
                elif half == 0:
                    pe.wait_ge(F_ready, n)
                for j in (2 * half, 2 * half + 1):
                    hd = GROUP * g + j
                    out = core_bank[g][:, P * j:P * (j + 1)]
                    if phase == 0:
                        last = mm(out, src[:, hd, :], src[:, hd, :], start=True, stop=True)
                    else:
                        last = mm(out, EE[:, hd, :], F[:, hd, :], start=True, stop=True)
                if half:
                    last.then_inc(square_ready if phase == 0 else product_ready, 1)

            def transpose_x_ctx(p):
                pe.wait_ge(pre_xn_ready, p + 1)
                wait_prior(pe, A_T_copied, GROUPS * p)
                wait_prior(pe, E_first_ready, GROUPS * p)
                nc.tensor.transpose(pre_bank[0][:, 0:P], xn_pre[:], ident)
                pe.wait_ge(ctx_pre_loaded, 16 * p + 16)
                nc.tensor.transpose(pre_bank[0][:, P:2 * P], ctx_pre[:], ident).then_inc(pre_T_ready, 1)

            def project_qkv0(p):
                pe.wait_ge(pre_T_copied, p + 1)
                bank = pre_bank[1]
                mm(bank[:, 0:P], field("wq0"), xcT_pre[:, 0:P], start=True, stop=True)
                mm(bank[:, P:2 * P], field("wk0"), xcT_pre[:, P:2 * P], start=True, stop=True)
                mm(bank[:, 2 * P:3 * P], xcT_pre[:, P:2 * P], field("wv0"), start=True, stop=True).then_inc(qkv0_ready, 1)

            def scores0(p, g):
                if g == 0:
                    pe.wait_ge(k0_masked, p + 1)
                elif g == 1:
                    pe.wait_ge(v0_copied, p + 1)
                else:
                    pe.wait_ge(A_T_copied, GROUPS * p + g - 1)
                rows = slice(32 * g, 32 * g + 32)
                mm(pre_bank[g % 2][:, :], q0T[rows, :], k0m[rows, :, :], start=True, stop=True).then_inc(scores0_ready, 1)

            def transpose_A(p, g):
                pe.wait_ge(A_ready, GROUPS * p + g + 1)
                for j in range(GROUP):
                    last = nc.tensor.transpose(pre_bank[g % 2][:, P * j:P * (j + 1)], A[:, GROUP * g + j, :], ident)
                last.then_inc(A_T_ready, 1)

            def apply_A(p):
                pe.wait_ge(A_T_copied, GROUPS * p + GROUPS)
                for hd in range(HEADS):
                    last = mm(pre_bank[0][:, DH * hd:DH * (hd + 1)], A_T[:, hd, :], v0[:, hd, :], start=True, stop=True)
                last.then_inc(Av_ready, 1)

            def transpose_colsum(p):
                pe.wait_ge(colsum_ready, GROUPS * p + GROUPS)
                nc.tensor.transpose(pre_bank[1][0:HEADS, 0:P], colsum[:, :], ident).then_inc(colsumT_ready, 1)

            def spread_scale(p):
                pe.wait_ge(colmax_steps, 3 * p + 3)
                mm(pre_bank[1][:, P:P + HEADS], field("ones")[0:HEADS, :], scale_diag[0:HEADS, :],
                   start=True, stop=True).then_inc(scale_ready, 1)

            def gram(p, g):
                if g == 0:
                    pe.wait_ge(Av_copied, p + 1)
                elif g == 1:
                    pe.wait_ge(scale_copied, p + 1)
                else:
                    pe.wait_ge(E_first_ready, GROUPS * p + g - 1)
                for j in range(GROUP):
                    a_t = A_T[:, GROUP * g + j, :]
                    last = mm(pre_bank[g % 2][:, P * j:P * (j + 1)], a_t, a_t, start=True, stop=True)
                last.then_inc(gram_ready, 1)

            def before(p, h):
                if h == 5:
                    transpose_x_ctx(p)
                if h == 8:
                    project_qkv0(p)
                for g, at in enumerate((13, 15, 25, 27)):
                    if h == at:
                        scores0(p, g)
                for g, at in enumerate((21, 23, 33, 35)):
                    if h == at:
                        transpose_A(p, g)
                if h == 38:
                    apply_A(p)
                if h == 39:
                    transpose_colsum(p)
                if h == 42:
                    spread_scale(p)
                for g, at in enumerate((45, 49, 53, 57)):
                    if h == at:
                        gram(p, g)

            def apply_E(p, r, f):
                if r == 0:
                    pe.wait_ge(Av_kept, p + 1)
                    pe.wait_ge(E_copied, STEPS * GROUPS * p + (STEPS - 1) * GROUPS + 2 * (f + 1))
                    if f == 0:
                        wait_prior(pe, x4_ready, p)
                else:
                    pe.wait_ge(u_copied, 6 * p + 2 * r + f - 1)
                u = Av if r == 0 else U[r - 1]
                for k in range(HEADS // 2):
                    hd = HEADS // 2 * f + k
                    last = mm(post_bank[f][:, DH * k:DH * (k + 1)], E_last[:, hd, :], u[:, hd, :], start=True, stop=True)
                last.then_inc(u_ready, 1)

            def transpose_X0_ctx(p):
                pe.wait_ge(X0_ready, 2 * p + 2)
                nc.tensor.transpose(post_bank[0][:, 0:P], X0[:].rearrange("p h c -> p (h c)"), ident)
                pe.wait_ge(ctx_post_loaded, 16 * p + 16)
                nc.tensor.transpose(post_bank[0][:, P:2 * P], ctx_post[:], ident).then_inc(X0T_ready, 1)

            def project_out0_kv1(p):
                pe.wait_ge(rest_loaded, 16)
                pe.wait_ge(X0T_copied, p + 1)
                bank = post_bank[1]
                mm(bank[:, 0:P], XcT[:, 0:P], field("wo0"), start=True, stop=True)
                mm(bank[:, P:2 * P], field("wk1"), XcT[:, P:2 * P], start=True, stop=True)
                mm(bank[:, 2 * P:3 * P], XcT[:, P:2 * P], field("wv1"), start=True, stop=True).then_inc(proj0_ready, 1)

            def transpose_xn(p, n):
                pe.wait_ge(post_xn_ready, 3 * p + n + 1)
                bank = post_bank[n % 2]
                if n == 1:
                    pe.wait_ge(hiddenT_copied, 6 * p + 3)
                nc.tensor.transpose(bank[:, 0:P], xn_post[:], ident).then_inc(xnT_ready, 1)

            def gate_logits(p, n):
                pe.wait_ge(xnT_copied, 3 * p + 2 * n + 1)
                if n == 0:
                    pe.wait_ge(k1_copied, p + 1)
                    pe.wait_ge(v1_copied, p + 1)
                w = field("gate0") if n == 0 else field("gate1")
                mm(post_bank[1][:, 0:w.shape[1]], xnT[:], w, start=True, stop=True).then_inc(logits_ready, 1)

            def up_gate(p, i):
                if i == 1:
                    pe.wait_ge(swish_ready, 3 * p + 1)
                a = AT["w1"][0] + BANK * i
                mm(post_bank[0][:, :], xnT[:], W[:, a:a + BANK], start=True, stop=True).then_inc(gate_up_ready, 1)

            def up_linear(p, i):
                if i == 0:
                    pe.wait_ge(logits_copied, 2 * p + 1)
                else:
                    pe.wait_ge(hidden0_ready, 3 * p + 1)
                a = AT["w3"][0] + BANK * i
                mm(post_bank[1][:, :], xnT[:], W[:, a:a + BANK], start=True, stop=True).then_inc(up_ready, 1)

            def up_shared(p):
                pe.wait_ge(swish_ready, 3 * p + 2)
                mm(post_bank[0][:, 0:P], xnT[:], field("w1s"), start=True, stop=True)
                mm(post_bank[0][:, P:2 * P], xnT[:], field("w3s"), start=True, stop=True).then_inc(shared_up_ready, 1)

            def transpose_hidden(p, n, i):
                if n == 0 and i == 0:
                    pe.wait_ge(hidden0_scaled, 2 * p + 1)
                    pe.wait_ge(hidden0_ready, 3 * p + 2)
                elif n == 0 and i == 1:
                    pe.wait_ge(hidden0_scaled, 2 * p + 2)
                    pe.wait_ge(hidden0_ready, 3 * p + 3)
                elif n == 1:
                    pe.wait_ge(hidden1_ready, 3 * p + i + 1)
                    if i == 0:
                        pe.wait_ge(relu_done, 3 * p + 2)
                    if i == 1:
                        pe.wait_ge(relu_done, 3 * p + 3)
                if i == 2:
                    pe.wait_ge(hiddenT_copied, 6 * p + 3 * n + 1)
                for k in range(4 * i, min(4 * i + 4, CHUNKS)):
                    last = nc.tensor.transpose(post_bank[(i + 1) % 2][:, P * (k - 4 * i):P * (k - 4 * i + 1)],
                                               hidden[:, P * k:P * (k + 1)], ident)
                last.then_inc(hiddenT_ready, 1)

            def project_down(p, n):
                pe.wait_ge(hiddenT_copied, 6 * p + 3 * n + 3)
                a = AT["w2"][0] if n == 0 else AT["down1"][0]
                for k in range(CHUNKS):
                    last = mm(post_bank[0][:, 0:P], hiddenT[:, k, :], W[:, a + P * k:a + P * (k + 1)],
                              start=(k == 0), stop=(k == CHUNKS - 1))
                last.then_inc(down_ready, 1)

            def project_q1(p):
                pe.wait_ge(xnT_copied, 3 * p + 2)
                pe.wait_ge(x2_ready, p + 1)
                mm(post_bank[0][:, 0:P], field("wq1"), xnT[:], start=True, stop=True).then_inc(q1_ready, 1)

            def scores1(p, g):
                if g < 2:
                    pe.wait_ge(q1_copied, p + 1)
                    pe.wait_ge(k1_masked, p + 1)
                else:
                    pe.wait_ge(P1_T_copied, GROUPS * p + g - 1)
                rows = slice(32 * g, 32 * g + 32)
                mm(post_bank[(g + 1) % 2][:, :], q1T[rows, :], k1m[rows, :, :], start=True, stop=True).then_inc(scores1_ready, 1)

            def transpose_P1(p, g):
                pe.wait_ge(exp1_done, GROUPS * p + g + 1)
                pe.wait_ge(scores1_copied, GROUPS * p + g + 1)
                for j in range(GROUP):
                    last = nc.tensor.transpose(post_bank[(g + 1) % 2][:, P * j:P * (j + 1)], P1[:, GROUP * g + j, :], ident)
                last.then_inc(P1_T_ready, 1)

            def apply_P1(p):
                pe.wait_ge(P1_T_copied, GROUPS * p + GROUPS)
                for hd in range(HEADS):
                    last = mm(post_bank[1][:, DH * hd:DH * (hd + 1)], P1_T[:, hd, :], v1[:, hd, :], start=True, stop=True)
                last.then_inc(av1_ready, 1)

            def transpose_X1(p):
                pe.wait_ge(X1_ready, p + 1)
                nc.tensor.transpose(post_bank[0][:, 0:P], X1[:].rearrange("p h c -> p (h c)"), ident).then_inc(X1T_ready, 1)

            def project_out1(p):
                pe.wait_ge(X1T_copied, p + 1)
                mm(post_bank[1][:, 0:P], X1T[:], field("wo1"), start=True, stop=True).then_inc(proj1_ready, 1)

            def up1(p, i):
                if i == 0:
                    pe.wait_ge(xnT_copied, 3 * p + 3)
                elif i == 1:
                    pe.wait_ge(logits_copied, 2 * p + 2)
                else:
                    pe.wait_ge(relu_done, 3 * p + 1)
                if i < 2:
                    a, n = AT["up1"][0] + BANK * i, BANK
                else:
                    a, n = AT["up1s"][0], P
                mm(post_bank[i % 2][:, 0:n], xnT[:], W[:, a:a + n], start=True, stop=True).then_inc(up1_ready, 1)

            def after(p, h):
                if h < 16 and h % 2 == 0:
                    apply_E(p, h // 4, h // 2 % 2)
                if h == 17:
                    transpose_X0_ctx(p)
                if h == 20:
                    project_out0_kv1(p)
                if h == 24:
                    transpose_xn(p, 0)
                if h == 26:
                    gate_logits(p, 0)
                    up_gate(p, 0)
                if h == 28:
                    up_linear(p, 0)
                if h == 30:
                    up_gate(p, 1)
                if h == 32:
                    up_linear(p, 1)
                if h == 34:
                    up_shared(p)
                if h == 36:
                    transpose_hidden(p, 0, 0)
                if h == 37:
                    transpose_hidden(p, 0, 1)
                if h == 38:
                    transpose_hidden(p, 0, 2)
                if h == 40:
                    project_down(p, 0)
                if h == 43:
                    transpose_xn(p, 1)
                if h == 44:
                    project_q1(p)
                for g, at in enumerate((46, 47, 54, 55)):
                    if h == at:
                        scores1(p, g)
                for g, at in enumerate((50, 51, 58, 59)):
                    if h == at:
                        transpose_P1(p, g)
                if h == 61:
                    apply_P1(p)
                if h == 63:
                    transpose_X1(p)
                if h == 65:
                    project_out1(p)
                if h == 68:
                    transpose_xn(p, 2)
                if h == 70:
                    gate_logits(p, 1)
                    up1(p, 0)
                if h == 71:
                    up1(p, 1)
                if h == 72:
                    up1(p, 2)
                if h == 75:
                    transpose_hidden(p, 1, 0)
                if h == 76:
                    transpose_hidden(p, 1, 1)
                if h == 77:
                    transpose_hidden(p, 1, 2)
                if h == 79:
                    project_down(p, 1)

            def body(c, has_next, has_previous):
                for h in range(HALVES):
                    core_half(c, h)
                    if has_previous:
                        after(c - 1, h)
                    if has_next:
                        before(c + 1, h)

            def edge(first, last):
                for h in range(HALVES):
                    if first is not None:
                        before(first, h)
                    if last is not None:
                        after(last, h)

            pipeline(pe, body, edge)

        @block.scalar
        def _(act):
            act.wait_ge(first_loaded, 16)
            activation = nc.scalar.activation

            def core_half(c, h):
                if h == 30:
                    wait_prior(act, X0_ready, 2 * c)
                    act.wait_ge(Av_copied, c + 1)
                    activation(Av[:], Av_next[:], ACT.Copy).then_inc(Av_kept, 1)
                if h % 2 == 0:
                    return
                slot = h // 2
                step, phase, g = slot // (2 * GROUPS), slot // GROUPS % 2, slot % GROUPS
                n = STEPS * GROUPS * c + GROUPS * step + g + 1
                bank = by_head(core_bank[g][:, :], P)
                if phase == 0:
                    act.wait_ge(square_ready, n)
                    activation(group(EE, g), bank, ACT.Copy).then_inc(square_copied, 1)
                else:
                    dst = E_work if step < STEPS - 1 else E_last
                    act.wait_ge(product_ready, n)
                    activation(group(dst, g), bank, ACT.Copy, scale=0.25).then_inc(E_copied, 1)

            def before(p, h):
                if h == 5:
                    act.wait_ge(pre_T_ready, p + 1)
                    activation(xcT_pre[:], pre_bank[0][:, 0:2 * P], ACT.Copy).then_inc(pre_T_copied, 1)
                if h == 8:
                    act.wait_ge(v0_copied, p + 1)
                    activation(q0T[:], pre_bank[1][:, 0:P], ACT.Identity, bias=field("bq0"))
                    activation(k0T[:], pre_bank[1][:, P:2 * P], ACT.Identity, bias=field("bk0")).then_inc(q0k0_copied, 1)
                for g, at in enumerate((13, 15, 25, 27)):
                    if h == at + 2:
                        act.wait_ge(negmax0_ready, GROUPS * p + g + 1)
                        for j in range(GROUP):
                            hd = GROUP * g + j
                            last = activation(A[:, hd, :], pre_bank[g % 2][:, P * j:P * (j + 1)], ACT.Exp,
                                              bias=negmax0[:, hd:hd + 1], accum_out=rowsum0[:, hd:hd + 1])
                        last.then_inc(exp0_done, 1)
                for g, at in enumerate((21, 23, 33, 35)):
                    if h == at:
                        act.wait_ge(A_T_ready, GROUPS * p + g + 1)
                        activation(group(A_T, g), by_head(pre_bank[g % 2][:, :], P), ACT.Copy).then_inc(A_T_copied, 1)

            def after(p, h):
                if h == 17:
                    act.wait_ge(X0T_ready, p + 1)
                    activation(XcT[:], post_bank[0][:, 0:2 * P], ACT.Copy).then_inc(X0T_copied, 1)
                if h == 20:
                    act.wait_ge(v1_copied, p + 1)
                    activation(k1T[:], post_bank[1][:, P:2 * P], ACT.Identity, bias=field("bk1")).then_inc(k1_copied, 1)
                for n, at in enumerate((24, 43, 68)):
                    if h == at:
                        act.wait_ge(xnT_ready, 3 * p + n + 1)
                        activation(xnT[:], post_bank[n % 2][:, 0:P], ACT.Copy).then_inc(xnT_copied, 1)
                for n, at in enumerate((27, 70)):
                    if h == at:
                        act.wait_ge(logits_copied, 2 * p + n + 1)
                        e = E0N if n == 0 else E1N
                        activation(gate_e[:, 0:e], logits[:, 0:e], ACT.Exp, scale=-1.0).then_inc(gate_exp_done, 1)
                for i, at in enumerate((26, 30, 34)):
                    if h == at:
                        n = BANK if i < 2 else P
                        if i < 2:
                            act.wait_ge(gate_up_ready, 2 * p + i + 1)
                        else:
                            act.wait_ge(shared_up_ready, p + 1)
                        if i > 0:
                            act.wait_ge(swish_ready, 3 * p + i)
                        activation(act_t[:, 0:n], post_bank[0][:, 0:n], ACT.Tanh, scale=0.5).then_inc(tanh_done, 1)
                for k, at in enumerate((36, 37, 38, 75, 76, 77)):
                    if h == at:
                        n, i = k // 3, k % 3
                        act.wait_ge(hiddenT_ready, 6 * p + k + 1)
                        m = min(4, CHUNKS - 4 * i)
                        activation(hiddenT[:, 4 * i:4 * i + m, :], by_head(post_bank[(i + 1) % 2][:, 0:P * m], P),
                                   ACT.Copy).then_inc(hiddenT_copied, 1)
                for g, at in enumerate((48, 49, 56, 57)):
                    if h == at:
                        act.wait_ge(negmax1_ready, GROUPS * p + g + 1)
                        for j in range(GROUP):
                            hd = GROUP * g + j
                            last = activation(P1[:, hd, :], S1[:, hd, :], ACT.Exp,
                                              bias=negmax1[:, hd:hd + 1], accum_out=rowsum1[:, hd:hd + 1])
                        last.then_inc(exp1_done, 1)
                for g, at in enumerate((50, 51, 58, 59)):
                    if h == at:
                        act.wait_ge(P1_T_ready, GROUPS * p + g + 1)
                        activation(group(P1_T, g), by_head(post_bank[(g + 1) % 2][:, :], P), ACT.Copy).then_inc(P1_T_copied, 1)
                if h == 63:
                    act.wait_ge(X1T_ready, p + 1)
                    activation(X1T[:], post_bank[0][:, 0:P], ACT.Copy).then_inc(X1T_copied, 1)
                for i, at in enumerate((70, 71, 72)):
                    if h == at:
                        n = BANK if i < 2 else P
                        act.wait_ge(up1_ready, 3 * p + i + 1)
                        if i == 1:
                            act.wait_ge(hidden1_ready, 3 * p + i)
                        if i == 2:
                            act.wait_ge(hidden1_ready, 3 * p + i)
                        activation(act_t[:, 0:n], post_bank[i % 2][:, 0:n], ACT.Relu).then_inc(relu_done, 1)

            def body(c, has_next, has_previous):
                for h in range(HALVES):
                    core_half(c, h)
                    if has_previous:
                        after(c - 1, h)
                    if has_next:
                        before(c + 1, h)

            def edge(first, last):
                for h in range(HALVES):
                    if first is not None:
                        before(first, h)
                    if last is not None:
                        after(last, h)

            pipeline(act, body, edge)

        @block.vector
        def _(dve):
            v = nc.vector
            dve.wait_ge(first_loaded, 16)
            dve.wait_ge(pool_consts, 1)

            def hold():
                v.tensor_copy(held[:], const_eps[:])

            def core_half(c, h):
                slot = h // 2
                step, phase, g = slot // (2 * GROUPS), slot // GROUPS % 2, slot % GROUPS
                if h % 2 == 0 or phase == 1:
                    return
                src = E_first if step == 0 else E_work
                n = STEPS * GROUPS * c + GROUPS * step + g + 1
                if step == 0:
                    dve.wait_ge(E_first_ready, GROUPS * c + g + 1)
                dve.wait_ge(square_copied, n)
                v.scalar_tensor_tensor(out=group(F, g), in0=group(src, g), scalar=3.0, in1=by_head(core_bank[g][:, :], P),
                                       op0=ALU.mult, op1=ALU.add).then_inc(F_ready, 1)

            def before(p, h):
                if h == 0:
                    dve.wait_ge(x_pre_loaded, 16 * p + 16)
                    v.bn_stats(stats_pre[:], x_pre[:]).then_inc(pre_stats_done, 1)
                    dve.wait_ge(pre_stats_done, p + 1)
                    hold()
                    v.bn_aggr(mv_pre[:], stats_pre[:]).then_inc(pre_var_ready, 1)
                if h == 3:
                    dve.wait_ge(pre_rstd_ready, p + 1)
                    v.tensor_scalar(xn_pre[:], x_pre[:], mv_pre[:, 0:1], rstd_pre[:, 1:2], ALU.subtract,
                                    ALU.mult).then_inc(pre_xn_ready, 1)
                if h == 8:
                    dve.wait_ge(qkv0_ready, p + 1)
                    v.tensor_tensor(v0[:].rearrange("p h c -> p (h c)"), pre_bank[1][:, 2 * P:3 * P], field("bv0"),
                                    ALU.add).then_inc(v0_copied, 1)
                for g, at in enumerate((13, 15, 25, 27)):
                    if h == at:
                        dve.wait_ge(scores0_ready, GROUPS * p + g + 1)
                        v.tensor_reduce(negmax0[:, GROUP * g:GROUP * (g + 1)], by_head(pre_bank[g % 2][:, :], P), AX.X, ALU.max,
                                        negate=True).then_inc(negmax0_ready, 1)
                    if h == at + 4:
                        dve.wait_ge(exp0_done, GROUPS * p + g + 1)
                        v.reciprocal(rinv0[:, GROUP * g:GROUP * (g + 1)], rowsum0[:, GROUP * g:GROUP * (g + 1)])\
                            .then_inc(rinv0_ready, 1)
                for g, at in enumerate((21, 23, 33, 35)):
                    if h == at:
                        dve.wait_ge(A_T_copied, GROUPS * p + g + 1)
                        v.tensor_reduce(colsum[:, GROUP * g:GROUP * (g + 1)], group(A_T, g), AX.X,
                                        ALU.add).then_inc(colsum_ready, 1)
                if h == 38:
                    dve.wait_ge(Av_ready, p + 1)
                    wait_prior(dve, Av_kept, p)
                    v.tensor_copy(Av_next[:].rearrange("p h c -> p (h c)"), pre_bank[0][:, 0:P]).then_inc(Av_copied, 1)
                if h == 39:
                    dve.wait_ge(colsumT_ready, p + 1)
                    v.tensor_reduce(colmax[0:HEADS, 0:1], pre_bank[1][0:HEADS, 0:P], AX.X, ALU.max,
                                    negate=True).then_inc(colmax_steps, 1)
                    dve.wait_ge(colmax_steps, 3 * p + 1)
                    v.reciprocal(colmax[0:HEADS, 1:2], colmax[0:HEADS, 0:1]).then_inc(colmax_steps, 1)
                    dve.wait_ge(colmax_steps, 3 * p + 2)
                    v.tensor_scalar(scale_diag[0:HEADS, :], ident[0:HEADS, 0:HEADS], colmax[0:HEADS, 1:2], None,
                                    ALU.mult).then_inc(colmax_steps, 1)
                if h == 42:
                    dve.wait_ge(scale_ready, p + 1)
                    v.tensor_copy(neg_scale[:], pre_bank[1][:, P:P + HEADS]).then_inc(scale_copied, 1)
                for g, at in enumerate((45, 49, 53, 57)):
                    if h == at:
                        dve.wait_ge(gram_ready, GROUPS * p + g + 1)
                        dve.wait_ge(scale_copied, p + 1)
                        for j in range(GROUP):
                            hd = GROUP * g + j
                            last = v.scalar_tensor_tensor(out=E_first[:, hd, :], in0=pre_bank[g % 2][:, P * j:P * (j + 1)],
                                                          scalar=neg_scale[:, hd:hd + 1], in1=ident, op0=ALU.mult, op1=ALU.add)
                        last.then_inc(E_first_ready, 1)

            def norm_stats(p, n, x):
                v.bn_stats(stats_post[:], x[:]).then_inc(post_stats_done, 1)
                dve.wait_ge(post_stats_done, 3 * p + n + 1)
                hold()
                v.bn_aggr(mv_post[:], stats_post[:]).then_inc(post_var_ready, 1)

            def norm_apply(p, n, x):
                dve.wait_ge(post_rstd_ready, 3 * p + n + 1)
                v.tensor_scalar(xn_post[:], x[:], mv_post[:, 0:1], rstd_post[:, 1:2], ALU.subtract,
                                ALU.mult).then_inc(post_xn_ready, 1)

            def count_better(step, values, n, low):
                g3, e3 = (t[:, 0:n * n].rearrange("p (i j) -> p i j", j=n) for t in (greater, equal))
                v.tensor_tensor(g3, repeated(values, n), across(values, n), ALU.is_gt).then_inc(gate_steps, 1)
                v.tensor_tensor(e3, repeated(values, n), across(values, n), ALU.is_equal).then_inc(gate_steps, 1)
                step(2)
                v.tensor_tensor(equal[:, 0:n * n], equal[:, 0:n * n], low, ALU.mult).then_inc(gate_steps, 1)
                step(3)
                v.tensor_tensor(greater[:, 0:n * n], greater[:, 0:n * n], equal[:, 0:n * n], ALU.add).then_inc(gate_steps, 1)
                step(4)
                v.tensor_reduce(rank[:, 0:n], g3, AX.X, ALU.add).then_inc(gate_steps, 1)
                step(5)

            def weigh_chosen(step, n, k):
                v.scalar_tensor_tensor(out=chosen[:, 0:n], in0=rank[:, 0:n], scalar=float(k), in1=score[:, 0:n],
                                       op0=ALU.is_lt, op1=ALU.mult).then_inc(gate_steps, 1)
                step(1)
                v.tensor_reduce(total[:, 0:1], chosen[:, 0:n], AX.X, ALU.add).then_inc(gate_steps, 1)
                step(2)

            def gate0_front(p):
                at = GATES * p

                def step(k):
                    dve.wait_ge(gate_steps, at + k)
                dve.wait_ge(gate_exp_done, 2 * p + 1)
                v.tensor_scalar(gate_d[:], gate_e[:], 1.0, None, ALU.add).then_inc(gate_steps, 1)
                step(1)
                v.reciprocal(score[:], gate_d[:]).then_inc(gate_steps, 1)
                step(2)
                s3 = score[:].rearrange("p (g e) -> p g e", g=G0N)
                v.tensor_tensor(pairs[:, :, 0:3], s3[:, :, 0:3], s3[:, :, 1:4], ALU.add)
                v.tensor_tensor(pairs[:, :, 3:5], s3[:, :, 0:2], s3[:, :, 2:4], ALU.add)
                v.tensor_tensor(pairs[:, :, 5:6], s3[:, :, 0:1], s3[:, :, 3:4], ALU.add).then_inc(gate_steps, 1)
                step(3)
                v.tensor_reduce(gscore[:], pairs[:, :, :], AX.X, ALU.max).then_inc(gate_steps, 1)
                step(4)
                count_better(lambda k: step(4 + k), gscore[:], G0N, field("low4"))
                v.tensor_scalar(penalty[:], rank[:, 0:G0N], 2.0, -4.0, ALU.is_ge, ALU.mult).then_inc(gate_steps, 1)
                step(10)
                v.tensor_tensor(choice[:].rearrange("p (g e) -> p g e", g=G0N), s3, across(penalty[:], E0N // G0N),
                                ALU.add).then_inc(gate_steps, 1)
                step(11)

            def gate0_back(p):
                at = GATES * p

                def step(k):
                    dve.wait_ge(gate_steps, at + 11 + k)
                count_better(step, choice[:], E0N, field("low16"))
                weigh_chosen(lambda k: step(5 + k), E0N, 4)
                finish_gate(p, 0, E0N)

            def gate1(p):
                at = GATES * p + GATE0

                def step(k):
                    dve.wait_ge(gate_steps, at + k)
                dve.wait_ge(logits_copied, 2 * p + 2)
                v.tensor_tensor(choice[:, 0:E1N], logits[:, 0:E1N], field("lb"), ALU.add)
                dve.wait_ge(gate_exp_done, 2 * p + 2)
                v.tensor_scalar(gate_d[:, 0:E1N], gate_e[:, 0:E1N], 1.0, None, ALU.add).then_inc(gate_steps, 1)
                step(1)
                v.reciprocal(score[:, 0:E1N], gate_d[:, 0:E1N])
                count_better(lambda k: step(1 + k), choice[:, 0:E1N], E1N, field("low8"))
                weigh_chosen(lambda k: step(6 + k), E1N, 2)
                finish_gate(p, 1, E1N)

            def finish_gate(p, n, experts):
                v.tensor_scalar(total[:, 1:2], total[:, 0:1], SUM_EPS, None, ALU.add).then_inc(total_eps, 1)
                dve.wait_ge(total_eps, 2 * p + n + 1)
                v.reciprocal(total[:, 2:3], total[:, 1:2]).then_inc(total_inverse, 1)
                dve.wait_ge(total_inverse, 2 * p + n + 1)
                v.tensor_scalar(combine[:, 0:experts], chosen[:, 0:experts], total[:, 2:3], None,
                                ALU.mult).then_inc(combine_ready, 1)

            def swish_and_gate(p, i):
                n = BANK if i < 2 else P
                lin = post_bank[1][:, 0:n] if i < 2 else post_bank[0][:, P:2 * P]
                if i > 0:
                    dve.wait_ge(hidden0_ready, 3 * p + i)
                else:
                    wait_prior(dve, hidden1_ready, 3 * p)
                dve.wait_ge(tanh_done, 3 * p + i + 1)
                v.scalar_tensor_tensor(out=act_g[:, 0:n], in0=act_t[:, 0:n], scalar=1.0, in1=post_bank[0][:, 0:n],
                                       op0=ALU.add, op1=ALU.mult).then_inc(swish_ready, 1)
                if i < 2:
                    dve.wait_ge(up_ready, 2 * p + i + 1)
                dve.wait_ge(swish_ready, 3 * p + i + 1)
                if i == 0:
                    wait_prior(dve, down_ready, 2 * p)
                v.scalar_tensor_tensor(out=hidden[:, BANK * i:BANK * i + n], in0=act_g[:, 0:n], scalar=0.5, in1=lin,
                                       op0=ALU.mult, op1=ALU.mult).then_inc(hidden0_ready, 1)

            def after(p, h):
                if h < 12 and h % 2 == 0:
                    r, f = h // 4, h // 2 % 2
                    n = HEADS // 2
                    dve.wait_ge(u_ready, 8 * p + h // 2 + 1)
                    v.tensor_copy(U[r][:, n * f:n * (f + 1), :], by_head(post_bank[f][:, 0:P // 2], DH)).then_inc(u_copied, 1)
                if h in (12, 14):
                    f = h // 2 % 2
                    n = HEADS // 2
                    part = slice(n * f, n * (f + 1))
                    dve.wait_ge(u_ready, 8 * p + h // 2 + 1)
                    dve.wait_ge(u_copied, 6 * p + 5 + f)
                    v.scalar_tensor_tensor(out=u34[:, part, :], in0=U[2][:, part, :], scalar=3.0,
                                           in1=by_head(post_bank[f][:, 0:P // 2], DH), op0=ALU.mult,
                                           op1=ALU.add).then_inc(u34_ready, 1)
                    dve.wait_ge(u34_ready, 2 * p + f + 1)
                    v.scalar_tensor_tensor(out=X0[:, part, :], in0=u34[:, part, :], scalar=-0.25, in1=Av[:, part, :],
                                           op0=ALU.mult, op1=ALU.add).then_inc(X0_ready, 1)
                if h == 20:
                    dve.wait_ge(x_bo_ready, p + 1)
                    dve.wait_ge(proj0_ready, p + 1)
                    v.tensor_tensor(x1[:], post_bank[1][:, 0:P], x_bo[:], ALU.add).then_inc(x1_ready, 1)
                    v.tensor_tensor(v1[:].rearrange("p h c -> p (h c)"), post_bank[1][:, 2 * P:3 * P], field("bv1"),
                                    ALU.add).then_inc(v1_copied, 1)
                    dve.wait_ge(x1_ready, p + 1)
                    norm_stats(p, 0, x1)
                if h == 22:
                    norm_apply(p, 0, x1)
                for n, at in enumerate((26, 70)):
                    if h == at:
                        dve.wait_ge(logits_ready, 2 * p + n + 1)
                        e = E0N if n == 0 else E1N
                        v.tensor_copy(logits[:, 0:e], post_bank[1][:, 0:e]).then_inc(logits_copied, 1)
                if h == 28:
                    swish_and_gate(p, 0)
                    gate0_front(p)
                if h == 31:
                    gate0_back(p)
                if h == 32:
                    swish_and_gate(p, 1)
                if h == 34:
                    swish_and_gate(p, 2)
                if h == 40:
                    dve.wait_ge(down_ready, 2 * p + 1)
                    wait_prior(dve, x2_bo_ready, p)
                    v.tensor_tensor(x2[:], post_bank[0][:, 0:P], x1[:], ALU.add).then_inc(x2_ready, 1)
                    dve.wait_ge(x2_ready, p + 1)
                    norm_stats(p, 1, x2)
                if h == 42:
                    norm_apply(p, 1, x2)
                if h == 44:
                    dve.wait_ge(q1_ready, p + 1)
                    v.tensor_scalar(q1T[:], post_bank[0][:, 0:P], field("bq1"), SCORE_SCALE, ALU.add,
                                    ALU.mult).then_inc(q1_copied, 1)
                for g, at in enumerate((46, 47, 54, 55)):
                    if h == at:
                        dve.wait_ge(scores1_ready, GROUPS * p + g + 1)
                        if g == 0:
                            dve.wait_ge(scores_filled, p + 1)
                            dve.wait_ge(mask_loaded, 16 * p + 16)
                        hold()
                        v.copy_predicated(group(S1, g), repeated(mask_post[:], GROUP), by_head(post_bank[(g + 1) % 2][:, :], P))\
                            .then_inc(scores1_copied, 1)
                        dve.wait_ge(scores1_copied, GROUPS * p + g + 1)
                        v.tensor_reduce(negmax1[:, GROUP * g:GROUP * (g + 1)], group(S1, g), AX.X, ALU.max,
                                        negate=True).then_inc(negmax1_ready, 1)
                if h == 60:
                    dve.wait_ge(exp1_done, GROUPS * p + GROUPS)
                    v.reciprocal(rinv1[:], rowsum1[:]).then_inc(rinv1_ready, 1)
                if h == 61:
                    dve.wait_ge(av1_ready, p + 1)
                    dve.wait_ge(rinv1_ready, p + 1)
                    v.tensor_tensor(X1[:], by_head(post_bank[1][:, 0:P], DH), across(rinv1[:], DH), ALU.mult).then_inc(X1_ready, 1)
                if h == 65:
                    dve.wait_ge(x2_bo_ready, p + 1)
                    dve.wait_ge(proj1_ready, p + 1)
                    v.tensor_tensor(x3[:], post_bank[1][:, 0:P], x2_bo[:], ALU.add).then_inc(x3_ready, 1)
                    dve.wait_ge(x3_ready, p + 1)
                    norm_stats(p, 2, x3)
                if h == 67:
                    norm_apply(p, 2, x3)
                if h == 71:
                    gate1(p)
                for i, at in enumerate((72, 73)):
                    if h == at:
                        dve.wait_ge(relu_done, 3 * p + i + 1)
                        dve.wait_ge(combine_ready, 2 * p + 2)
                        if i == 1:
                            dve.wait_ge(hidden1_ready, 3 * p + 1)
                        v.tensor_tensor(by_head(act_g[:], P), by_head(act_t[:], P), across(combine[:, 4 * i:4 * i + 4], P),
                                        ALU.mult).then_inc(relu_weighted, 1)
                if h == 79:
                    dve.wait_ge(down_ready, 2 * p + 2)
                    wait_prior(dve, out_stored, 16 * p)
                    v.tensor_tensor(x4[:], post_bank[0][:, 0:P], x3[:], ALU.add).then_inc(x4_ready, 1)

            total_eps, total_inverse = sem("total_eps"), sem("total_inverse")

            def body(c, has_next, has_previous):
                for h in range(HALVES):
                    core_half(c, h)
                    if has_previous:
                        after(c - 1, h)
                    if has_next:
                        before(c + 1, h)

            def edge(first, last):
                for h in range(HALVES):
                    if first is not None:
                        before(first, h)
                    if last is not None:
                        after(last, h)

            pipeline(dve, body, edge)

        @block.gpsimd
        def _(pool):
            g_ = nc.gpsimd
            g_.memset(const_eps[:], LN_EPS)
            g_.memset(const_mhalf[:], -0.5).then_inc(pool_consts, 1)
            pool.wait_ge(pool_consts, 1)
            pool.wait_ge(first_loaded, 16)

            def inverse_root(var, rstd, veps_sem, rstd_sem, count):
                g_.tensor_tensor(rstd[:, 0:1], var, const_eps[:], ALU.add).then_inc(veps_sem, 1)
                pool.wait_ge(veps_sem, count)
                g_.tensor_tensor(rstd[:, 1:2], rstd[:, 0:1], const_mhalf[:], ALU.pow).then_inc(rstd_sem, 1)

            def before(p, h):
                if h == 1:
                    pool.wait_ge(pre_var_ready, p + 1)
                    inverse_root(mv_pre[:, 1:2], rstd_pre, pre_veps_ready, pre_rstd_ready, p + 1)
                if h == 8:
                    pool.wait_ge(q0k0_copied, p + 1)
                    g_.tensor_tensor(k0m[:], repeated(k0T[:], GROUP), across(field("rowmask"), P), ALU.mult).then_inc(k0_masked, 1)
                for g, at in enumerate((13, 15, 25, 27)):
                    if h == at + 4:
                        pool.wait_ge(rinv0_ready, GROUPS * p + g + 1)
                        g_.tensor_tensor(group(A, g), group(A, g), across(rinv0[:, GROUP * g:GROUP * (g + 1)], P),
                                         ALU.mult).then_inc(A_ready, 1)

            def after(p, h):
                if h == 10:
                    pool.wait_ge(rest_loaded, 16)
                    pool.wait_ge(x_post_loaded, 16 * p + 16)
                    g_.tensor_tensor(x_bo[:], x_post[:], field("bo0"), ALU.add).then_inc(x_bo_ready, 1)
                if h == 14:
                    wait_prior(pool, exp1_done, GROUPS * p)
                    g_.tensor_tensor(held_pool[:], const_eps[:], const_eps[:], ALU.add)
                    g_.memset(S1[:], MASKED).then_inc(scores_filled, 1)
                for n, at in enumerate((20, 40, 65)):
                    if h == at:
                        pool.wait_ge(post_var_ready, 3 * p + n + 1)
                        inverse_root(mv_post[:, 1:2], rstd_post, post_veps_ready, post_rstd_ready, 3 * p + n + 1)
                if h == 22:
                    pool.wait_ge(k1_copied, p + 1)
                    g_.tensor_tensor(k1m[:], repeated(k1T[:], GROUP), across(field("rowmask"), P), ALU.mult).then_inc(k1_masked, 1)
                for i, at in enumerate((33, 34)):
                    if h == at:
                        pool.wait_ge(combine_ready, 2 * p + 1)
                        pool.wait_ge(hidden0_ready, 3 * p + i + 1)
                        part = hidden[:, BANK * i:BANK * (i + 1)].rearrange("p (e f) -> p e f", f=UP // E0N)
                        n = E0N // 2
                        g_.tensor_tensor(part, part, across(combine[:, n * i:n * (i + 1)], UP // E0N),
                                         ALU.mult).then_inc(hidden0_scaled, 1)
                if h == 42:
                    pool.wait_ge(x2_ready, p + 1)
                    wait_prior(pool, x3_ready, p)
                    g_.tensor_tensor(x2_bo[:], x2[:], field("bo1"), ALU.add).then_inc(x2_bo_ready, 1)
                for i, at in enumerate((72, 73, 74)):
                    if h == at:
                        if i < 2:
                            pool.wait_ge(relu_weighted, 2 * p + i + 1)
                            g_.tensor_tensor(hidden[:, BANK * i:BANK * (i + 1)], act_g[:], act_t[:], ALU.mult)\
                                .then_inc(hidden1_ready, 1)
                        else:
                            pool.wait_ge(relu_done, 3 * p + 3)
                            g_.tensor_tensor(hidden[:, UP:UP + P], act_t[:, 0:P], act_t[:, 0:P], ALU.mult)\
                                .then_inc(hidden1_ready, 1)

            def body(c, has_next, has_previous):
                for h in range(HALVES):
                    if has_previous:
                        after(c - 1, h)
                    if has_next:
                        before(c + 1, h)

            def edge(first, last):
                for h in range(HALVES):
                    if first is not None:
                        before(first, h)
                    if last is not None:
                        after(last, h)

            pipeline(pool, body, edge)


def pack_weights(np, a):
    def row(v):
        return np.broadcast_to(np.asarray(v)[None, :], (P, len(v)))

    def col(v):
        return np.asarray(v)[:, None]

    def low(n):
        return row(np.tril(np.ones((n, n), np.float32), -1).ravel())

    def chunks(w, shared):
        w = np.concatenate([w, shared], 0)
        return w.reshape(CHUNKS, P, P).transpose(1, 0, 2).reshape(P, CHUNKS * P)

    rows = np.arange(P)
    rowmask = (rows[:, None] % 32 // DH == np.arange(GROUP)[None, :]).astype(np.float32)
    f = {
        "wq0": a["L0_xattn_Wq"], "wk0": a["L0_xattn_Wk"], "wv0": a["L0_xattn_Wv"], "wo0": a["L0_xattn_Wo"],
        "bq0": col(a["L0_xattn_bq"]), "bk0": col(a["L0_xattn_bk"]), "bv0": row(a["L0_xattn_bv"]),
        "bo0": row(a["L0_xattn_bo"]),
        "wq1": a["L1_xattn_Wq"].T, "wk1": a["L1_xattn_Wk"].T, "wv1": a["L1_xattn_Wv"].T, "wo1": a["L1_xattn_Wo"].T,
        "bq1": col(a["L1_xattn_bq"]), "bk1": col(a["L1_xattn_bk"]), "bv1": row(a["L1_xattn_bv"]),
        "bo1": row(a["L1_xattn_bo"]),
        "ident": np.eye(P, dtype=np.float32), "rowmask": rowmask, "ones": np.ones((P, P), np.float32),
        "gate0": a["L0_ffn_w_gate"].T, "gate1": a["L1_ffn_gate_w"].T, "lb": row(a["L1_ffn_lb_bias"]),
        "low4": low(G0N), "low16": low(E0N), "low8": low(E1N),
        "w1": a["L0_ffn_w1_e"].reshape(UP, P).T, "w3": a["L0_ffn_w3_e"].reshape(UP, P).T,
        "w1s": a["L0_ffn_w1_s"].T, "w3s": a["L0_ffn_w3_s"].T,
        "w2": chunks(a["L0_ffn_w2_e"].transpose(0, 2, 1).reshape(UP, P), a["L0_ffn_w2_s"].T),
        "up1": a["L1_ffn_w1"].reshape(UP, P).T, "up1s": a["L1_ffn_cfc"].T,
        "down1": chunks(a["L1_ffn_w2"].transpose(0, 2, 1).reshape(UP, P), a["L1_ffn_cproj"].T),
    }
    return np.ascontiguousarray(np.concatenate([f[name] for name, _ in FIELDS], axis=1))


def kernel(**inputs):
    import numpy as np
    import concourse.bacc as bacc
    from concourse.bass_utils import run_bass_kernel_spmd

    a = {k: np.asarray(val) for k, val in inputs.items()}
    arrays = {
        "x_dram": np.ascontiguousarray(a["x"]),
        "ctx_dram": np.ascontiguousarray(a["ctx_1024"]),
        "mask_dram": np.ascontiguousarray(a["mask_BxSxS2_bf1"]),
        "weights_dram": pack_weights(np, a),
    }
    nc = bacc.Bacc("TRN2", target_bir_lowering=False, num_devices=1)
    aps = [nc.dram_tensor(n, arr.shape, mybir.dt.from_np(arr.dtype), kind="ExternalInput").ap() for n, arr in arrays.items()]
    out = nc.dram_tensor("out_dram", a["x"].shape, F32, kind="ExternalOutput").ap()
    build(nc, *aps, out)
    r = run_bass_kernel_spmd(nc, [arrays], core_ids=[0])
    return r.results[0]["out_dram"]
```

```python
from contextlib import ExitStack

import concourse.bass as bass
from concourse import mybir

ALU = mybir.AluOpType
ACT = mybir.ActivationFunctionType
AX = mybir.AxisListType
F32 = mybir.dt.float32
U8 = mybir.dt.uint8

P = 128
HEADS = 16
DH = P // HEADS
GROUP = 4
GROUPS = HEADS // GROUP
STEPS = 5
SLOTS = STEPS * 2 * GROUPS
HALVES = 2 * SLOTS
BANK = 512
LN_EPS = 1e-5
SUM_EPS = 1e-6
MASKED = -1e9
SCORE_SCALE = float(DH) ** -0.5

E0N, E1N = 16, 8
G0N = 4
UP = E0N * 64
CHUNKS = UP // P + 1

FIELDS = [("wq0", P), ("wk0", P), ("wv0", P), ("bq0", 1), ("bk0", 1), ("bv0", P), ("ident", P), ("rowmask", HEADS),
          ("ones", P),
          ("wo0", GROUPS * P), ("bo0", P), ("wk1", P), ("wv1", P), ("bk1", 1), ("bv1", P), ("wq1", P), ("bq1", 1),
          ("gate0", E0N), ("low4", G0N * G0N), ("low16", E0N * E0N), ("low8", E1N * E1N),
          ("w1", UP), ("w3", UP), ("w1s", P), ("w3s", P), ("w2", CHUNKS * P),
          ("wo1", GROUPS * P), ("bo1", P), ("gate1", E1N), ("lb", E1N), ("up1", UP), ("up1s", P), ("down1", CHUNKS * P)]
AT = {}
_at = 0
for _name, _n in FIELDS:
    AT[_name] = (_at, _at + _n)
    _at += _n
PACKED = _at
FIRST = AT["ones"][1]


def build(nc, x_d, ctx_d, mask_d, w_d, out_d):
    B = x_d.shape[0]
    with ExitStack() as ctx:
        def sb(name, *shape, dt=F32):
            return ctx.enter_context(nc.sbuf_tensor(name, [P, *shape], dt))

        def sem(name):
            return ctx.enter_context(nc.semaphore(name))

        def both(name, *shape):
            return [sb(f"{name}_{layer}", *shape) for layer in (0, 1)]

        core_bank = [ctx.enter_context(nc.psum_tensor(f"core_bank{g}", [P, BANK], F32)) for g in range(GROUPS)]
        pre_bank = [ctx.enter_context(nc.psum_tensor(f"pre_bank{i}", [P, BANK], F32)) for i in range(2)]
        bank = [ctx.enter_context(nc.psum_tensor(f"layer_bank{i}", [P, BANK], F32)) for i in range(2)]

        W = sb("packed", PACKED)

        def field(name):
            return W[:, AT[name][0]:AT[name][1]]

        E_first = sb("E_first", HEADS, P)
        E_work = sb("E_work", HEADS, P)
        E_last = sb("E_last", HEADS, P)
        EE = sb("EE", HEADS, P)
        F = sb("F", HEADS, P)
        x_pre, ctx_pre = sb("x_pre", P), sb("ctx_pre", P)
        stats_pre, mv_pre, rstd_pre = sb("stats_pre", 6), sb("mv_pre", 2), sb("rstd_pre", 2)
        xn_pre = sb("xn_pre", P)
        xcT_pre = sb("xcT_pre", 2 * P)
        q0T, k0T = sb("q0T", P), sb("k0T", P)
        k0m = sb("k0m", HEADS, P)
        v0 = sb("v0", HEADS, DH)
        negmax0, rowsum0, rinv0 = sb("negmax0", HEADS), sb("rowsum0", HEADS), sb("rinv0", HEADS)
        A, A_T = sb("A", HEADS, P), sb("A_T", HEADS, P)
        colsum, colmax = sb("colsum", HEADS), sb("colmax", 2)
        scale_diag, neg_scale = sb("scale_diag", HEADS), sb("neg_scale", HEADS)
        Av_next, Av = sb("Av_next", HEADS, DH), sb("Av", HEADS, DH)
        AvT_next, AvT = sb("AvT_next", GROUPS, P), sb("AvT", GROUPS, P)
        uT = sb("uT", GROUPS, P)
        U = sb("U", HEADS, DH)
        u34T = sb("u34T", GROUPS, P)
        X0T = sb("X0T", GROUPS, P)
        x_post, x_bo, x1 = sb("x_post", P), sb("x_bo", P), sb("x1", P)
        pairs, gscore, penalty = sb("pairs", G0N, 6), sb("gscore", G0N), sb("penalty", G0N)
        ctx_post = sb("ctx_post", P)
        mask_post = sb("mask_post", P, dt=U8)
        x2, x2_bo, x3, x4 = sb("x2", P), sb("x2_bo", P), sb("x3", P), sb("x4", P)
        xcT_post = sb("xcT_post", 2 * P)
        q1T, k1T = sb("q1T", P), sb("k1T", P)
        k1m = sb("k1m", HEADS, P)
        v1 = sb("v1", HEADS, DH)
        S1 = sb("S1", HEADS, P)
        P1, P1_T = sb("P1", HEADS, P), sb("P1_T", HEADS, P)
        negmax1, rowsum1, rinv1 = sb("negmax1", HEADS), sb("rowsum1", HEADS), sb("rinv1", HEADS)
        X1T = sb("X1T", GROUPS, P)
        stats_q, mv_q, rstd_q, xn_q = sb("stats_q", 6), sb("mv_q", 2), sb("rstd_q", 2), sb("xn_q", P)
        stats, mv, rstd, xn, xnT = both("stats", 6), both("mv", 2), both("rstd", 2), both("xn", P), both("xnT", P)
        logits, gate_e, gate_d, score = both("logits", E0N), both("gate_e", E0N), both("gate_d", E0N), both("score", E0N)
        greater, equal, rank = both("greater", E0N * E0N), both("equal", E0N * E0N), both("rank", E0N)
        choice, chosen, total, combine = both("choice", E0N), both("chosen", E0N), both("total", 3), both("combine", E0N)
        act_t = both("act_t", BANK)
        act_g = both("act_g", BANK)
        hidden, hiddenT = both("hidden", CHUNKS * P), both("hiddenT", CHUNKS, P)
        held, held_pool = sb("held", 1), sb("held_pool", 1)
        const_eps, const_mhalf = sb("const_eps", 1), sb("const_mhalf", 1)
        ident = field("ident")

        first_loaded, rest_loaded = sem("first_loaded"), sem("rest_loaded")
        pool_consts = sem("pool_consts")
        x_pre_loaded, ctx_pre_loaded = sem("x_pre_loaded"), sem("ctx_pre_loaded")
        pre_stats_done, pre_var_ready, pre_veps_ready = sem("pre_stats_done"), sem("pre_var_ready"), sem("pre_veps_ready")
        pre_rstd_ready, pre_xn_ready = sem("pre_rstd_ready"), sem("pre_xn_ready")
        pre_T_ready, pre_T_copied = sem("pre_T_ready"), sem("pre_T_copied")
        qkv0_ready, q0k0_copied, v0_copied = sem("qkv0_ready"), sem("q0k0_copied"), sem("v0_copied")
        k0_masked = sem("k0_masked")
        scores0_ready, negmax0_ready, exp0_done = sem("scores0_ready"), sem("negmax0_ready"), sem("exp0_done")
        rinv0_ready, A_ready = sem("rinv0_ready"), sem("A_ready")
        A_T_ready, A_T_copied, colsum_ready = sem("A_T_ready"), sem("A_T_copied"), sem("colsum_ready")
        AvT_ready, AvT_copied = sem("AvT_ready"), sem("AvT_copied")
        Av_ready, Av_copied, Av_kept = sem("Av_ready"), sem("Av_copied"), sem("Av_kept")
        colsumT_ready, colmax_steps = sem("colsumT_ready"), sem("colmax_steps")
        scale_ready, scale_copied = sem("scale_ready"), sem("scale_copied")
        gram_ready, E_first_ready = sem("gram_ready"), sem("E_first_ready")
        square_ready, square_copied, F_ready = sem("square_ready"), sem("square_copied"), sem("F_ready")
        product_ready, E_copied = sem("product_ready"), sem("E_copied")
        x_post_loaded, x_bo_ready = sem("x_post_loaded"), sem("x_bo_ready")
        uT_ready, uT_copied = sem("uT_ready"), sem("uT_copied")
        u_ready, u_copied = sem("u_ready"), sem("u_copied")
        u34_ready, X0T_ready = sem("u34_ready"), sem("X0T_ready")
        proj0_ready, x1_ready, x2_ready = sem("proj0_ready"), sem("x1_ready"), sem("x2_ready")
        gate_up_ready, up_ready, shared_up_ready = sem("gate_up_ready"), sem("up_ready"), sem("shared_up_ready")
        tanh_done, swish_ready, hidden0_ready = sem("tanh_done"), sem("swish_ready"), sem("hidden0_ready")
        hidden0_scaled = sem("hidden0_scaled")
        ctx_post_loaded, mask_loaded = sem("ctx_post_loaded"), sem("mask_loaded")
        q_stats_done, q_var_ready, q_veps_ready = sem("q_stats_done"), sem("q_var_ready"), sem("q_veps_ready")
        q_rstd_ready, q_xn_ready = sem("q_rstd_ready"), sem("q_xn_ready")
        post_T_ready, post_T_copied = sem("post_T_ready"), sem("post_T_copied")
        qkv1_ready, v1_copied, q1_copied, k1_copied = sem("qkv1_ready"), sem("v1_copied"), sem("q1_copied"), sem("k1_copied")
        k1_masked = sem("k1_masked")
        x2_bo_ready, scores_filled = sem("x2_bo_ready"), sem("scores_filled")
        scores1_ready, scores1_copied = sem("scores1_ready"), sem("scores1_copied")
        negmax1_ready, exp1_done = sem("negmax1_ready"), sem("exp1_done")
        rinv1_ready, P1_ready = sem("rinv1_ready"), sem("P1_ready")
        P1_T_ready, P1_T_copied = sem("P1_T_ready"), sem("P1_T_copied")
        X1T_ready, X1T_copied, proj1_ready, x3_ready = sem("X1T_ready"), sem("X1T_copied"), sem("proj1_ready"), sem("x3_ready")
        up1_ready, relu_done, relu_weighted, hidden1_ready = sem("up1_ready"), sem("relu_done"), sem("relu_weighted"), sem("hidden1_ready")
        x4_ready, out_stored = sem("x4_ready"), sem("out_stored")

        def both_sems(name):
            return [sem(f"{name}_{layer}") for layer in (0, 1)]

        stats_done, var_ready, veps_ready = both_sems("stats_done"), both_sems("var_ready"), both_sems("veps_ready")
        rstd_ready, xn_ready = both_sems("rstd_ready"), both_sems("xn_ready")
        xnT_ready, xnT_copied = both_sems("xnT_ready"), both_sems("xnT_copied")
        logits_ready, logits_copied, gate_exp_done = both_sems("logits_ready"), both_sems("logits_copied"), both_sems("gate_exp_done")
        gate_steps = both_sems("gate_steps")
        combine_ready = both_sems("combine_ready")
        hiddenT_ready, hiddenT_copied, down_ready = both_sems("hiddenT_ready"), both_sems("hiddenT_copied"), both_sems("down_ready")

        GATE_STEPS = [20, 10]

        def group(t, g):
            return t[:, GROUP * g:GROUP * (g + 1), :]

        def of_group(t, g):
            return t[:, GROUP * g:GROUP * (g + 1)]

        def by(ap, n):
            return ap.rearrange("p (h c) -> p h c", c=n)

        def flat(t):
            return t[:].rearrange("p h c -> p (h c)")

        def head_columns(t, g):
            return t[:, GROUP * g:GROUP * (g + 1), :].rearrange("p h c -> p (h c)")

        def across(ap, n):
            return ap.unsqueeze(2).broadcast_to([ap.shape[0], ap.shape[1], n])

        def repeated(ap, n):
            return ap.unsqueeze(1).broadcast_to([ap.shape[0], n, ap.shape[1]])

        def unstaggered(ps, g):
            lead = 32 if g == GROUPS - 1 else 0
            lo = P * g - lead
            return ps[:, lo:lo + GROUP * (32 + DH)].rearrange("p (j c) -> p j c", c=32 + DH)[:, :, lead:lead + DH]

        def core_place(h):
            slot = h // 2
            return slot // (2 * GROUPS), slot // GROUPS % 2, slot % GROUPS

        def wait_prior(engine, semaphore, count):
            if not (isinstance(count, int) and count <= 0):
                engine.wait_ge(semaphore, count)

        block = ctx.enter_context(nc.Block())

        def pipeline(engine, core, before, finish, second):
            def body(c, has_core=True, has_before=True, has_finish=True, has_second=True):
                for h in range(HALVES):
                    if has_core:
                        core(c, h)
                    if has_second:
                        second(c - 2, h)
                    if has_finish:
                        finish(c - 1, h)
                    if has_before:
                        before(c + 1, h)

            body(-1, has_core=False, has_finish=False, has_second=False)
            body(0, has_finish=False, has_second=False)
            body(1, has_second=False)
            body(2)
            with engine.Fori(3, B - 1) as c:
                body(c)
            body(B - 1, has_before=False)
            body(B, has_core=False, has_before=False)
            body(B + 1, has_core=False, has_before=False, has_finish=False)

        SCORES0_AT, A_T_AT, GRAM_AT = (13, 15, 25, 27), (21, 23, 33, 35), (48, 52, 56, 60)
        ROUND_AT, TURN_AT = (0, 5, 10, 15), (3, 8, 13)
        UP0_AT, HIDDEN0_AT = (27, 33, 39), (44, 46, 49)
        SCORES1_AT, P1_T_AT = (13, 16, 19, 22), (24, 27, 30, 33)
        UP1_AT, HIDDEN1_AT = (48, 51, 54), (61, 64, 66)

        @block.sync
        def _(sp):
            sp.dma_start(W[:, 0:FIRST], w_d[:, 0:FIRST]).then_inc(first_loaded, 16)

            def load_before(p):
                wait_prior(sp, pre_xn_ready, p)
                sp.dma_start(x_pre[:], x_d[p]).then_inc(x_pre_loaded, 16)
                wait_prior(sp, pre_T_ready, p)
                sp.dma_start(ctx_pre[:], ctx_d[p]).then_inc(ctx_pre_loaded, 16)

            def load_ctx_second(p):
                wait_prior(sp, post_T_ready, p)
                sp.dma_start(ctx_post[:], ctx_d[p]).then_inc(ctx_post_loaded, 16)

            def load_finish(p):
                wait_prior(sp, x_bo_ready, p)
                sp.dma_start(x_post[:], x_d[p]).then_inc(x_post_loaded, 16)

            def load_mask(p):
                wait_prior(sp, scores1_copied, GROUPS * p)
                sp.dma_start(mask_post[:], mask_d[p]).then_inc(mask_loaded, 16)

            def store(p):
                sp.wait_ge(x4_ready, p + 1)
                sp.dma_start(out_d[p], x4[:]).then_inc(out_stored, 16)

            def during(c, has_before=True, has_finish=True, has_store=True):
                if has_before:
                    load_before(c + 2)
                load_ctx_second(c - 1)
                if has_finish:
                    load_finish(c)
                load_mask(c - 1)
                if has_store:
                    store(c - 2)

            load_before(0)
            sp.dma_start(W[:, FIRST:PACKED], w_d[:, FIRST:PACKED]).then_inc(rest_loaded, 16)
            load_before(1)
            load_before(2)
            load_finish(0)
            during(1, has_store=False)
            with sp.Fori(2, B - 2) as c:
                during(c)
            during(B - 2, has_before=False)
            during(B - 1, has_before=False)
            during(B, has_before=False, has_finish=False)
            store(B - 1)
            sp.wait_ge(out_stored, 16 * B)

        @block.tensor
        def _(pe):
            mm = nc.tensor.matmul
            turn = nc.tensor.transpose
            pe.wait_ge(first_loaded, 16)

            def core(c, h):
                step, phase, g = core_place(h)
                half = h % 2
                src = E_first if step == 0 else E_work
                n = STEPS * GROUPS * c + GROUPS * step + g + 1
                if half == 0 and phase == 0 and step == 0:
                    pe.wait_ge(E_first_ready, GROUPS * c + g + 1)
                    wait_prior(pe, E_copied, STEPS * GROUPS * (c - 1) + (STEPS - 1) * GROUPS + g + 1)
                elif half == 0 and phase == 0:
                    pe.wait_ge(E_copied, n - GROUPS)
                elif half == 0:
                    pe.wait_ge(F_ready, n)
                for j in (2 * half, 2 * half + 1):
                    hd = GROUP * g + j
                    out = core_bank[g][:, P * j:P * (j + 1)]
                    if phase == 0:
                        last = mm(out, src[:, hd, :], src[:, hd, :], start=True, stop=True)
                    else:
                        last = mm(out, EE[:, hd, :], F[:, hd, :], start=True, stop=True)
                if half:
                    last.then_inc(square_ready if phase == 0 else product_ready, 1)

            def apply_transposed(out, u, m):
                for g in range(GROUPS):
                    for j in range(GROUP):
                        last = mm(out[32 * j:32 * j + 32, P * g:P * (g + 1)], head_columns(u, g), m[:, GROUP * g + j, :],
                                  start=True, stop=True)
                return last

            def turn_back(out, u_t):
                for g in range(GROUPS):
                    last = turn(out[:, P * g:P * (g + 1)], u_t[:, g, :], ident)
                return last

            def transpose_x_ctx(p):
                pe.wait_ge(pre_xn_ready, p + 1)
                wait_prior(pe, E_first_ready, GROUPS * p)
                turn(pre_bank[0][:, 0:P], xn_pre[:], ident)
                pe.wait_ge(ctx_pre_loaded, 16 * p + 16)
                turn(pre_bank[0][:, P:2 * P], ctx_pre[:], ident).then_inc(pre_T_ready, 1)

            def project_qkv0(p):
                pe.wait_ge(pre_T_copied, p + 1)
                out = pre_bank[1]
                mm(out[:, 0:P], field("wq0"), xcT_pre[:, 0:P], start=True, stop=True)
                mm(out[:, P:2 * P], field("wk0"), xcT_pre[:, P:2 * P], start=True, stop=True)
                mm(out[:, 2 * P:3 * P], xcT_pre[:, P:2 * P], field("wv0"), start=True, stop=True).then_inc(qkv0_ready, 1)

            def scores0(p, g):
                pe.wait_ge(k0_masked, GROUPS * p + g + 1)
                if g >= 2:
                    pe.wait_ge(A_T_copied, GROUPS * p + g - 1)
                mm(pre_bank[g % 2][:, :], q0T[:], group(k0m, g), start=True, stop=True).then_inc(scores0_ready, 1)

            def transpose_A(p, g):
                pe.wait_ge(A_ready, GROUPS * p + g + 1)
                for j in range(GROUP):
                    last = turn(pre_bank[g % 2][:, P * j:P * (j + 1)], A[:, GROUP * g + j, :], ident)
                last.then_inc(A_T_ready, 1)

            def apply_A(p):
                pe.wait_ge(A_T_copied, GROUPS * p + GROUPS)
                apply_transposed(pre_bank[0], v0, A_T).then_inc(AvT_ready, 1)

            def turn_Av(p):
                pe.wait_ge(AvT_copied, p + 1)
                turn_back(pre_bank[0], AvT_next).then_inc(Av_ready, 1)

            def transpose_colsum(p):
                pe.wait_ge(colsum_ready, GROUPS * p + GROUPS)
                turn(pre_bank[1][0:HEADS, 0:P], colsum[:, :], ident).then_inc(colsumT_ready, 1)

            def spread_scale(p):
                pe.wait_ge(colmax_steps, 3 * p + 3)
                mm(pre_bank[1][:, P:P + HEADS], field("ones")[0:HEADS, :], scale_diag[0:HEADS, :],
                   start=True, stop=True).then_inc(scale_ready, 1)

            def gram(p, g):
                if g == 0:
                    pe.wait_ge(Av_copied, p + 1)
                elif g == 1:
                    pe.wait_ge(scale_copied, p + 1)
                else:
                    pe.wait_ge(E_first_ready, GROUPS * p + g - 1)
                for j in range(GROUP):
                    a_t = A_T[:, GROUP * g + j, :]
                    last = mm(pre_bank[g % 2][:, P * j:P * (j + 1)], a_t, a_t, start=True, stop=True)
                last.then_inc(gram_ready, 1)

            def before(p, h):
                if h == 5:
                    transpose_x_ctx(p)
                if h == 8:
                    project_qkv0(p)
                if h in SCORES0_AT:
                    scores0(p, SCORES0_AT.index(h))
                if h in A_T_AT:
                    transpose_A(p, A_T_AT.index(h))
                if h == 38:
                    apply_A(p)
                if h == 39:
                    transpose_colsum(p)
                if h == 41:
                    turn_Av(p)
                if h == 43:
                    spread_scale(p)
                if h in GRAM_AT:
                    gram(p, GRAM_AT.index(h))

            def apply_E(p, r):
                if r == 0:
                    pe.wait_ge(Av_kept, p + 1)
                    pe.wait_ge(E_copied, STEPS * GROUPS * (p + 1))
                    wait_prior(pe, x2_ready, p)
                else:
                    pe.wait_ge(u_copied, 3 * p + r)
                apply_transposed(bank[0], Av if r == 0 else U, E_last).then_inc(uT_ready, 1)

            def turn_u(p, r):
                pe.wait_ge(uT_copied, 3 * p + r + 1)
                turn_back(bank[0], uT).then_inc(u_ready, 1)

            def project_out(p, layer):
                if layer == 0:
                    pe.wait_ge(rest_loaded, 16)
                    pe.wait_ge(X0T_ready, p + 1)
                    x_t, weights, done = X0T, AT["wo0"][0], proj0_ready
                else:
                    pe.wait_ge(X1T_copied, p + 1)
                    x_t, weights, done = X1T, AT["wo1"][0], proj1_ready
                for g in range(GROUPS):
                    last = mm(bank[layer][:, 0:P], x_t[:, g, :], W[:, weights + P * g:weights + P * (g + 1)],
                              start=(g == 0), stop=(g == GROUPS - 1))
                last.then_inc(done, 1)

            def transpose_xn(p, layer):
                pe.wait_ge(xn_ready[layer], p + 1)
                turn(bank[layer][:, 0:P], xn[layer][:], ident).then_inc(xnT_ready[layer], 1)

            def gate_logits(p, layer):
                pe.wait_ge(xnT_copied[layer], p + 1)
                w = field("gate0") if layer == 0 else field("gate1")
                mm(bank[layer][:, 0:w.shape[1]], xnT[layer][:], w, start=True, stop=True).then_inc(logits_ready[layer], 1)

            def transpose_hidden(p, layer, i):
                if layer == 0 and i < 2:
                    pe.wait_ge(hidden0_scaled, 2 * p + i + 1)
                if layer == 0:
                    pe.wait_ge(hidden0_ready, 3 * p + 3)
                if layer == 1:
                    pe.wait_ge(hidden1_ready, 3 * p + i + 1)
                    if i == 0:
                        pe.wait_ge(relu_done, 3 * p + 3)
                if i > 0:
                    pe.wait_ge(hiddenT_copied[layer], 3 * p + i)
                for k in range(4 * i, min(4 * i + 4, CHUNKS)):
                    last = turn(bank[layer][:, P * (k - 4 * i):P * (k - 4 * i + 1)], hidden[layer][:, P * k:P * (k + 1)], ident)
                last.then_inc(hiddenT_ready[layer], 1)

            def project_down(p, layer):
                pe.wait_ge(hiddenT_copied[layer], 3 * p + 3)
                a = AT["w2"][0] if layer == 0 else AT["down1"][0]
                for k in range(CHUNKS):
                    last = mm(bank[layer][:, 0:P], hiddenT[layer][:, k, :], W[:, a + P * k:a + P * (k + 1)],
                              start=(k == 0), stop=(k == CHUNKS - 1))
                last.then_inc(down_ready[layer], 1)

            def up_gate(p, i):
                if i == 0:
                    pe.wait_ge(logits_copied[0], p + 1)
                else:
                    pe.wait_ge(hidden0_ready, 3 * p + i)
                a = AT["w1"][0] + BANK * i
                mm(bank[0][:, :], xnT[0][:], W[:, a:a + BANK], start=True, stop=True).then_inc(gate_up_ready, 1)

            def up_linear(p, i):
                pe.wait_ge(swish_ready, 3 * p + i + 1)
                a = AT["w3"][0] + BANK * i
                mm(bank[0][:, :], xnT[0][:], W[:, a:a + BANK], start=True, stop=True).then_inc(up_ready, 1)

            def up_shared(p):
                pe.wait_ge(hidden0_ready, 3 * p + 2)
                mm(bank[0][:, 0:P], xnT[0][:], field("w1s"), start=True, stop=True)
                mm(bank[0][:, P:2 * P], xnT[0][:], field("w3s"), start=True, stop=True).then_inc(shared_up_ready, 1)

            def finish(p, h):
                if h in ROUND_AT:
                    apply_E(p, ROUND_AT.index(h))
                if h in TURN_AT:
                    turn_u(p, TURN_AT.index(h))
                if h == 19:
                    project_out(p, 0)
                if h == 23:
                    transpose_xn(p, 0)
                if h == 25:
                    gate_logits(p, 0)
                if h in UP0_AT[:2]:
                    up_gate(p, UP0_AT.index(h))
                if h - 3 in UP0_AT[:2]:
                    up_linear(p, UP0_AT.index(h - 3))
                if h == UP0_AT[2]:
                    up_shared(p)
                if h in HIDDEN0_AT:
                    transpose_hidden(p, 0, HIDDEN0_AT.index(h))
                if h == 51:
                    project_down(p, 0)

            def transpose_x2_ctx(p):
                pe.wait_ge(q_xn_ready, p + 1)
                wait_prior(pe, x4_ready, p)
                turn(bank[1][:, 0:P], xn_q[:], ident)
                pe.wait_ge(ctx_post_loaded, 16 * p + 16)
                turn(bank[1][:, P:2 * P], ctx_post[:], ident).then_inc(post_T_ready, 1)

            def project_qkv1(p):
                pe.wait_ge(post_T_copied, p + 1)
                out = bank[1]
                mm(out[:, 0:P], field("wq1"), xcT_post[:, 0:P], start=True, stop=True)
                mm(out[:, P:2 * P], field("wk1"), xcT_post[:, P:2 * P], start=True, stop=True)
                mm(out[:, 2 * P:3 * P], xcT_post[:, P:2 * P], field("wv1"), start=True, stop=True).then_inc(qkv1_ready, 1)

            def scores1(p, g):
                pe.wait_ge(k1_masked, GROUPS * p + g + 1)
                if g > 0:
                    pe.wait_ge(scores1_copied, GROUPS * p + g)
                mm(bank[1][:, :], q1T[:], group(k1m, g), start=True, stop=True).then_inc(scores1_ready, 1)

            def transpose_P1(p, g):
                pe.wait_ge(P1_ready, GROUPS * p + g + 1)
                if g == 0:
                    pe.wait_ge(scores1_copied, GROUPS * p + GROUPS)
                else:
                    pe.wait_ge(P1_T_copied, GROUPS * p + g)
                for j in range(GROUP):
                    last = turn(bank[1][:, P * j:P * (j + 1)], P1[:, GROUP * g + j, :], ident)
                last.then_inc(P1_T_ready, 1)

            def apply_P1(p):
                pe.wait_ge(P1_T_copied, GROUPS * p + GROUPS)
                apply_transposed(bank[1], v1, P1_T).then_inc(X1T_ready, 1)

            def up1(p, i):
                if i == 0:
                    pe.wait_ge(logits_copied[1], p + 1)
                else:
                    pe.wait_ge(relu_done, 3 * p + i)
                if i < 2:
                    a, n = AT["up1"][0] + BANK * i, BANK
                else:
                    a, n = AT["up1s"][0], P
                mm(bank[1][:, 0:n], xnT[1][:], W[:, a:a + n], start=True, stop=True).then_inc(up1_ready, 1)

            def second(p, h):
                if h == 4:
                    transpose_x2_ctx(p)
                if h == 7:
                    project_qkv1(p)
                if h in SCORES1_AT:
                    scores1(p, SCORES1_AT.index(h))
                if h in P1_T_AT:
                    transpose_P1(p, P1_T_AT.index(h))
                if h == 36:
                    apply_P1(p)
                if h == 39:
                    project_out(p, 1)
                if h == 43:
                    transpose_xn(p, 1)
                if h == 46:
                    gate_logits(p, 1)
                if h in UP1_AT:
                    up1(p, UP1_AT.index(h))
                if h in HIDDEN1_AT:
                    transpose_hidden(p, 1, HIDDEN1_AT.index(h))
                if h == 69:
                    project_down(p, 1)

            pipeline(pe, core, before, finish, second)

        @block.scalar
        def _(act):
            act.wait_ge(first_loaded, 16)
            activation = nc.scalar.activation

            def core(c, h):
                if h == 36:
                    wait_prior(act, X0T_ready, c)
                    act.wait_ge(Av_copied, c + 1)
                    activation(Av[:], Av_next[:], ACT.Copy)
                    activation(AvT[:], AvT_next[:], ACT.Copy).then_inc(Av_kept, 1)
                if h % 2 == 0:
                    return
                step, phase, g = core_place(h)
                n = STEPS * GROUPS * c + GROUPS * step + g + 1
                product = by(core_bank[g][:, :], P)
                if phase == 0:
                    act.wait_ge(square_ready, n)
                    activation(group(EE, g), product, ACT.Copy).then_inc(square_copied, 1)
                else:
                    dst = E_work if step < STEPS - 1 else E_last
                    act.wait_ge(product_ready, n)
                    activation(group(dst, g), product, ACT.Copy, scale=0.25).then_inc(E_copied, 1)

            def exp_heads(g, out, scores, negmax, rowsum):
                for j in range(GROUP):
                    hd = GROUP * g + j
                    last = activation(out[:, hd, :], scores(j), ACT.Exp, bias=negmax[:, hd:hd + 1],
                                      accum_out=rowsum[:, hd:hd + 1])
                return last

            def before(p, h):
                if h == 5:
                    act.wait_ge(pre_T_ready, p + 1)
                    activation(xcT_pre[:], pre_bank[0][:, 0:2 * P], ACT.Copy).then_inc(pre_T_copied, 1)
                if h == 8:
                    act.wait_ge(v0_copied, p + 1)
                    activation(q0T[:], pre_bank[1][:, 0:P], ACT.Identity, bias=field("bq0"))
                    activation(k0T[:], pre_bank[1][:, P:2 * P], ACT.Identity, bias=field("bk0")).then_inc(q0k0_copied, 1)
                if h - 1 in SCORES0_AT:
                    g = SCORES0_AT.index(h - 1)
                    act.wait_ge(negmax0_ready, GROUPS * p + g + 1)
                    exp_heads(g, A, lambda j: pre_bank[g % 2][:, P * j:P * (j + 1)], negmax0, rowsum0).then_inc(exp0_done, 1)
                if h in A_T_AT:
                    g = A_T_AT.index(h)
                    act.wait_ge(A_T_ready, GROUPS * p + g + 1)
                    activation(group(A_T, g), by(pre_bank[g % 2][:, :], P), ACT.Copy).then_inc(A_T_copied, 1)
                if h == 38:
                    act.wait_ge(AvT_ready, p + 1)
                    wait_prior(act, Av_kept, p)
                    activation(AvT_next[:], by(pre_bank[0][:, :], P), ACT.Copy).then_inc(AvT_copied, 1)

            def copy_xnT(p, layer):
                act.wait_ge(xnT_ready[layer], p + 1)
                activation(xnT[layer][:], bank[layer][:, 0:P], ACT.Copy).then_inc(xnT_copied[layer], 1)

            def gate_exp(p, layer):
                act.wait_ge(logits_copied[layer], p + 1)
                e = (E0N, E1N)[layer]
                activation(gate_e[layer][:, 0:e], logits[layer][:, 0:e], ACT.Exp, scale=-1.0).then_inc(gate_exp_done[layer], 1)

            def copy_hiddenT(p, layer, i):
                act.wait_ge(hiddenT_ready[layer], 3 * p + i + 1)
                m = min(4, CHUNKS - 4 * i)
                activation(hiddenT[layer][:, 4 * i:4 * i + m, :], by(bank[layer][:, 0:P * m], P),
                           ACT.Copy).then_inc(hiddenT_copied[layer], 1)

            def finish(p, h):
                if h in ROUND_AT[:3]:
                    r = ROUND_AT.index(h)
                    act.wait_ge(uT_ready, 4 * p + r + 1)
                    activation(uT[:], by(bank[0][:, :], P), ACT.Copy).then_inc(uT_copied, 1)
                if h == 23:
                    copy_xnT(p, 0)
                if h == 26:
                    gate_exp(p, 0)
                if h in UP0_AT:
                    i = UP0_AT.index(h)
                    n = BANK if i < 2 else P
                    if i < 2:
                        act.wait_ge(gate_up_ready, 2 * p + i + 1)
                    else:
                        act.wait_ge(shared_up_ready, p + 1)
                    if i > 0:
                        act.wait_ge(swish_ready, 3 * p + i)
                    activation(act_t[0][:, 0:n], bank[0][:, 0:n], ACT.Tanh, scale=0.5).then_inc(tanh_done, 1)
                if h in HIDDEN0_AT:
                    copy_hiddenT(p, 0, HIDDEN0_AT.index(h))

            def second(p, h):
                if h == 4:
                    act.wait_ge(post_T_ready, p + 1)
                    activation(xcT_post[:], bank[1][:, 0:2 * P], ACT.Copy).then_inc(post_T_copied, 1)
                if h == 7:
                    act.wait_ge(q1_copied, p + 1)
                    activation(k1T[:], bank[1][:, P:2 * P], ACT.Identity, bias=field("bk1")).then_inc(k1_copied, 1)
                if h - 1 in SCORES1_AT:
                    g = SCORES1_AT.index(h - 1)
                    act.wait_ge(negmax1_ready, GROUPS * p + g + 1)
                    exp_heads(g, P1, lambda j: S1[:, GROUP * g + j, :], negmax1, rowsum1).then_inc(exp1_done, 1)
                if h in P1_T_AT:
                    g = P1_T_AT.index(h)
                    act.wait_ge(P1_T_ready, GROUPS * p + g + 1)
                    activation(group(P1_T, g), by(bank[1][:, :], P), ACT.Copy).then_inc(P1_T_copied, 1)
                if h == 36:
                    act.wait_ge(X1T_ready, p + 1)
                    activation(X1T[:], by(bank[1][:, :], P), ACT.Copy).then_inc(X1T_copied, 1)
                if h == 43:
                    copy_xnT(p, 1)
                if h == 46:
                    gate_exp(p, 1)
                if h in UP1_AT:
                    i = UP1_AT.index(h)
                    n = BANK if i < 2 else P
                    act.wait_ge(up1_ready, 3 * p + i + 1)
                    if i > 0:
                        act.wait_ge(hidden1_ready, 3 * p + i)
                    activation(act_t[1][:, 0:n], bank[1][:, 0:n], ACT.Relu).then_inc(relu_done, 1)
                if h in HIDDEN1_AT:
                    copy_hiddenT(p, 1, HIDDEN1_AT.index(h))

            pipeline(act, core, before, finish, second)

        @block.vector
        def _(dve):
            v = nc.vector
            dve.wait_ge(first_loaded, 16)
            dve.wait_ge(pool_consts, 1)

            def hold():
                v.tensor_copy(held[:], const_eps[:])

            def core(c, h):
                step, phase, g = core_place(h)
                if h % 2 == 0 or phase == 1:
                    return
                src = E_first if step == 0 else E_work
                n = STEPS * GROUPS * c + GROUPS * step + g + 1
                if step == 0:
                    dve.wait_ge(E_first_ready, GROUPS * c + g + 1)
                dve.wait_ge(square_copied, n)
                v.scalar_tensor_tensor(out=group(F, g), in0=group(src, g), scalar=3.0, in1=by(core_bank[g][:, :], P),
                                       op0=ALU.mult, op1=ALU.add).then_inc(F_ready, 1)

            def norm_stats(x, st, m, stats_sem, var_sem, n):
                v.bn_stats(st[:], x[:]).then_inc(stats_sem, 1)
                dve.wait_ge(stats_sem, n)
                hold()
                v.bn_aggr(m[:], st[:]).then_inc(var_sem, 1)

            def norm_apply(x, m, rs, out, rstd_sem, xn_sem, n):
                dve.wait_ge(rstd_sem, n)
                v.tensor_scalar(out[:], x[:], m[:, 0:1], rs[:, 1:2], ALU.subtract, ALU.mult).then_inc(xn_sem, 1)

            def before(p, h):
                if h == 0:
                    dve.wait_ge(x_pre_loaded, 16 * p + 16)
                    norm_stats(x_pre, stats_pre, mv_pre, pre_stats_done, pre_var_ready, p + 1)
                if h == 3:
                    norm_apply(x_pre, mv_pre, rstd_pre, xn_pre, pre_rstd_ready, pre_xn_ready, p + 1)
                if h == 8:
                    dve.wait_ge(qkv0_ready, p + 1)
                    v.tensor_tensor(flat(v0), pre_bank[1][:, 2 * P:3 * P], field("bv0"), ALU.add).then_inc(v0_copied, 1)
                if h in SCORES0_AT:
                    g = SCORES0_AT.index(h)
                    dve.wait_ge(scores0_ready, GROUPS * p + g + 1)
                    v.tensor_reduce(of_group(negmax0, g), by(pre_bank[g % 2][:, :], P), AX.X, ALU.max,
                                    negate=True).then_inc(negmax0_ready, 1)
                if h - 4 in SCORES0_AT:
                    g = SCORES0_AT.index(h - 4)
                    dve.wait_ge(exp0_done, GROUPS * p + g + 1)
                    v.reciprocal(of_group(rinv0, g), of_group(rowsum0, g)).then_inc(rinv0_ready, 1)
                if h - 1 in A_T_AT:
                    g = A_T_AT.index(h - 1)
                    dve.wait_ge(A_T_copied, GROUPS * p + g + 1)
                    v.tensor_reduce(of_group(colsum, g), group(A_T, g), AX.X, ALU.add).then_inc(colsum_ready, 1)
                if h == 40:
                    dve.wait_ge(colsumT_ready, p + 1)
                    v.tensor_reduce(colmax[0:HEADS, 0:1], pre_bank[1][0:HEADS, 0:P], AX.X, ALU.max,
                                    negate=True).then_inc(colmax_steps, 1)
                    dve.wait_ge(colmax_steps, 3 * p + 1)
                    v.reciprocal(colmax[0:HEADS, 1:2], colmax[0:HEADS, 0:1]).then_inc(colmax_steps, 1)
                    dve.wait_ge(colmax_steps, 3 * p + 2)
                    v.tensor_scalar(scale_diag[0:HEADS, :], ident[0:HEADS, 0:HEADS], colmax[0:HEADS, 1:2], None,
                                    ALU.mult).then_inc(colmax_steps, 1)
                if h == 42:
                    dve.wait_ge(Av_ready, p + 1)
                    for g in range(GROUPS):
                        last = v.tensor_copy(group(Av_next, g), unstaggered(pre_bank[0], g))
                    last.then_inc(Av_copied, 1)
                if h == 44:
                    dve.wait_ge(scale_ready, p + 1)
                    v.tensor_copy(neg_scale[:], pre_bank[1][:, P:P + HEADS]).then_inc(scale_copied, 1)
                if h in GRAM_AT:
                    g = GRAM_AT.index(h)
                    dve.wait_ge(gram_ready, GROUPS * p + g + 1)
                    dve.wait_ge(scale_copied, p + 1)
                    for j in range(GROUP):
                        hd = GROUP * g + j
                        last = v.scalar_tensor_tensor(out=E_first[:, hd, :], in0=pre_bank[g % 2][:, P * j:P * (j + 1)],
                                                      scalar=neg_scale[:, hd:hd + 1], in1=ident, op0=ALU.mult, op1=ALU.add)
                    last.then_inc(E_first_ready, 1)

            def count_better(layer, step, values, n, low):
                done = gate_steps[layer]
                gt, eq = greater[layer][:, 0:n * n], equal[layer][:, 0:n * n]
                v.tensor_tensor(by(gt, n), repeated(values, n), across(values, n), ALU.is_gt).then_inc(done, 1)
                v.tensor_tensor(by(eq, n), repeated(values, n), across(values, n), ALU.is_equal).then_inc(done, 1)
                step(2)
                v.tensor_tensor(eq, eq, low, ALU.mult).then_inc(done, 1)
                step(3)
                v.tensor_tensor(gt, gt, eq, ALU.add).then_inc(done, 1)
                step(4)
                v.tensor_reduce(rank[layer][:, 0:n], by(gt, n), AX.X, ALU.add).then_inc(done, 1)
                step(5)

            def weigh_chosen(p, layer, step, n, k):
                done = gate_steps[layer]
                v.scalar_tensor_tensor(out=chosen[layer][:, 0:n], in0=rank[layer][:, 0:n], scalar=float(k),
                                       in1=score[layer][:, 0:n], op0=ALU.is_lt, op1=ALU.mult).then_inc(done, 1)
                step(1)
                v.tensor_reduce(total[layer][:, 0:1], chosen[layer][:, 0:n], AX.X, ALU.add).then_inc(done, 1)
                step(2)
                v.tensor_scalar(total[layer][:, 1:2], total[layer][:, 0:1], SUM_EPS, None, ALU.add).then_inc(done, 1)
                step(3)
                v.reciprocal(total[layer][:, 2:3], total[layer][:, 1:2]).then_inc(done, 1)
                step(4)
                v.tensor_scalar(combine[layer][:, 0:n], chosen[layer][:, 0:n], total[layer][:, 2:3], None,
                                ALU.mult).then_inc(combine_ready[layer], 1)

            def gate0_front(p):
                done = gate_steps[0]

                def step(k):
                    dve.wait_ge(done, GATE_STEPS[0] * p + k)
                dve.wait_ge(gate_exp_done[0], p + 1)
                v.tensor_scalar(gate_d[0][:], gate_e[0][:], 1.0, None, ALU.add).then_inc(done, 1)
                step(1)
                v.reciprocal(score[0][:], gate_d[0][:]).then_inc(done, 1)
                step(2)
                s3 = by(score[0][:], E0N // G0N)
                v.tensor_tensor(pairs[:, :, 0:3], s3[:, :, 0:3], s3[:, :, 1:4], ALU.add)
                v.tensor_tensor(pairs[:, :, 3:5], s3[:, :, 0:2], s3[:, :, 2:4], ALU.add)
                v.tensor_tensor(pairs[:, :, 5:6], s3[:, :, 0:1], s3[:, :, 3:4], ALU.add).then_inc(done, 1)
                step(3)
                v.tensor_reduce(gscore[:], pairs[:, :, :], AX.X, ALU.max).then_inc(done, 1)
                step(4)
                count_better(0, lambda k: step(4 + k), gscore[:], G0N, field("low4"))
                v.tensor_scalar(penalty[:], rank[0][:, 0:G0N], 2.0, -4.0, ALU.is_ge, ALU.mult).then_inc(done, 1)
                step(10)
                v.tensor_tensor(by(choice[0][:], E0N // G0N), s3, across(penalty[:], E0N // G0N), ALU.add).then_inc(done, 1)

            def gate0_back(p):
                def step(k):
                    dve.wait_ge(gate_steps[0], GATE_STEPS[0] * p + 11 + k)
                step(0)
                count_better(0, step, choice[0][:], E0N, field("low16"))
                weigh_chosen(p, 0, lambda k: step(5 + k), E0N, 4)

            def gate1(p):
                def step(k):
                    dve.wait_ge(gate_steps[1], GATE_STEPS[1] * p + k)
                dve.wait_ge(logits_copied[1], p + 1)
                v.tensor_tensor(choice[1][:, 0:E1N], logits[1][:, 0:E1N], field("lb"), ALU.add)
                dve.wait_ge(gate_exp_done[1], p + 1)
                v.tensor_scalar(gate_d[1][:, 0:E1N], gate_e[1][:, 0:E1N], 1.0, None, ALU.add).then_inc(gate_steps[1], 1)
                step(1)
                v.reciprocal(score[1][:, 0:E1N], gate_d[1][:, 0:E1N])
                count_better(1, lambda k: step(1 + k), choice[1][:, 0:E1N], E1N, field("low8"))
                weigh_chosen(p, 1, lambda k: step(6 + k), E1N, 2)

            def copy_logits(p, layer):
                dve.wait_ge(logits_ready[layer], p + 1)
                e = (E0N, E1N)[layer]
                v.tensor_copy(logits[layer][:, 0:e], bank[layer][:, 0:e]).then_inc(logits_copied[layer], 1)

            def swish(p, i):
                n = BANK if i < 2 else P
                if i > 0:
                    dve.wait_ge(hidden0_ready, 3 * p + i)
                else:
                    wait_prior(dve, hidden0_ready, 3 * p)
                dve.wait_ge(tanh_done, 3 * p + i + 1)
                v.scalar_tensor_tensor(out=act_g[0][:, 0:n], in0=act_t[0][:, 0:n], scalar=1.0, in1=bank[0][:, 0:n],
                                       op0=ALU.add, op1=ALU.mult).then_inc(swish_ready, 1)

            def times_linear(p, i):
                n = BANK if i < 2 else P
                lin = bank[0][:, 0:n] if i < 2 else bank[0][:, P:2 * P]
                if i < 2:
                    dve.wait_ge(up_ready, 2 * p + i + 1)
                dve.wait_ge(swish_ready, 3 * p + i + 1)
                if i == 0:
                    wait_prior(dve, down_ready[0], p)
                v.scalar_tensor_tensor(out=hidden[0][:, BANK * i:BANK * i + n], in0=act_g[0][:, 0:n], scalar=0.5, in1=lin,
                                       op0=ALU.mult, op1=ALU.mult).then_inc(hidden0_ready, 1)

            def finish(p, h):
                if h in TURN_AT:
                    r = TURN_AT.index(h)
                    dve.wait_ge(u_ready, 3 * p + r + 1)
                    for g in range(GROUPS):
                        last = v.tensor_copy(group(U, g), unstaggered(bank[0], g))
                    last.then_inc(u_copied, 1)
                if h == ROUND_AT[3]:
                    dve.wait_ge(uT_ready, 4 * p + 4)
                    v.scalar_tensor_tensor(out=u34T[:], in0=uT[:], scalar=3.0, in1=by(bank[0][:, :], P), op0=ALU.mult,
                                           op1=ALU.add).then_inc(u34_ready, 1)
                    dve.wait_ge(u34_ready, p + 1)
                    v.scalar_tensor_tensor(out=X0T[:], in0=u34T[:], scalar=-0.25, in1=AvT[:], op0=ALU.mult,
                                           op1=ALU.add).then_inc(X0T_ready, 1)
                if h == 19:
                    dve.wait_ge(x_bo_ready, p + 1)
                    dve.wait_ge(proj0_ready, p + 1)
                    v.tensor_tensor(x1[:], bank[0][:, 0:P], x_bo[:], ALU.add).then_inc(x1_ready, 1)
                    dve.wait_ge(x1_ready, p + 1)
                    norm_stats(x1, stats[0], mv[0], stats_done[0], var_ready[0], p + 1)
                if h == 21:
                    norm_apply(x1, mv[0], rstd[0], xn[0], rstd_ready[0], xn_ready[0], p + 1)
                if h == 25:
                    copy_logits(p, 0)
                if h - 1 in UP0_AT:
                    swish(p, UP0_AT.index(h - 1))
                if h - 3 in UP0_AT[:2]:
                    times_linear(p, UP0_AT.index(h - 3))
                if h - 1 == UP0_AT[2]:
                    times_linear(p, 2)
                if h == 29:
                    gate0_front(p)
                if h == 32:
                    gate0_back(p)
                if h == 51:
                    dve.wait_ge(down_ready[0], p + 1)
                    wait_prior(dve, x2_bo_ready, p)
                    v.tensor_tensor(x2[:], bank[0][:, 0:P], x1[:], ALU.add).then_inc(x2_ready, 1)

            def second(p, h):
                if h == 0:
                    dve.wait_ge(x2_ready, p + 1)
                    norm_stats(x2, stats_q, mv_q, q_stats_done, q_var_ready, p + 1)
                if h == 2:
                    norm_apply(x2, mv_q, rstd_q, xn_q, q_rstd_ready, q_xn_ready, p + 1)
                if h == 7:
                    dve.wait_ge(qkv1_ready, p + 1)
                    v.tensor_tensor(flat(v1), bank[1][:, 2 * P:3 * P], field("bv1"), ALU.add)
                    v.tensor_scalar(q1T[:], bank[1][:, 0:P], field("bq1"), SCORE_SCALE, ALU.add,
                                    ALU.mult).then_inc(q1_copied, 1)
                if h in SCORES1_AT:
                    g = SCORES1_AT.index(h)
                    dve.wait_ge(scores1_ready, GROUPS * p + g + 1)
                    if g == 0:
                        dve.wait_ge(scores_filled, p + 1)
                        dve.wait_ge(mask_loaded, 16 * p + 16)
                    hold()
                    v.copy_predicated(group(S1, g), repeated(mask_post[:], GROUP), by(bank[1][:, :], P)).then_inc(scores1_copied, 1)
                    dve.wait_ge(scores1_copied, GROUPS * p + g + 1)
                    v.tensor_reduce(of_group(negmax1, g), group(S1, g), AX.X, ALU.max, negate=True).then_inc(negmax1_ready, 1)
                if h - 3 in SCORES1_AT:
                    g = SCORES1_AT.index(h - 3)
                    dve.wait_ge(exp1_done, GROUPS * p + g + 1)
                    v.reciprocal(of_group(rinv1, g), of_group(rowsum1, g)).then_inc(rinv1_ready, 1)
                if h == 39:
                    dve.wait_ge(x2_bo_ready, p + 1)
                    dve.wait_ge(proj1_ready, p + 1)
                    v.tensor_tensor(x3[:], bank[1][:, 0:P], x2_bo[:], ALU.add).then_inc(x3_ready, 1)
                    dve.wait_ge(x3_ready, p + 1)
                    norm_stats(x3, stats[1], mv[1], stats_done[1], var_ready[1], p + 1)
                if h == 41:
                    norm_apply(x3, mv[1], rstd[1], xn[1], rstd_ready[1], xn_ready[1], p + 1)
                if h == 46:
                    copy_logits(p, 1)
                if h == 48:
                    gate1(p)
                if h - 1 in UP1_AT[:2]:
                    i = UP1_AT.index(h - 1)
                    dve.wait_ge(relu_done, 3 * p + i + 1)
                    dve.wait_ge(combine_ready[1], p + 1)
                    if i == 1:
                        dve.wait_ge(hidden1_ready, 3 * p + 1)
                    v.tensor_tensor(by(act_g[1][:], P), by(act_t[1][:], P), across(combine[1][:, 4 * i:4 * i + 4], P),
                                    ALU.mult).then_inc(relu_weighted, 1)
                if h == 69:
                    dve.wait_ge(down_ready[1], p + 1)
                    wait_prior(dve, out_stored, 16 * p)
                    v.tensor_tensor(x4[:], bank[1][:, 0:P], x3[:], ALU.add).then_inc(x4_ready, 1)

            pipeline(dve, core, before, finish, second)

        @block.gpsimd
        def _(pool):
            g_ = nc.gpsimd
            g_.memset(const_eps[:], LN_EPS)
            g_.memset(const_mhalf[:], -0.5).then_inc(pool_consts, 1)
            pool.wait_ge(pool_consts, 1)
            pool.wait_ge(first_loaded, 16)

            def inverse_root(m, rs, var_sem, veps_sem, rstd_sem, n):
                pool.wait_ge(var_sem, n)
                g_.tensor_tensor(rs[:, 0:1], m[:, 1:2], const_eps[:], ALU.add).then_inc(veps_sem, 1)
                pool.wait_ge(veps_sem, n)
                g_.tensor_tensor(rs[:, 1:2], rs[:, 0:1], const_mhalf[:], ALU.pow).then_inc(rstd_sem, 1)

            def mask_keys(g, out, k_t):
                return g_.tensor_tensor(group(out, g), repeated(k_t[:], GROUP), across(of_group(field("rowmask"), g), P), ALU.mult)

            def core(c, h):
                pass

            def before(p, h):
                if h == 1:
                    inverse_root(mv_pre, rstd_pre, pre_var_ready, pre_veps_ready, pre_rstd_ready, p + 1)
                if 8 <= h < 8 + GROUPS:
                    pool.wait_ge(q0k0_copied, p + 1)
                    mask_keys(h - 8, k0m, k0T).then_inc(k0_masked, 1)
                if h - 4 in SCORES0_AT:
                    g = SCORES0_AT.index(h - 4)
                    pool.wait_ge(rinv0_ready, GROUPS * p + g + 1)
                    g_.tensor_tensor(group(A, g), group(A, g), across(of_group(rinv0, g), P), ALU.mult).then_inc(A_ready, 1)

            def finish(p, h):
                if h == 4:
                    pool.wait_ge(rest_loaded, 16)
                    pool.wait_ge(x_post_loaded, 16 * p + 16)
                    g_.tensor_tensor(x_bo[:], x_post[:], field("bo0"), ALU.add).then_inc(x_bo_ready, 1)
                if h == 20:
                    inverse_root(mv[0], rstd[0], var_ready[0], veps_ready[0], rstd_ready[0], p + 1)
                if h in (37, 38):
                    i = h - 37
                    pool.wait_ge(combine_ready[0], p + 1)
                    pool.wait_ge(hidden0_ready, 3 * p + i + 1)
                    part = by(hidden[0][:, BANK * i:BANK * (i + 1)], UP // E0N)
                    n = E0N // 2
                    g_.tensor_tensor(part, part, across(combine[0][:, n * i:n * (i + 1)], UP // E0N),
                                     ALU.mult).then_inc(hidden0_scaled, 1)

            def second(p, h):
                if h == 1:
                    inverse_root(mv_q, rstd_q, q_var_ready, q_veps_ready, q_rstd_ready, p + 1)
                    pool.wait_ge(rest_loaded, 16)
                    wait_prior(pool, x3_ready, p)
                    g_.tensor_tensor(x2_bo[:], x2[:], field("bo1"), ALU.add).then_inc(x2_bo_ready, 1)
                if h == 5:
                    wait_prior(pool, exp1_done, GROUPS * p)
                    g_.tensor_tensor(held_pool[:], const_eps[:], const_eps[:], ALU.add)
                    g_.memset(S1[:], MASKED).then_inc(scores_filled, 1)
                if 8 <= h < 8 + GROUPS:
                    pool.wait_ge(k1_copied, p + 1)
                    mask_keys(h - 8, k1m, k1T).then_inc(k1_masked, 1)
                if h - 3 in SCORES1_AT:
                    g = SCORES1_AT.index(h - 3)
                    pool.wait_ge(rinv1_ready, GROUPS * p + g + 1)
                    g_.tensor_tensor(group(P1, g), group(P1, g), across(of_group(rinv1, g), P), ALU.mult).then_inc(P1_ready, 1)
                if h == 40:
                    inverse_root(mv[1], rstd[1], var_ready[1], veps_ready[1], rstd_ready[1], p + 1)
                if h - 2 in UP1_AT:
                    i = UP1_AT.index(h - 2)
                    if i == 0:
                        wait_prior(pool, down_ready[1], p)
                    if i < 2:
                        pool.wait_ge(relu_weighted, 2 * p + i + 1)
                        g_.tensor_tensor(hidden[1][:, BANK * i:BANK * (i + 1)], act_g[1][:], act_t[1][:], ALU.mult)\
                            .then_inc(hidden1_ready, 1)
                    else:
                        pool.wait_ge(relu_done, 3 * p + 3)
                        g_.tensor_tensor(hidden[1][:, UP:UP + P], act_t[1][:, 0:P], act_t[1][:, 0:P], ALU.mult)\
                            .then_inc(hidden1_ready, 1)

            pipeline(pool, core, before, finish, second)


def pack_weights(np, a):
    def row(v):
        return np.broadcast_to(np.asarray(v)[None, :], (P, len(v)))

    def col(v):
        return np.asarray(v)[:, None]

    def low(n):
        return row(np.tril(np.ones((n, n), np.float32), -1).ravel())

    def chunks(w, shared):
        w = np.concatenate([w, shared], 0)
        return w.reshape(CHUNKS, P, P).transpose(1, 0, 2).reshape(P, CHUNKS * P)

    rows = np.arange(P)
    rowmask = (rows[:, None] // DH == np.arange(HEADS)[None, :]).astype(np.float32)

    def staggered(w):
        out = np.zeros((GROUP, 32, GROUPS, P), w.dtype)
        w = w.reshape(GROUPS, GROUP, DH, P)
        for j in range(GROUP):
            out[j, DH * j:DH * (j + 1)] = w[:, j].transpose(1, 0, 2)
        return out.reshape(P, GROUPS * P)
    f = {
        "wq0": a["L0_xattn_Wq"], "wk0": a["L0_xattn_Wk"], "wv0": a["L0_xattn_Wv"], "wo0": staggered(a["L0_xattn_Wo"]),
        "bq0": col(a["L0_xattn_bq"]), "bk0": col(a["L0_xattn_bk"]), "bv0": row(a["L0_xattn_bv"]),
        "bo0": row(a["L0_xattn_bo"]),
        "wq1": a["L1_xattn_Wq"].T, "wk1": a["L1_xattn_Wk"].T, "wv1": a["L1_xattn_Wv"].T, "wo1": staggered(a["L1_xattn_Wo"].T),
        "bq1": col(a["L1_xattn_bq"]), "bk1": col(a["L1_xattn_bk"]), "bv1": row(a["L1_xattn_bv"]),
        "bo1": row(a["L1_xattn_bo"]),
        "ident": np.eye(P, dtype=np.float32), "rowmask": rowmask, "ones": np.ones((P, P), np.float32),
        "gate0": a["L0_ffn_w_gate"].T, "gate1": a["L1_ffn_gate_w"].T, "lb": row(a["L1_ffn_lb_bias"]),
        "low4": low(G0N), "low16": low(E0N), "low8": low(E1N),
        "w1": a["L0_ffn_w1_e"].reshape(UP, P).T, "w3": a["L0_ffn_w3_e"].reshape(UP, P).T,
        "w1s": a["L0_ffn_w1_s"].T, "w3s": a["L0_ffn_w3_s"].T,
        "w2": chunks(a["L0_ffn_w2_e"].transpose(0, 2, 1).reshape(UP, P), a["L0_ffn_w2_s"].T),
        "up1": a["L1_ffn_w1"].reshape(UP, P).T, "up1s": a["L1_ffn_cfc"].T,
        "down1": chunks(a["L1_ffn_w2"].transpose(0, 2, 1).reshape(UP, P), a["L1_ffn_cproj"].T),
    }
    return np.ascontiguousarray(np.concatenate([f[name] for name, _ in FIELDS], axis=1))


def kernel(**inputs):
    import numpy as np
    import concourse.bacc as bacc
    from concourse.bass_utils import run_bass_kernel_spmd

    a = {k: np.asarray(val) for k, val in inputs.items()}
    arrays = {
        "x_dram": np.ascontiguousarray(a["x"]),
        "ctx_dram": np.ascontiguousarray(a["ctx_1024"]),
        "mask_dram": np.ascontiguousarray(a["mask_BxSxS2_bf1"]),
        "weights_dram": pack_weights(np, a),
    }
    nc = bacc.Bacc("TRN2", target_bir_lowering=False, num_devices=1)
    aps = [nc.dram_tensor(n, arr.shape, mybir.dt.from_np(arr.dtype), kind="ExternalInput").ap() for n, arr in arrays.items()]
    out = nc.dram_tensor("out_dram", a["x"].shape, F32, kind="ExternalOutput").ap()
    build(nc, *aps, out)
    r = run_bass_kernel_spmd(nc, [arrays], core_ids=[0])
    return r.results[0]["out_dram"]
```

```python
from contextlib import ExitStack

import concourse.bass as bass
from concourse import mybir

ALU = mybir.AluOpType
ACT = mybir.ActivationFunctionType
AX = mybir.AxisListType
F32 = mybir.dt.float32
U8 = mybir.dt.uint8

P = 128
HEADS = 16
DH = P // HEADS
GROUP = 4
GROUPS = HEADS // GROUP
STEPS = 5
SLOTS = STEPS * 2 * GROUPS
SPREAD = GROUPS * (P + DH)
HALVES = 2 * SLOTS
BANK = 512
LN_EPS = 1e-5
SUM_EPS = 1e-6
MASKED = -1e9
SCORE_SCALE = float(DH) ** -0.5

E0N, E1N = 16, 8
G0N = 4
UP = E0N * 64
CHUNKS = UP // P + 1

FIELDS = [("wq0", P), ("wk0", P), ("wv0", P), ("bq0", 1), ("bk0", 1), ("bv0", P), ("ident", P), ("rowmask", HEADS),
          ("ones", P),
          ("wo0", P), ("bo0", P), ("wk1", P), ("wv1", P), ("bk1", 1), ("bv1", P), ("wq1", P), ("bq1", 1),
          ("gate0", E0N), ("low4", G0N * G0N), ("low16", E0N * E0N), ("low8", E1N * E1N),
          ("w1", UP), ("w3", UP), ("w1s", P), ("w3s", P), ("w2", CHUNKS * P),
          ("wo1", P), ("bo1", P), ("gate1", E1N), ("lb", E1N), ("up1", UP), ("up1s", P), ("down1", CHUNKS * P)]
AT = {}
_at = 0
for _name, _n in FIELDS:
    AT[_name] = (_at, _at + _n)
    _at += _n
PACKED = _at
FIRST = AT["ones"][1]


def build(nc, x_d, ctx_d, mask_d, w_d, out_d):
    B = x_d.shape[0]
    with ExitStack() as ctx:
        def sb(name, *shape, dt=F32):
            return ctx.enter_context(nc.sbuf_tensor(name, [P, *shape], dt))

        def sem(name):
            return ctx.enter_context(nc.semaphore(name))

        def both(name, *shape):
            return [sb(f"{name}_{layer}", *shape) for layer in (0, 1)]

        core_bank = [ctx.enter_context(nc.psum_tensor(f"core_bank{g}", [P, BANK], F32)) for g in range(GROUPS)]
        pre_bank = [ctx.enter_context(nc.psum_tensor(f"pre_bank{i}", [P, BANK], F32)) for i in range(2)]
        bank = [ctx.enter_context(nc.psum_tensor(f"layer_bank{i}", [P, BANK], F32)) for i in range(2)]

        W = sb("packed", PACKED)

        def field(name):
            return W[:, AT[name][0]:AT[name][1]]

        E_first = sb("E_first", HEADS, P)
        E_work = sb("E_work", HEADS, P)
        E_last = sb("E_last", HEADS, P)
        EE = sb("EE", HEADS, P)
        F = sb("F", HEADS, P)
        x_pre, ctx_pre = sb("x_pre", P), sb("ctx_pre", P)
        stats_pre, mv_pre, rstd_pre = sb("stats_pre", 6), sb("mv_pre", 2), sb("rstd_pre", 2)
        xn_pre = sb("xn_pre", P)
        xcT_pre = sb("xcT_pre", 2 * P)
        q0T, k0T = sb("q0T", P), sb("k0T", P)
        k0m = sb("k0m", HEADS, P)
        v0 = sb("v0", SPREAD)
        negmax0, rowsum0, rinv0 = sb("negmax0", HEADS), sb("rowsum0", HEADS), sb("rinv0", HEADS)
        A, A_T = sb("A", HEADS, P), sb("A_T", HEADS, P)
        colsum, colmax = sb("colsum", HEADS), sb("colmax", 2)
        scale_diag, neg_scale = sb("scale_diag", HEADS), sb("neg_scale", HEADS)
        Av_next, Av = sb("Av_next", P), sb("Av", SPREAD)
        AvT_next, AvT = sb("AvT_next", P), sb("AvT", P)
        uT, U = sb("uT", P), sb("U", SPREAD)
        u34T, X0T = sb("u34T", P), sb("X0T", P)
        x_post, x_bo, x1 = sb("x_post", P), sb("x_bo", P), sb("x1", P)
        pairs, gscore, penalty = sb("pairs", G0N, 6), sb("gscore", G0N), sb("penalty", G0N)
        ctx_post = sb("ctx_post", P)
        mask_post = sb("mask_post", P, dt=U8)
        x2, x2_bo, x3, x4 = sb("x2", P), sb("x2_bo", P), sb("x3", P), sb("x4", P)
        xcT_post = sb("xcT_post", 2 * P)
        q1T, k1T = sb("q1T", P), sb("k1T", P)
        k1m = sb("k1m", HEADS, P)
        v1 = sb("v1", SPREAD)
        S1 = sb("S1", HEADS, P)
        P1, P1_T = sb("P1", HEADS, P), sb("P1_T", HEADS, P)
        negmax1, rowsum1, rinv1 = sb("negmax1", HEADS), sb("rowsum1", HEADS), sb("rinv1", HEADS)
        X1T = sb("X1T", P)
        stats_q, mv_q, rstd_q, xn_q = sb("stats_q", 6), sb("mv_q", 2), sb("rstd_q", 2), sb("xn_q", P)
        stats, mv, rstd, xn, xnT = both("stats", 6), both("mv", 2), both("rstd", 2), both("xn", P), both("xnT", P)
        logits, gate_e, gate_d, score = both("logits", E0N), both("gate_e", E0N), both("gate_d", E0N), both("score", E0N)
        greater, equal, rank = both("greater", E0N * E0N), both("equal", E0N * E0N), both("rank", E0N)
        choice, chosen, total, combine = both("choice", E0N), both("chosen", E0N), both("total", 3), both("combine", E0N)
        act_t, act_g = sb("act_t", BANK), sb("act_g", BANK)
        hidden = sb("hidden", CHUNKS * P)
        hiddenT = both("hiddenT", CHUNKS, P)
        weighted = sb("weighted", E1N, P)
        relu1 = sb("relu1", CHUNKS, P)
        moe, x3_moe = sb("moe", P), sb("x3_moe", P)
        held, held_pool = sb("held", 8), sb("held_pool", 1)
        const_eps, const_mhalf = sb("const_eps", 1), sb("const_mhalf", 1)
        ident = field("ident")

        first_loaded, rest_loaded = sem("first_loaded"), sem("rest_loaded")
        pool_consts = sem("pool_consts")
        x_pre_loaded, ctx_pre_loaded = sem("x_pre_loaded"), sem("ctx_pre_loaded")
        pre_stats_done, pre_var_ready, pre_veps_ready = sem("pre_stats_done"), sem("pre_var_ready"), sem("pre_veps_ready")
        pre_rstd_ready, pre_xn_ready = sem("pre_rstd_ready"), sem("pre_xn_ready")
        pre_T_ready, pre_T_copied = sem("pre_T_ready"), sem("pre_T_copied")
        qkv0_ready, q0k0_copied, v0_copied = sem("qkv0_ready"), sem("q0k0_copied"), sem("v0_copied")
        k0_masked = sem("k0_masked")
        scores0_ready, negmax0_ready, exp0_done = sem("scores0_ready"), sem("negmax0_ready"), sem("exp0_done")
        rinv0_ready, A_ready = sem("rinv0_ready"), sem("A_ready")
        A_T_ready, A_T_copied, colsum_ready = sem("A_T_ready"), sem("A_T_copied"), sem("colsum_ready")
        AvT_ready, AvT_copied = sem("AvT_ready"), sem("AvT_copied")
        Av_ready, Av_copied, Av_kept = sem("Av_ready"), sem("Av_copied"), sem("Av_kept")
        colsumT_ready, colmax_steps = sem("colsumT_ready"), sem("colmax_steps")
        scale_ready, scale_copied = sem("scale_ready"), sem("scale_copied")
        gram_ready, E_first_ready = sem("gram_ready"), sem("E_first_ready")
        square_ready, square_copied, F_ready = sem("square_ready"), sem("square_copied"), sem("F_ready")
        product_ready, E_copied = sem("product_ready"), sem("E_copied")
        x_post_loaded, x_bo_ready = sem("x_post_loaded"), sem("x_bo_ready")
        uT_ready, uT_copied = sem("uT_ready"), sem("uT_copied")
        u_ready, u_copied = sem("u_ready"), sem("u_copied")
        u34_ready, X0T_ready = sem("u34_ready"), sem("X0T_ready")
        proj0_ready, x1_ready, x2_ready = sem("proj0_ready"), sem("x1_ready"), sem("x2_ready")
        gate_up_ready, up_ready, shared_up_ready = sem("gate_up_ready"), sem("up_ready"), sem("shared_up_ready")
        tanh_done, swish_ready, hidden0_ready = sem("tanh_done"), sem("swish_ready"), sem("hidden0_ready")
        hiddenT_ready, hiddenT_copied, down0_ready = sem("hiddenT_ready"), sem("hiddenT_copied"), sem("down0_ready")
        hidden0_scaled = sem("hidden0_scaled")
        ctx_post_loaded, mask_loaded = sem("ctx_post_loaded"), sem("mask_loaded")
        q_stats_done, q_var_ready, q_veps_ready = sem("q_stats_done"), sem("q_var_ready"), sem("q_veps_ready")
        q_rstd_ready, q_xn_ready = sem("q_rstd_ready"), sem("q_xn_ready")
        post_T_ready, post_T_copied = sem("post_T_ready"), sem("post_T_copied")
        qkv1_ready, v1_copied, q1_copied, k1_copied = sem("qkv1_ready"), sem("v1_copied"), sem("q1_copied"), sem("k1_copied")
        k1_masked = sem("k1_masked")
        x2_bo_ready, scores_filled = sem("x2_bo_ready"), sem("scores_filled")
        scores1_ready, scores1_copied = sem("scores1_ready"), sem("scores1_copied")
        negmax1_ready, exp1_done = sem("negmax1_ready"), sem("exp1_done")
        rinv1_ready, P1_ready = sem("rinv1_ready"), sem("P1_ready")
        P1_T_ready, P1_T_copied = sem("P1_T_ready"), sem("P1_T_copied")
        X1T_ready, X1T_copied, proj1_ready, x3_ready = sem("X1T_ready"), sem("X1T_copied"), sem("proj1_ready"), sem("x3_ready")
        up1_ready, relu_done, hidden1_ready = sem("up1_ready"), sem("relu_done"), sem("hidden1_ready")
        down1_ready, down_weighted = sem("down1_ready"), sem("down_weighted")
        moe_ready, x3_moe_ready = sem("moe_ready"), sem("x3_moe_ready")
        x4_ready, out_stored = sem("x4_ready"), sem("out_stored")

        def both_sems(name):
            return [sem(f"{name}_{layer}") for layer in (0, 1)]

        stats_done, var_ready, veps_ready = both_sems("stats_done"), both_sems("var_ready"), both_sems("veps_ready")
        rstd_ready, xn_ready = both_sems("rstd_ready"), both_sems("xn_ready")
        xnT_ready, xnT_copied = both_sems("xnT_ready"), both_sems("xnT_copied")
        logits_ready, logits_copied, gate_exp_done = both_sems("logits_ready"), both_sems("logits_copied"), both_sems("gate_exp_done")
        gate_steps = both_sems("gate_steps")
        combine_ready = both_sems("combine_ready")

        GATE_STEPS = [20, 10]

        def group(t, g):
            return t[:, GROUP * g:GROUP * (g + 1), :]

        def of_group(t, g):
            return t[:, GROUP * g:GROUP * (g + 1)]

        def by(ap, n):
            return ap.rearrange("p (h c) -> p h c", c=n)

        def spread(t):
            return by(t[:], P + DH)[:, :, 0:P].rearrange("p g (j c) -> p g j c", c=32)[:, :, :, 0:DH]

        def natural(ap):
            return ap.rearrange("p (g j c) -> p g j c", g=GROUPS, c=DH)

        def mixed(ap):
            return ap.rearrange("p (j g c) -> p g j c", g=GROUPS, c=DH)

        def across(ap, n):
            return ap.unsqueeze(2).broadcast_to([ap.shape[0], ap.shape[1], n])

        def repeated(ap, n):
            return ap.unsqueeze(1).broadcast_to([ap.shape[0], n, ap.shape[1]])

        def core_place(h):
            slot = h // 2
            return slot // (2 * GROUPS), slot // GROUPS % 2, slot % GROUPS

        def wait_prior(engine, semaphore, count):
            if not (isinstance(count, int) and count <= 0):
                engine.wait_ge(semaphore, count)

        block = ctx.enter_context(nc.Block())

        def pipeline(engine, core, before, finish, second):
            def body(c, has_core=True, has_before=True, has_finish=True, has_second=True, wide=False):
                for h in range(HALVES):
                    if has_core:
                        core(c, h)
                    if has_second:
                        second(c - 2, h, wide)
                    if has_finish:
                        finish(c - 1, h, wide)
                    if has_before:
                        before(c + 1, h, wide)

            body(-1, has_core=False, has_finish=False, has_second=False, wide=True)
            body(0, has_finish=False, has_second=False)
            body(1, has_second=False)
            body(2)
            with engine.Fori(3, B - 1) as c:
                body(c)
            body(B - 1, has_before=False)
            body(B, has_core=False, has_before=False, wide=True)
            body(B + 1, has_core=False, has_before=False, has_finish=False, wide=True)

        def before_bank(g, wide):
            return core_bank[g] if wide else pre_bank[g % 2]

        def second_bank(i, wide):
            return core_bank[i % 4] if wide else bank[1]

        def finish_bank(i, wide):
            return pre_bank[i] if wide and i < 2 else bank[0]

        PE_AT = {
            "before.x_ctx_T": (15,), "before.qkv": (17,), "before.scores": (23, 30, 52, 56),
            "before.A_T": (37, 51, 64, 67), "before.A_v": (70,), "before.colsum_T": (70,),
            "before.Av_turned": (72,), "before.scale": (73,), "before.gram": (74, 75, 76, 77),
            "finish.u_E": (2, 8, 14, 18), "finish.u_turned": (6, 12, 17), "finish.out": (21,),
            "finish.xn_T": (33,), "finish.logits": (38,), "finish.up_gate": (41, 51),
            "finish.up_linear": (45, 60), "finish.up_shared": (63,), "finish.hidden_T": (71, 73, 75),
            "finish.down": (77,),
            "second.x_ctx_T": (5,), "second.qkv": (8,), "second.scores": (14, 18, 27, 32),
            "second.P_T": (36, 45, 46, 49), "second.P_v": (53,), "second.out": (55,), "second.xn_T": (63,),
            "second.logits": (64,), "second.up": (66, 70, 73), "second.down": (75, 77, 78),
        }
        ACT_AT = {
            "core.Av_kept": (48,),
            "before.x_ctx_T": (14,), "before.q_k": (17,), "before.exp": (24, 29, 56, 57),
            "before.A_T": (39, 50, 65, 66), "before.A_v": (67,),
            "finish.u_E": (1, 7, 12), "finish.xn_T": (31,), "finish.gate_exp": (35,),
            "finish.tanh": (41, 52, 61), "finish.hidden_T": (68, 72, 75),
            "second.x_ctx_T": (3,), "second.k": (7,), "second.exp": (18, 21, 29, 33),
            "second.P_T": (42, 45, 46, 50), "second.P_v": (53,), "second.xn_T": (61,), "second.gate_exp": (64,),
            "second.relu": (64, 68, 70),
        }
        DVE_AT = {
            "before.norm_stats": (2,), "before.norm": (3,), "before.v": (16,), "before.max": (22, 25, 53, 55),
            "before.inverse_sum": (29, 39, 55, 57), "before.colsum": (50, 51, 64, 65), "before.colmax": (68,),
            "before.Av": (68,), "before.scale": (68,), "before.E_first": (74, 77, 78, 79),
            "finish.u_turned": (2, 13, 14), "finish.X": (17,), "finish.x1": (19,), "finish.norm": (23,),
            "finish.logits": (33,), "finish.swish": (42, 54, 58), "finish.linear": (48, 57),
            "finish.linear_shared": (66,), "finish.gate_groups": (47,), "finish.gate_experts": (48,),
            "finish.x2": (78,),
            "second.norm_stats": (0,), "second.norm": (0,), "second.q_v": (4,), "second.max": (14, 17, 23, 32),
            "second.inverse_sum": (19, 28, 38, 42), "second.x3": (54,), "second.norm3": (56,),
            "second.logits": (58,), "second.gate": (59,), "second.hidden": (63, 68, 69),
            "second.weigh": (77, 78), "second.sum": (78,), "second.x4": (79,),
        }
        POOL_AT = {
            "before.root": (58,), "before.mask_k": (71, 72, 75, 76), "before.normalise": (76, 77, 78, 79),
            "finish.x_bo": (36,), "finish.root": (74,), "finish.combine": (78, 79),
            "second.root_bo": (6,), "second.fill": (68,), "second.mask_k": (70, 71, 72, 73),
            "second.normalise": (74, 76, 77, 78), "second.root3": (78,),
        }

        @block.sync
        def _(sp):
            sp.dma_start(W[:, 0:FIRST], w_d[:, 0:FIRST]).then_inc(first_loaded, 16)

            def load_before(p):
                wait_prior(sp, pre_xn_ready, p)
                sp.dma_start(x_pre[:], x_d[p]).then_inc(x_pre_loaded, 16)
                wait_prior(sp, pre_T_ready, p)
                sp.dma_start(ctx_pre[:], ctx_d[p]).then_inc(ctx_pre_loaded, 16)

            def load_ctx_second(p):
                wait_prior(sp, post_T_ready, p)
                sp.dma_start(ctx_post[:], ctx_d[p]).then_inc(ctx_post_loaded, 16)

            def load_finish(p):
                wait_prior(sp, x_bo_ready, p)
                sp.dma_start(x_post[:], x_d[p]).then_inc(x_post_loaded, 16)

            def load_mask(p):
                wait_prior(sp, scores1_copied, GROUPS * p)
                sp.dma_start(mask_post[:], mask_d[p]).then_inc(mask_loaded, 16)

            def store(p):
                sp.wait_ge(x4_ready, p + 1)
                sp.dma_start(out_d[p], x4[:]).then_inc(out_stored, 16)

            def during(c, has_before=True, has_finish=True, has_store=True):
                if has_before:
                    load_before(c + 2)
                load_ctx_second(c - 1)
                if has_finish:
                    load_finish(c)
                load_mask(c - 1)
                if has_store:
                    store(c - 2)

            load_before(0)
            sp.dma_start(W[:, FIRST:PACKED], w_d[:, FIRST:PACKED]).then_inc(rest_loaded, 16)
            load_before(1)
            load_before(2)
            load_finish(0)
            during(1, has_store=False)
            with sp.Fori(2, B - 2) as c:
                during(c)
            during(B - 2, has_before=False)
            during(B - 1, has_before=False)
            during(B, has_before=False, has_finish=False)
            store(B - 1)
            sp.wait_ge(out_stored, 16 * B)

        @block.tensor
        def _(pe):
            at = PE_AT
            mm = nc.tensor.matmul
            turn = nc.tensor.transpose
            pe.wait_ge(first_loaded, 16)

            def core(c, h):
                step, phase, g = core_place(h)
                half = h % 2
                src = E_first if step == 0 else E_work
                n = STEPS * GROUPS * c + GROUPS * step + g + 1
                if half == 0 and phase == 0 and step == 0:
                    pe.wait_ge(E_first_ready, GROUPS * c + g + 1)
                    wait_prior(pe, E_copied, STEPS * GROUPS * (c - 1) + (STEPS - 1) * GROUPS + g + 1)
                elif half == 0 and phase == 0:
                    pe.wait_ge(E_copied, n - GROUPS)
                elif half == 0:
                    pe.wait_ge(F_ready, n)
                for j in (2 * half, 2 * half + 1):
                    hd = GROUP * g + j
                    out = core_bank[g][:, P * j:P * (j + 1)]
                    if phase == 0:
                        last = mm(out, src[:, hd, :], src[:, hd, :], start=True, stop=True)
                    else:
                        last = mm(out, EE[:, hd, :], F[:, hd, :], start=True, stop=True)
                if half:
                    last.then_inc(square_ready if phase == 0 else product_ready, 1)

            def apply_transposed(out, u, m):
                for g in range(GROUPS):
                    for j in range(GROUP):
                        a = P * g + 32 * j
                        last = mm(out[32 * j:32 * j + 32, 0:P], u[:, a:a + 32], m[:, GROUP * g + j, :],
                                  start=(g == 0), stop=(g == GROUPS - 1))
                return last

            def transpose_x_ctx(p):
                pe.wait_ge(pre_xn_ready, p + 1)
                wait_prior(pe, E_first_ready, GROUPS * p)
                turn(pre_bank[0][:, 0:P], xn_pre[:], ident)
                pe.wait_ge(ctx_pre_loaded, 16 * p + 16)
                turn(pre_bank[0][:, P:2 * P], ctx_pre[:], ident).then_inc(pre_T_ready, 1)

            def project_qkv0(p):
                pe.wait_ge(pre_T_copied, p + 1)
                out = pre_bank[1]
                mm(out[:, 0:P], field("wq0"), xcT_pre[:, 0:P], start=True, stop=True)
                mm(out[:, P:2 * P], field("wk0"), xcT_pre[:, P:2 * P], start=True, stop=True)
                mm(out[:, 2 * P:3 * P], xcT_pre[:, P:2 * P], field("wv0"), start=True, stop=True).then_inc(qkv0_ready, 1)

            def scores0(p, g, wide):
                pe.wait_ge(k0_masked, GROUPS * p + g + 1)
                if g >= 2 and not wide:
                    pe.wait_ge(A_T_copied, GROUPS * p + g - 1)
                mm(before_bank(g, wide)[:, :], q0T[:], group(k0m, g), start=True, stop=True).then_inc(scores0_ready, 1)

            def transpose_A(p, g, wide):
                pe.wait_ge(A_ready, GROUPS * p + g + 1)
                for j in range(GROUP):
                    last = turn(before_bank(g, wide)[:, P * j:P * (j + 1)], A[:, GROUP * g + j, :], ident)
                last.then_inc(A_T_ready, 1)

            def apply_A(p):
                pe.wait_ge(A_T_copied, GROUPS * p + GROUPS)
                apply_transposed(pre_bank[0], v0, A_T).then_inc(AvT_ready, 1)

            def turn_Av(p):
                pe.wait_ge(AvT_copied, p + 1)
                turn(pre_bank[0][:, P:2 * P], AvT_next[:], ident).then_inc(Av_ready, 1)

            def transpose_colsum(p):
                pe.wait_ge(colsum_ready, GROUPS * p + GROUPS)
                turn(pre_bank[1][0:HEADS, 0:P], colsum[:, :], ident).then_inc(colsumT_ready, 1)

            def spread_scale(p):
                pe.wait_ge(colmax_steps, 3 * p + 3)
                mm(pre_bank[1][:, P:P + HEADS], field("ones")[0:HEADS, :], scale_diag[0:HEADS, :],
                   start=True, stop=True).then_inc(scale_ready, 1)

            def gram(p, g, wide):
                if wide:
                    pass
                elif g == 0:
                    pe.wait_ge(Av_copied, p + 1)
                elif g == 1:
                    pe.wait_ge(scale_copied, p + 1)
                else:
                    pe.wait_ge(E_first_ready, GROUPS * p + g - 1)
                for j in range(GROUP):
                    a_t = A_T[:, GROUP * g + j, :]
                    last = mm(before_bank(g, wide)[:, P * j:P * (j + 1)], a_t, a_t, start=True, stop=True)
                last.then_inc(gram_ready, 1)

            def before(p, h, wide):
                if h in at["before.x_ctx_T"]:
                    transpose_x_ctx(p)
                if h in at["before.qkv"]:
                    project_qkv0(p)
                if h in at["before.scores"]:
                    scores0(p, at["before.scores"].index(h), wide)
                if h in at["before.A_T"]:
                    transpose_A(p, at["before.A_T"].index(h), wide)
                if h in at["before.A_v"]:
                    apply_A(p)
                if h in at["before.colsum_T"]:
                    transpose_colsum(p)
                if h in at["before.Av_turned"]:
                    turn_Av(p)
                if h in at["before.scale"]:
                    spread_scale(p)
                if h in at["before.gram"]:
                    gram(p, at["before.gram"].index(h), wide)

            def apply_E(p, r):
                if r == 0:
                    pe.wait_ge(Av_kept, p + 1)
                    pe.wait_ge(E_copied, STEPS * GROUPS * (p + 1))
                    wait_prior(pe, x2_ready, p)
                else:
                    pe.wait_ge(u_copied, 3 * p + r)
                apply_transposed(bank[0], Av if r == 0 else U, E_last).then_inc(uT_ready, 1)

            def turn_u(p, r):
                pe.wait_ge(uT_copied, 3 * p + r + 1)
                turn(bank[0][:, P:2 * P], uT[:], ident).then_inc(u_ready, 1)

            def project_out(p, layer):
                if layer == 0:
                    pe.wait_ge(rest_loaded, 16)
                    pe.wait_ge(X0T_ready, p + 1)
                    mm(bank[0][:, 0:P], X0T[:], field("wo0"), start=True, stop=True).then_inc(proj0_ready, 1)
                else:
                    pe.wait_ge(X1T_copied, p + 1)
                    mm(bank[1][:, 0:P], X1T[:], field("wo1"), start=True, stop=True).then_inc(proj1_ready, 1)

            def transpose_xn(p, layer):
                pe.wait_ge(xn_ready[layer], p + 1)
                turn(bank[layer][:, 0:P], xn[layer][:], ident).then_inc(xnT_ready[layer], 1)

            def gate_logits(p, layer):
                pe.wait_ge(xnT_copied[layer], p + 1)
                w = field("gate0") if layer == 0 else field("gate1")
                mm(bank[layer][:, 0:w.shape[1]], xnT[layer][:], w, start=True, stop=True).then_inc(logits_ready[layer], 1)

            def transpose_hidden(p, i, wide):
                if i < 2:
                    pe.wait_ge(hidden0_scaled, 2 * p + i + 1)
                pe.wait_ge(hidden0_ready, 3 * p + (i + 1 if wide else 3))
                if i > 0 and not wide:
                    pe.wait_ge(hiddenT_copied, 3 * p + i)
                for k in range(4 * i, min(4 * i + 4, CHUNKS)):
                    last = turn(finish_bank(i, wide)[:, P * (k - 4 * i):P * (k - 4 * i + 1)], hidden[:, P * k:P * (k + 1)], ident)
                last.then_inc(hiddenT_ready, 1)

            def project_down(p):
                pe.wait_ge(hiddenT_copied, 3 * p + 3)
                a = AT["w2"][0]
                for k in range(CHUNKS):
                    last = mm(bank[0][:, 0:P], hiddenT[0][:, k, :], W[:, a + P * k:a + P * (k + 1)],
                              start=(k == 0), stop=(k == CHUNKS - 1))
                last.then_inc(down0_ready, 1)

            def up_gate(p, i, wide):
                if i == 0:
                    pe.wait_ge(logits_copied[0], p + 1)
                elif wide:
                    pe.wait_ge(swish_ready, 3 * p + i)
                else:
                    pe.wait_ge(hidden0_ready, 3 * p + i)
                a = AT["w1"][0] + BANK * i
                mm(bank[0][:, :], xnT[0][:], W[:, a:a + BANK], start=True, stop=True).then_inc(gate_up_ready, 1)

            def up_linear(p, i, wide):
                if not wide:
                    pe.wait_ge(swish_ready, 3 * p + i + 1)
                a = AT["w3"][0] + BANK * i
                mm(finish_bank(i, wide)[:, :], xnT[0][:], W[:, a:a + BANK], start=True, stop=True).then_inc(up_ready, 1)

            def up_shared(p, wide):
                pe.wait_ge(swish_ready if wide else hidden0_ready, 3 * p + 2)
                mm(bank[0][:, 0:P], xnT[0][:], field("w1s"), start=True, stop=True)
                mm(bank[0][:, P:2 * P], xnT[0][:], field("w3s"), start=True, stop=True).then_inc(shared_up_ready, 1)

            def finish(p, h, wide):
                if h in at["finish.u_E"]:
                    apply_E(p, at["finish.u_E"].index(h))
                if h in at["finish.u_turned"]:
                    turn_u(p, at["finish.u_turned"].index(h))
                if h in at["finish.out"]:
                    project_out(p, 0)
                if h in at["finish.xn_T"]:
                    transpose_xn(p, 0)
                if h in at["finish.logits"]:
                    gate_logits(p, 0)
                if h in at["finish.up_gate"]:
                    up_gate(p, at["finish.up_gate"].index(h), wide)
                if h in at["finish.up_linear"]:
                    up_linear(p, at["finish.up_linear"].index(h), wide)
                if h in at["finish.up_shared"]:
                    up_shared(p, wide)
                if h in at["finish.hidden_T"]:
                    transpose_hidden(p, at["finish.hidden_T"].index(h), wide)
                if h in at["finish.down"]:
                    project_down(p)

            def transpose_x2_ctx(p):
                pe.wait_ge(q_xn_ready, p + 1)
                wait_prior(pe, x4_ready, p)
                turn(bank[1][:, 0:P], xn_q[:], ident)
                pe.wait_ge(ctx_post_loaded, 16 * p + 16)
                turn(bank[1][:, P:2 * P], ctx_post[:], ident).then_inc(post_T_ready, 1)

            def project_qkv1(p):
                pe.wait_ge(post_T_copied, p + 1)
                out = bank[1]
                mm(out[:, 0:P], field("wq1"), xcT_post[:, 0:P], start=True, stop=True)
                mm(out[:, P:2 * P], field("wk1"), xcT_post[:, P:2 * P], start=True, stop=True)
                mm(out[:, 2 * P:3 * P], xcT_post[:, P:2 * P], field("wv1"), start=True, stop=True).then_inc(qkv1_ready, 1)

            def scores1(p, g, wide):
                pe.wait_ge(k1_masked, GROUPS * p + g + 1)
                if wide and g == 0:
                    pe.wait_ge(E_copied, STEPS * GROUPS * B)
                if g > 0 and not wide:
                    pe.wait_ge(scores1_copied, GROUPS * p + g)
                mm(second_bank(g, wide)[:, :], q1T[:], group(k1m, g), start=True, stop=True).then_inc(scores1_ready, 1)

            def transpose_P1(p, g, wide):
                pe.wait_ge(P1_ready, GROUPS * p + g + 1)
                if wide:
                    pass
                elif g == 0:
                    pe.wait_ge(scores1_copied, GROUPS * p + GROUPS)
                else:
                    pe.wait_ge(P1_T_copied, GROUPS * p + g)
                for j in range(GROUP):
                    last = turn(second_bank(g, wide)[:, P * j:P * (j + 1)], P1[:, GROUP * g + j, :], ident)
                last.then_inc(P1_T_ready, 1)

            def apply_P1(p):
                pe.wait_ge(P1_T_copied, GROUPS * p + GROUPS)
                apply_transposed(bank[1], v1, P1_T).then_inc(X1T_ready, 1)

            def up1(p, i, wide):
                if wide:
                    pass
                elif i == 0:
                    pe.wait_ge(logits_copied[1], p + 1)
                else:
                    pe.wait_ge(relu_done, 3 * p + i)
                a = AT["up1"][0] + BANK * i if i < 2 else AT["up1s"][0]
                for k in range(4 if i < 2 else 1):
                    last = mm(second_bank(i, wide)[:, P * k:P * (k + 1)], W[:, a + P * k:a + P * (k + 1)], xnT[1][:],
                              start=True, stop=True)
                last.then_inc(up1_ready, 1)

            def down1(p, i, wide):
                pe.wait_ge(hidden1_ready, 3 * p + (i + 1 if wide else 3))
                if i > 0 and not wide:
                    pe.wait_ge(down_weighted, 2 * p + i)
                a = AT["down1"][0]
                for k in range(4 * i, min(4 * i + 4, CHUNKS)):
                    last = mm(second_bank(3 + i, wide)[:, P * (k - 4 * i):P * (k - 4 * i + 1)], hiddenT[1][:, k, :],
                              W[:, a + P * k:a + P * (k + 1)], start=True, stop=True)
                last.then_inc(down1_ready, 1)

            def second(p, h, wide):
                if h in at["second.x_ctx_T"]:
                    transpose_x2_ctx(p)
                if h in at["second.qkv"]:
                    project_qkv1(p)
                if h in at["second.scores"]:
                    scores1(p, at["second.scores"].index(h), wide)
                if h in at["second.P_T"]:
                    transpose_P1(p, at["second.P_T"].index(h), wide)
                if h in at["second.P_v"]:
                    apply_P1(p)
                if h in at["second.out"]:
                    project_out(p, 1)
                if h in at["second.xn_T"]:
                    transpose_xn(p, 1)
                if h in at["second.logits"]:
                    gate_logits(p, 1)
                if h in at["second.up"]:
                    up1(p, at["second.up"].index(h), wide)
                if h in at["second.down"]:
                    down1(p, at["second.down"].index(h), wide)

            pipeline(pe, core, before, finish, second)

        @block.scalar
        def _(act):
            at = ACT_AT
            act.wait_ge(first_loaded, 16)
            act.wait_ge(pool_consts, 1)
            activation = nc.scalar.activation

            def core(c, h):
                if h in at["core.Av_kept"]:
                    wait_prior(act, X0T_ready, c)
                    act.wait_ge(Av_copied, c + 1)
                    activation(spread(Av), mixed(Av_next[:]), ACT.Copy)
                    activation(AvT[:], AvT_next[:], ACT.Copy).then_inc(Av_kept, 1)
                if h % 2 == 0:
                    return
                step, phase, g = core_place(h)
                n = STEPS * GROUPS * c + GROUPS * step + g + 1
                product = by(core_bank[g][:, :], P)
                if phase == 0:
                    act.wait_ge(square_ready, n)
                    activation(group(EE, g), product, ACT.Copy).then_inc(square_copied, 1)
                else:
                    dst = E_work if step < STEPS - 1 else E_last
                    act.wait_ge(product_ready, n)
                    activation(group(dst, g), product, ACT.Copy, scale=0.25).then_inc(E_copied, 1)

            def exp_heads(g, out, scores, negmax, rowsum):
                for j in range(GROUP):
                    hd = GROUP * g + j
                    last = activation(out[:, hd, :], scores(j), ACT.Exp, bias=negmax[:, hd:hd + 1],
                                      accum_out=rowsum[:, hd:hd + 1])
                return last

            def before(p, h, wide):
                if h in at["before.x_ctx_T"]:
                    act.wait_ge(pre_T_ready, p + 1)
                    activation(xcT_pre[:], pre_bank[0][:, 0:2 * P], ACT.Copy).then_inc(pre_T_copied, 1)
                if h in at["before.q_k"]:
                    act.wait_ge(v0_copied, p + 1)
                    activation(q0T[:], pre_bank[1][:, 0:P], ACT.Identity, bias=field("bq0"))
                    activation(k0T[:], pre_bank[1][:, P:2 * P], ACT.Identity, bias=field("bk0")).then_inc(q0k0_copied, 1)
                if h in at["before.exp"]:
                    g = at["before.exp"].index(h)
                    act.wait_ge(negmax0_ready, GROUPS * p + g + 1)
                    exp_heads(g, A, lambda j: before_bank(g, wide)[:, P * j:P * (j + 1)], negmax0, rowsum0).then_inc(exp0_done, 1)
                if h in at["before.A_T"]:
                    g = at["before.A_T"].index(h)
                    act.wait_ge(A_T_ready, GROUPS * p + g + 1)
                    activation(group(A_T, g), by(before_bank(g, wide)[:, :], P), ACT.Copy).then_inc(A_T_copied, 1)
                if h in at["before.A_v"]:
                    act.wait_ge(AvT_ready, p + 1)
                    wait_prior(act, Av_kept, p)
                    activation(AvT_next[:], pre_bank[0][:, 0:P], ACT.Copy).then_inc(AvT_copied, 1)

            def copy_xnT(p, layer):
                act.wait_ge(xnT_ready[layer], p + 1)
                activation(xnT[layer][:], bank[layer][:, 0:P], ACT.Copy).then_inc(xnT_copied[layer], 1)

            def gate_exp(p, layer):
                act.wait_ge(logits_copied[layer], p + 1)
                e = (E0N, E1N)[layer]
                activation(gate_e[layer][:, 0:e], logits[layer][:, 0:e], ACT.Exp, scale=-1.0).then_inc(gate_exp_done[layer], 1)

            def copy_hiddenT(p, i, wide):
                act.wait_ge(hiddenT_ready, 3 * p + i + 1)
                m = min(4, CHUNKS - 4 * i)
                activation(hiddenT[0][:, 4 * i:4 * i + m, :], by(finish_bank(i, wide)[:, 0:P * m], P),
                           ACT.Copy).then_inc(hiddenT_copied, 1)

            def finish(p, h, wide):
                if h in at["finish.u_E"]:
                    r = at["finish.u_E"].index(h)
                    act.wait_ge(uT_ready, 4 * p + r + 1)
                    activation(uT[:], bank[0][:, 0:P], ACT.Copy).then_inc(uT_copied, 1)
                if h in at["finish.xn_T"]:
                    copy_xnT(p, 0)
                if h in at["finish.gate_exp"]:
                    gate_exp(p, 0)
                if h in at["finish.tanh"]:
                    i = at["finish.tanh"].index(h)
                    n = BANK if i < 2 else P
                    if i < 2:
                        act.wait_ge(gate_up_ready, 2 * p + i + 1)
                    else:
                        act.wait_ge(shared_up_ready, p + 1)
                    if i > 0:
                        act.wait_ge(swish_ready, 3 * p + i)
                    activation(act_t[:, 0:n], bank[0][:, 0:n], ACT.Tanh, scale=0.5).then_inc(tanh_done, 1)
                if h in at["finish.hidden_T"]:
                    copy_hiddenT(p, at["finish.hidden_T"].index(h), wide)

            def second(p, h, wide):
                if h in at["second.x_ctx_T"]:
                    act.wait_ge(post_T_ready, p + 1)
                    activation(xcT_post[:], bank[1][:, 0:2 * P], ACT.Copy).then_inc(post_T_copied, 1)
                if h in at["second.k"]:
                    act.wait_ge(q1_copied, p + 1)
                    activation(k1T[:], bank[1][:, P:2 * P], ACT.Identity, bias=field("bk1")).then_inc(k1_copied, 1)
                if h in at["second.exp"]:
                    g = at["second.exp"].index(h)
                    act.wait_ge(negmax1_ready, GROUPS * p + g + 1)
                    exp_heads(g, P1, lambda j: S1[:, GROUP * g + j, :], negmax1, rowsum1).then_inc(exp1_done, 1)
                if h in at["second.P_T"]:
                    g = at["second.P_T"].index(h)
                    act.wait_ge(P1_T_ready, GROUPS * p + g + 1)
                    activation(group(P1_T, g), by(second_bank(g, wide)[:, :], P), ACT.Copy).then_inc(P1_T_copied, 1)
                if h in at["second.P_v"]:
                    act.wait_ge(X1T_ready, p + 1)
                    activation(X1T[:], bank[1][:, 0:P], ACT.Copy).then_inc(X1T_copied, 1)
                if h in at["second.xn_T"]:
                    copy_xnT(p, 1)
                if h in at["second.gate_exp"]:
                    gate_exp(p, 1)
                if h in at["second.relu"]:
                    i = at["second.relu"].index(h)
                    act.wait_ge(up1_ready, 3 * p + i + 1)
                    wait_prior(act, hidden1_ready, 3 * p)
                    m = min(4, CHUNKS - 4 * i)
                    activation(relu1[:, 4 * i:4 * i + m, :], by(second_bank(i, wide)[:, 0:P * m], P),
                               ACT.Relu).then_inc(relu_done, 1)

            pipeline(act, core, before, finish, second)

        @block.vector
        def _(dve):
            at = DVE_AT
            v = nc.vector
            dve.wait_ge(first_loaded, 16)
            dve.wait_ge(pool_consts, 1)

            def hold(k):
                v.tensor_copy(held[:, k:k + 1], const_eps[:])

            def core(c, h):
                step, phase, g = core_place(h)
                if h % 2 == 0 or phase == 1:
                    return
                src = E_first if step == 0 else E_work
                n = STEPS * GROUPS * c + GROUPS * step + g + 1
                if step == 0:
                    dve.wait_ge(E_first_ready, GROUPS * c + g + 1)
                dve.wait_ge(square_copied, n)
                v.scalar_tensor_tensor(out=group(F, g), in0=group(src, g), scalar=3.0, in1=by(core_bank[g][:, :], P),
                                       op0=ALU.mult, op1=ALU.add).then_inc(F_ready, 1)

            def norm_stats(x, st, m, stats_sem, var_sem, n, k):
                v.bn_stats(st[:], x[:]).then_inc(stats_sem, 1)
                dve.wait_ge(stats_sem, n)
                hold(k)
                v.bn_aggr(m[:], st[:]).then_inc(var_sem, 1)

            def norm_apply(x, m, rs, out, rstd_sem, xn_sem, n):
                dve.wait_ge(rstd_sem, n)
                v.tensor_scalar(out[:], x[:], m[:, 0:1], rs[:, 1:2], ALU.subtract, ALU.mult).then_inc(xn_sem, 1)

            def before(p, h, wide):
                if h in at["before.norm_stats"]:
                    dve.wait_ge(x_pre_loaded, 16 * p + 16)
                    norm_stats(x_pre, stats_pre, mv_pre, pre_stats_done, pre_var_ready, p + 1, 4)
                if h in at["before.norm"]:
                    norm_apply(x_pre, mv_pre, rstd_pre, xn_pre, pre_rstd_ready, pre_xn_ready, p + 1)
                if h in at["before.v"]:
                    dve.wait_ge(qkv0_ready, p + 1)
                    v.tensor_tensor(spread(v0), natural(pre_bank[1][:, 2 * P:3 * P]), natural(field("bv0")), ALU.add).then_inc(v0_copied, 1)
                if h in at["before.max"]:
                    g = at["before.max"].index(h)
                    dve.wait_ge(scores0_ready, GROUPS * p + g + 1)
                    v.tensor_reduce(of_group(negmax0, g), by(before_bank(g, wide)[:, :], P), AX.X, ALU.max,
                                    negate=True).then_inc(negmax0_ready, 1)
                if h in at["before.inverse_sum"]:
                    g = at["before.inverse_sum"].index(h)
                    dve.wait_ge(exp0_done, GROUPS * p + g + 1)
                    v.reciprocal(of_group(rinv0, g), of_group(rowsum0, g)).then_inc(rinv0_ready, 1)
                if h in at["before.colsum"]:
                    g = at["before.colsum"].index(h)
                    dve.wait_ge(A_T_copied, GROUPS * p + g + 1)
                    v.tensor_reduce(of_group(colsum, g), group(A_T, g), AX.X, ALU.add).then_inc(colsum_ready, 1)
                if h in at["before.colmax"]:
                    dve.wait_ge(colsumT_ready, p + 1)
                    v.tensor_reduce(colmax[0:HEADS, 0:1], pre_bank[1][0:HEADS, 0:P], AX.X, ALU.max,
                                    negate=True).then_inc(colmax_steps, 1)
                    dve.wait_ge(colmax_steps, 3 * p + 1)
                    v.reciprocal(colmax[0:HEADS, 1:2], colmax[0:HEADS, 0:1]).then_inc(colmax_steps, 1)
                    dve.wait_ge(colmax_steps, 3 * p + 2)
                    v.tensor_scalar(scale_diag[0:HEADS, :], ident[0:HEADS, 0:HEADS], colmax[0:HEADS, 1:2], None,
                                    ALU.mult).then_inc(colmax_steps, 1)
                if h in at["before.Av"]:
                    dve.wait_ge(Av_ready, p + 1)
                    v.tensor_copy(Av_next[:], pre_bank[0][:, P:2 * P]).then_inc(Av_copied, 1)
                if h in at["before.scale"]:
                    dve.wait_ge(scale_ready, p + 1)
                    v.tensor_copy(neg_scale[:], pre_bank[1][:, P:P + HEADS]).then_inc(scale_copied, 1)
                if h in at["before.E_first"]:
                    g = at["before.E_first"].index(h)
                    dve.wait_ge(gram_ready, GROUPS * p + g + 1)
                    dve.wait_ge(scale_copied, p + 1)
                    for j in range(GROUP):
                        hd = GROUP * g + j
                        last = v.scalar_tensor_tensor(out=E_first[:, hd, :], in0=before_bank(g, wide)[:, P * j:P * (j + 1)],
                                                      scalar=neg_scale[:, hd:hd + 1], in1=ident, op0=ALU.mult, op1=ALU.add)
                    last.then_inc(E_first_ready, 1)

            def count_better(layer, step, values, n, low):
                done = gate_steps[layer]
                gt, eq = greater[layer][:, 0:n * n], equal[layer][:, 0:n * n]
                v.tensor_tensor(by(gt, n), repeated(values, n), across(values, n), ALU.is_gt).then_inc(done, 1)
                v.tensor_tensor(by(eq, n), repeated(values, n), across(values, n), ALU.is_equal).then_inc(done, 1)
                step(2)
                v.tensor_tensor(eq, eq, low, ALU.mult).then_inc(done, 1)
                step(3)
                v.tensor_tensor(gt, gt, eq, ALU.add).then_inc(done, 1)
                step(4)
                v.tensor_reduce(rank[layer][:, 0:n], by(gt, n), AX.X, ALU.add).then_inc(done, 1)
                step(5)

            def weigh_chosen(p, layer, step, n, k):
                done = gate_steps[layer]
                v.scalar_tensor_tensor(out=chosen[layer][:, 0:n], in0=rank[layer][:, 0:n], scalar=float(k),
                                       in1=score[layer][:, 0:n], op0=ALU.is_lt, op1=ALU.mult).then_inc(done, 1)
                step(1)
                v.tensor_reduce(total[layer][:, 0:1], chosen[layer][:, 0:n], AX.X, ALU.add).then_inc(done, 1)
                step(2)
                v.tensor_scalar(total[layer][:, 1:2], total[layer][:, 0:1], SUM_EPS, None, ALU.add).then_inc(done, 1)
                step(3)
                v.reciprocal(total[layer][:, 2:3], total[layer][:, 1:2]).then_inc(done, 1)
                step(4)
                v.tensor_scalar(combine[layer][:, 0:n], chosen[layer][:, 0:n], total[layer][:, 2:3], None,
                                ALU.mult).then_inc(combine_ready[layer], 1)

            def gate0_front(p):
                done = gate_steps[0]

                def step(k):
                    dve.wait_ge(done, GATE_STEPS[0] * p + k)
                dve.wait_ge(gate_exp_done[0], p + 1)
                v.tensor_scalar(gate_d[0][:], gate_e[0][:], 1.0, None, ALU.add).then_inc(done, 1)
                step(1)
                v.reciprocal(score[0][:], gate_d[0][:]).then_inc(done, 1)
                step(2)
                s3 = by(score[0][:], E0N // G0N)
                v.tensor_tensor(pairs[:, :, 0:3], s3[:, :, 0:3], s3[:, :, 1:4], ALU.add)
                v.tensor_tensor(pairs[:, :, 3:5], s3[:, :, 0:2], s3[:, :, 2:4], ALU.add)
                v.tensor_tensor(pairs[:, :, 5:6], s3[:, :, 0:1], s3[:, :, 3:4], ALU.add).then_inc(done, 1)
                step(3)
                v.tensor_reduce(gscore[:], pairs[:, :, :], AX.X, ALU.max).then_inc(done, 1)
                step(4)
                count_better(0, lambda k: step(4 + k), gscore[:], G0N, field("low4"))
                v.tensor_scalar(penalty[:], rank[0][:, 0:G0N], 2.0, -4.0, ALU.is_ge, ALU.mult).then_inc(done, 1)
                step(10)
                v.tensor_tensor(by(choice[0][:], E0N // G0N), s3, across(penalty[:], E0N // G0N), ALU.add).then_inc(done, 1)

            def gate0_back(p):
                def step(k):
                    dve.wait_ge(gate_steps[0], GATE_STEPS[0] * p + 11 + k)
                step(0)
                count_better(0, step, choice[0][:], E0N, field("low16"))
                weigh_chosen(p, 0, lambda k: step(5 + k), E0N, 4)

            def gate1(p):
                def step(k):
                    dve.wait_ge(gate_steps[1], GATE_STEPS[1] * p + k)
                dve.wait_ge(logits_copied[1], p + 1)
                v.tensor_tensor(choice[1][:, 0:E1N], logits[1][:, 0:E1N], field("lb"), ALU.add)
                dve.wait_ge(gate_exp_done[1], p + 1)
                v.tensor_scalar(gate_d[1][:, 0:E1N], gate_e[1][:, 0:E1N], 1.0, None, ALU.add).then_inc(gate_steps[1], 1)
                step(1)
                v.reciprocal(score[1][:, 0:E1N], gate_d[1][:, 0:E1N])
                count_better(1, lambda k: step(1 + k), choice[1][:, 0:E1N], E1N, field("low8"))
                weigh_chosen(p, 1, lambda k: step(6 + k), E1N, 2)

            def copy_logits(p, layer):
                dve.wait_ge(logits_ready[layer], p + 1)
                e = (E0N, E1N)[layer]
                v.tensor_copy(logits[layer][:, 0:e], bank[layer][:, 0:e]).then_inc(logits_copied[layer], 1)

            def swish(p, i):
                n = BANK if i < 2 else P
                if i > 0:
                    dve.wait_ge(hidden0_ready, 3 * p + i)
                else:
                    wait_prior(dve, hidden0_ready, 3 * p)
                dve.wait_ge(tanh_done, 3 * p + i + 1)
                v.scalar_tensor_tensor(out=act_g[:, 0:n], in0=act_t[:, 0:n], scalar=1.0, in1=bank[0][:, 0:n],
                                       op0=ALU.add, op1=ALU.mult).then_inc(swish_ready, 1)

            def times_linear(p, i, wide):
                n = BANK if i < 2 else P
                lin = finish_bank(i, wide)[:, 0:n] if i < 2 else bank[0][:, P:2 * P]
                if i < 2:
                    dve.wait_ge(up_ready, 2 * p + i + 1)
                dve.wait_ge(swish_ready, 3 * p + i + 1)
                if i == 0:
                    wait_prior(dve, down0_ready, p)
                v.scalar_tensor_tensor(out=hidden[:, BANK * i:BANK * i + n], in0=act_g[:, 0:n], scalar=0.5, in1=lin,
                                       op0=ALU.mult, op1=ALU.mult).then_inc(hidden0_ready, 1)

            def finish(p, h, wide):
                if h in at["finish.u_turned"]:
                    r = at["finish.u_turned"].index(h)
                    dve.wait_ge(u_ready, 3 * p + r + 1)
                    v.tensor_copy(spread(U), mixed(bank[0][:, P:2 * P])).then_inc(u_copied, 1)
                if h in at["finish.X"]:
                    dve.wait_ge(uT_ready, 4 * p + 4)
                    v.scalar_tensor_tensor(out=u34T[:], in0=uT[:], scalar=3.0, in1=bank[0][:, 0:P], op0=ALU.mult,
                                           op1=ALU.add).then_inc(u34_ready, 1)
                    dve.wait_ge(u34_ready, p + 1)
                    v.scalar_tensor_tensor(out=X0T[:], in0=u34T[:], scalar=-0.25, in1=AvT[:], op0=ALU.mult,
                                           op1=ALU.add).then_inc(X0T_ready, 1)
                if h in at["finish.x1"]:
                    dve.wait_ge(x_bo_ready, p + 1)
                    dve.wait_ge(proj0_ready, p + 1)
                    v.tensor_tensor(x1[:], bank[0][:, 0:P], x_bo[:], ALU.add).then_inc(x1_ready, 1)
                    dve.wait_ge(x1_ready, p + 1)
                    norm_stats(x1, stats[0], mv[0], stats_done[0], var_ready[0], p + 1, 6)
                if h in at["finish.norm"]:
                    norm_apply(x1, mv[0], rstd[0], xn[0], rstd_ready[0], xn_ready[0], p + 1)
                if h in at["finish.logits"]:
                    copy_logits(p, 0)
                if h in at["finish.swish"]:
                    swish(p, at["finish.swish"].index(h))
                if h in at["finish.linear"]:
                    times_linear(p, at["finish.linear"].index(h), wide)
                if h in at["finish.linear_shared"]:
                    times_linear(p, 2, wide)
                if h in at["finish.gate_groups"]:
                    gate0_front(p)
                if h in at["finish.gate_experts"]:
                    gate0_back(p)
                if h in at["finish.x2"]:
                    dve.wait_ge(down0_ready, p + 1)
                    wait_prior(dve, x2_bo_ready, p)
                    v.tensor_tensor(x2[:], bank[0][:, 0:P], x1[:], ALU.add).then_inc(x2_ready, 1)

            def second(p, h, wide):
                if h in at["second.norm_stats"]:
                    dve.wait_ge(x2_ready, p + 1)
                    norm_stats(x2, stats_q, mv_q, q_stats_done, q_var_ready, p + 1, 5)
                if h in at["second.norm"]:
                    norm_apply(x2, mv_q, rstd_q, xn_q, q_rstd_ready, q_xn_ready, p + 1)
                if h in at["second.q_v"]:
                    dve.wait_ge(qkv1_ready, p + 1)
                    v.tensor_tensor(spread(v1), natural(bank[1][:, 2 * P:3 * P]), natural(field("bv1")), ALU.add)
                    v.tensor_scalar(q1T[:], bank[1][:, 0:P], field("bq1"), SCORE_SCALE, ALU.add,
                                    ALU.mult).then_inc(q1_copied, 1)
                if h in at["second.max"]:
                    g = at["second.max"].index(h)
                    dve.wait_ge(scores1_ready, GROUPS * p + g + 1)
                    if g == 0:
                        dve.wait_ge(scores_filled, p + 1)
                        dve.wait_ge(mask_loaded, 16 * p + 16)
                    hold(g)
                    v.copy_predicated(group(S1, g), repeated(mask_post[:], GROUP), by(second_bank(g, wide)[:, :], P)).then_inc(scores1_copied, 1)
                    dve.wait_ge(scores1_copied, GROUPS * p + g + 1)
                    v.tensor_reduce(of_group(negmax1, g), group(S1, g), AX.X, ALU.max, negate=True).then_inc(negmax1_ready, 1)
                if h in at["second.inverse_sum"]:
                    g = at["second.inverse_sum"].index(h)
                    dve.wait_ge(exp1_done, GROUPS * p + g + 1)
                    v.reciprocal(of_group(rinv1, g), of_group(rowsum1, g)).then_inc(rinv1_ready, 1)
                if h in at["second.x3"]:
                    dve.wait_ge(x2_bo_ready, p + 1)
                    dve.wait_ge(proj1_ready, p + 1)
                    v.tensor_tensor(x3[:], bank[1][:, 0:P], x2_bo[:], ALU.add).then_inc(x3_ready, 1)
                    dve.wait_ge(x3_ready, p + 1)
                    norm_stats(x3, stats[1], mv[1], stats_done[1], var_ready[1], p + 1, 7)
                if h in at["second.norm3"]:
                    norm_apply(x3, mv[1], rstd[1], xn[1], rstd_ready[1], xn_ready[1], p + 1)
                if h in at["second.logits"]:
                    copy_logits(p, 1)
                if h in at["second.gate"]:
                    gate1(p)
                if h in at["second.hidden"]:
                    i = at["second.hidden"].index(h)
                    if i == 0:
                        wait_prior(dve, down1_ready, 3 * p)
                    e = slice(4 * i, min(4 * i + 4, CHUNKS))
                    dve.wait_ge(relu_done, 3 * p + i + 1)
                    v.tensor_tensor(hiddenT[1][:, e, :], relu1[:, e, :], relu1[:, e, :], ALU.mult).then_inc(hidden1_ready, 1)
                if h in at["second.weigh"]:
                    i = at["second.weigh"].index(h)
                    dve.wait_ge(combine_ready[1], p + 1)
                    dve.wait_ge(down1_ready, 3 * p + i + 1)
                    v.tensor_tensor(weighted[:, 4 * i:4 * i + 4, :], by(second_bank(3 + i, wide)[:, :], P),
                                    across(combine[1][:, 4 * i:4 * i + 4], P), ALU.mult).then_inc(down_weighted, 1)
                if h in at["second.sum"]:
                    dve.wait_ge(down_weighted, 2 * p + 2)
                    v.tensor_reduce(moe[:], weighted[:, :, :].rearrange("p e c -> p c e"), AX.X, ALU.add).then_inc(moe_ready, 1)
                    dve.wait_ge(moe_ready, p + 1)
                    v.tensor_tensor(x3_moe[:], moe[:], x3[:], ALU.add).then_inc(x3_moe_ready, 1)
                if h in at["second.x4"]:
                    dve.wait_ge(x3_moe_ready, p + 1)
                    dve.wait_ge(down1_ready, 3 * p + 3)
                    wait_prior(dve, out_stored, 16 * p)
                    v.tensor_tensor(x4[:], second_bank(3 + 2, wide)[:, 0:P], x3_moe[:], ALU.add).then_inc(x4_ready, 1)

            pipeline(dve, core, before, finish, second)

        @block.gpsimd
        def _(pool):
            at = POOL_AT
            g_ = nc.gpsimd
            for t in (v0, v1, Av, U):
                g_.memset(t[:], 0.0)
            g_.memset(const_eps[:], LN_EPS)
            g_.memset(const_mhalf[:], -0.5).then_inc(pool_consts, 1)
            pool.wait_ge(pool_consts, 1)
            pool.wait_ge(first_loaded, 16)

            def inverse_root(m, rs, var_sem, veps_sem, rstd_sem, n):
                pool.wait_ge(var_sem, n)
                g_.tensor_tensor(rs[:, 0:1], m[:, 1:2], const_eps[:], ALU.add).then_inc(veps_sem, 1)
                pool.wait_ge(veps_sem, n)
                g_.tensor_tensor(rs[:, 1:2], rs[:, 0:1], const_mhalf[:], ALU.pow).then_inc(rstd_sem, 1)

            def mask_keys(g, out, k_t):
                return g_.tensor_tensor(group(out, g), repeated(k_t[:], GROUP), across(of_group(field("rowmask"), g), P), ALU.mult)

            def core(c, h):
                pass

            def before(p, h, wide):
                if h in at["before.root"]:
                    inverse_root(mv_pre, rstd_pre, pre_var_ready, pre_veps_ready, pre_rstd_ready, p + 1)
                if h in at["before.mask_k"]:
                    pool.wait_ge(q0k0_copied, p + 1)
                    mask_keys(at["before.mask_k"].index(h), k0m, k0T).then_inc(k0_masked, 1)
                if h in at["before.normalise"]:
                    g = at["before.normalise"].index(h)
                    pool.wait_ge(rinv0_ready, GROUPS * p + g + 1)
                    g_.tensor_tensor(group(A, g), group(A, g), across(of_group(rinv0, g), P), ALU.mult).then_inc(A_ready, 1)

            def finish(p, h, wide):
                if h in at["finish.x_bo"]:
                    pool.wait_ge(rest_loaded, 16)
                    pool.wait_ge(x_post_loaded, 16 * p + 16)
                    g_.tensor_tensor(x_bo[:], x_post[:], field("bo0"), ALU.add).then_inc(x_bo_ready, 1)
                if h in at["finish.root"]:
                    inverse_root(mv[0], rstd[0], var_ready[0], veps_ready[0], rstd_ready[0], p + 1)
                if h in at["finish.combine"]:
                    i = at["finish.combine"].index(h)
                    pool.wait_ge(combine_ready[0], p + 1)
                    pool.wait_ge(hidden0_ready, 3 * p + i + 1)
                    part = by(hidden[:, BANK * i:BANK * (i + 1)], UP // E0N)
                    n = E0N // 2
                    g_.tensor_tensor(part, part, across(combine[0][:, n * i:n * (i + 1)], UP // E0N),
                                     ALU.mult).then_inc(hidden0_scaled, 1)

            def second(p, h, wide):
                if h in at["second.root_bo"]:
                    inverse_root(mv_q, rstd_q, q_var_ready, q_veps_ready, q_rstd_ready, p + 1)
                    pool.wait_ge(rest_loaded, 16)
                    wait_prior(pool, x3_ready, p)
                    g_.tensor_tensor(x2_bo[:], x2[:], field("bo1"), ALU.add).then_inc(x2_bo_ready, 1)
                if h in at["second.fill"]:
                    wait_prior(pool, exp1_done, GROUPS * p)
                    g_.tensor_tensor(held_pool[:], const_eps[:], const_eps[:], ALU.add)
                    g_.memset(S1[:], MASKED).then_inc(scores_filled, 1)
                if h in at["second.mask_k"]:
                    pool.wait_ge(k1_copied, p + 1)
                    mask_keys(at["second.mask_k"].index(h), k1m, k1T).then_inc(k1_masked, 1)
                if h in at["second.normalise"]:
                    g = at["second.normalise"].index(h)
                    pool.wait_ge(rinv1_ready, GROUPS * p + g + 1)
                    g_.tensor_tensor(group(P1, g), group(P1, g), across(of_group(rinv1, g), P), ALU.mult).then_inc(P1_ready, 1)
                if h in at["second.root3"]:
                    inverse_root(mv[1], rstd[1], var_ready[1], veps_ready[1], rstd_ready[1], p + 1)

            pipeline(pool, core, before, finish, second)


def pack_weights(np, a):
    def row(v):
        return np.broadcast_to(np.asarray(v)[None, :], (P, len(v)))

    def col(v):
        return np.asarray(v)[:, None]

    def low(n):
        return row(np.tril(np.ones((n, n), np.float32), -1).ravel())

    def chunks(w, shared):
        w = np.concatenate([w, shared], 0)
        return w.reshape(CHUNKS, P, P).transpose(1, 0, 2).reshape(P, CHUNKS * P)

    rows = np.arange(P)
    rowmask = (rows[:, None] // DH == np.arange(HEADS)[None, :]).astype(np.float32)

    def mixed(w):
        return w.reshape(GROUPS, GROUP, DH, P).transpose(1, 0, 2, 3).reshape(P, P)

    f = {
        "wq0": a["L0_xattn_Wq"], "wk0": a["L0_xattn_Wk"], "wv0": a["L0_xattn_Wv"], "wo0": mixed(a["L0_xattn_Wo"]),
        "bq0": col(a["L0_xattn_bq"]), "bk0": col(a["L0_xattn_bk"]), "bv0": row(a["L0_xattn_bv"]),
        "bo0": row(a["L0_xattn_bo"]),
        "wq1": a["L1_xattn_Wq"].T, "wk1": a["L1_xattn_Wk"].T, "wv1": a["L1_xattn_Wv"].T, "wo1": mixed(a["L1_xattn_Wo"].T),
        "bq1": col(a["L1_xattn_bq"]), "bk1": col(a["L1_xattn_bk"]), "bv1": row(a["L1_xattn_bv"]),
        "bo1": row(a["L1_xattn_bo"]),
        "ident": np.eye(P, dtype=np.float32), "rowmask": rowmask, "ones": np.ones((P, P), np.float32),
        "gate0": a["L0_ffn_w_gate"].T, "gate1": a["L1_ffn_gate_w"].T, "lb": row(a["L1_ffn_lb_bias"]),
        "low4": low(G0N), "low16": low(E0N), "low8": low(E1N),
        "w1": a["L0_ffn_w1_e"].reshape(UP, P).T, "w3": a["L0_ffn_w3_e"].reshape(UP, P).T,
        "w1s": a["L0_ffn_w1_s"].T, "w3s": a["L0_ffn_w3_s"].T,
        "w2": chunks(a["L0_ffn_w2_e"].transpose(0, 2, 1).reshape(UP, P), a["L0_ffn_w2_s"].T),
        "up1": a["L1_ffn_w1"].reshape(UP, P).T, "up1s": a["L1_ffn_cfc"].T,
        "down1": chunks(a["L1_ffn_w2"].transpose(0, 2, 1).reshape(UP, P), a["L1_ffn_cproj"].T),
    }
    return np.ascontiguousarray(np.concatenate([f[name] for name, _ in FIELDS], axis=1))


def kernel(**inputs):
    import numpy as np
    import concourse.bacc as bacc
    from concourse.bass_utils import run_bass_kernel_spmd

    a = {k: np.asarray(val) for k, val in inputs.items()}
    arrays = {
        "x_dram": np.ascontiguousarray(a["x"]),
        "ctx_dram": np.ascontiguousarray(a["ctx_1024"]),
        "mask_dram": np.ascontiguousarray(a["mask_BxSxS2_bf1"]),
        "weights_dram": pack_weights(np, a),
    }
    nc = bacc.Bacc("TRN2", target_bir_lowering=False, num_devices=1)
    aps = [nc.dram_tensor(n, arr.shape, mybir.dt.from_np(arr.dtype), kind="ExternalInput").ap() for n, arr in arrays.items()]
    out = nc.dram_tensor("out_dram", a["x"].shape, F32, kind="ExternalOutput").ap()
    build(nc, *aps, out)
    r = run_bass_kernel_spmd(nc, [arrays], core_ids=[0])
    return r.results[0]["out_dram"]
```
